# Optimizing a Trainium2 kernel written in Bass

```python
import numpy as np
import jax
import jax.numpy as jnp

def _softmax(x, axis=-1):
    return jax.nn.softmax(x, axis=axis)

def _gelu(x):
    return jax.nn.gelu(x, approximate=True)

def _silu(x):
    return jax.nn.silu(x)

def _sigmoid(x):
    return jax.nn.sigmoid(x)

def _layernorm(x, axis=-1, eps=1e-05):
    m = jnp.mean(x, axis=axis, keepdims=True)
    v = jnp.var(x, axis=axis, keepdims=True)
    return (x - m) / jnp.sqrt(v + eps)

def _scatter_add(tgt, idx, src, axis=0):
    return tgt.at[idx].add(src)

def _segment_sum(src, seg, n):
    return jax.ops.segment_sum(src, seg, n)
kernel_name = 'mk_xattn_seq_d4_seqx_r8_995ea3'

def setup_inputs(seed: int=0):
    np.random.seed(seed)
    _w = jnp.asarray

    def _rec_inputs():
        import jax
        import jax.numpy as jnp
        _rk = jax.random.key(seed)
        x = -0.0003929 + 0.9999 * jax.random.normal(jax.random.fold_in(_rk, 1), (16, 128, 128), jnp.float32)
        _lenS = 128 - jax.random.randint(jax.random.fold_in(_rk, 7), (16,), 0, max(1, 128 // 4) + 1, jnp.int32)
        _lenS2 = 120 - jax.random.randint(jax.random.fold_in(_rk, 8), (16,), 0, max(1, 120 // 4) + 1, jnp.int32)
        _ctx_512P = jax.random.normal(jax.random.fold_in(_rk, 11), (16, 16, 64), jnp.float32)
        _ctx_512c = jax.random.dirichlet(jax.random.fold_in(_rk, 511), 0.3 * jnp.ones((16,), jnp.float32), (16, 120))
        _ctx_512t = jnp.einsum('bsk,bkd->bsd', _ctx_512c, _ctx_512P)
        _ctx_512t = _ctx_512t * jax.lax.rsqrt(jnp.mean(jnp.square(_ctx_512t)) + 1e-12) * 0.953939
        ctx_512 = 4.13588e-05 + 0.999923 * (_ctx_512t + 0.3 * jax.random.normal(jax.random.fold_in(_rk, 611), (16, 120, 64), jnp.float32))
        _validS = jnp.arange(128)[None, :] < _lenS[:, None]
        _validS2 = jnp.arange(120)[None, :] < _lenS2[:, None]
        _causal = jnp.tril(jnp.ones((128, 128), dtype=bool))
        mask_BxSxS_ik0 = jnp.where(jnp.broadcast_to(_validS[:, None, :], (16, 128, 128)), 0, 1).astype(jnp.int32)
        mask_Bx1xS2_if1 = jnp.where(jnp.ones((16, 1, 120), dtype=bool), 1, 0).astype(jnp.int32)
        return (x, ctx_512, mask_BxSxS_ik0, mask_Bx1xS2_if1)
    x, ctx_512, mask_BxSxS_ik0, mask_Bx1xS2_if1 = _rec_inputs()

    def _L0_xattn_setup():
        import jax, jax.numpy as jnp
        import numpy as np
        QUERY_DIM = 128
        KEY_DIM = 64
        HIDDEN_DIM = 128
        B, LQ, LK = (8, 256, 256)
        key = jax.random.key(seed)
        ks = jax.random.split(key, 10)
        s_q = 1.0 / np.sqrt(QUERY_DIM)
        s_k = 1.0 / np.sqrt(KEY_DIM)
        s_h = 1.0 / np.sqrt(HIDDEN_DIM)
        return {'query': jax.random.normal(ks[0], (B, LQ, QUERY_DIM), jnp.float32), 'key': jax.random.normal(ks[1], (B, LK, KEY_DIM), jnp.float32), 'Wq': jax.random.uniform(ks[2], (QUERY_DIM, HIDDEN_DIM), jnp.float32, -s_q, s_q), 'bq': jax.random.uniform(ks[3], (HIDDEN_DIM,), jnp.float32, -s_q, s_q), 'Wk': jax.random.uniform(ks[4], (KEY_DIM, HIDDEN_DIM), jnp.float32, -s_k, s_k), 'bk': jax.random.uniform(ks[5], (HIDDEN_DIM,), jnp.float32, -s_k, s_k), 'Wv': jax.random.uniform(ks[6], (KEY_DIM, HIDDEN_DIM), jnp.float32, -s_k, s_k), 'bv': jax.random.uniform(ks[7], (HIDDEN_DIM,), jnp.float32, -s_k, s_k), 'Wo': jax.random.uniform(ks[8], (HIDDEN_DIM, QUERY_DIM), jnp.float32, -s_h, s_h), 'bo': jax.random.uniform(ks[9], (QUERY_DIM,), jnp.float32, -s_h, s_h)}
    _L0_xattn_all = _L0_xattn_setup()
    _L0_xattn_in = {k: v for k, v in _L0_xattn_all.items() if k in ('Wq', 'bq', 'Wk', 'bk', 'Wv', 'bv', 'Wo', 'bo')}
    del _L0_xattn_all

    def _L1_xattn_setup():
        import jax, jax.numpy as jnp
        import numpy as np
        B, T, E = (8, 512, 128)
        M, L = (32, 64)
        EPS = 1e-06
        key = jax.random.key(seed)
        ks = jax.random.split(key, 5)
        return {'emb': jax.random.normal(ks[0], (B, T, E), dtype=jnp.float32), 'latent': jax.random.normal(ks[1], (B, M, L), dtype=jnp.float32), 'Wq': jax.random.normal(ks[2], (E, E), dtype=jnp.float32) * (1.0 / np.sqrt(E)), 'bq': jnp.zeros((E,), dtype=jnp.float32), 'Wk': jax.random.normal(ks[3], (L, E), dtype=jnp.float32) * (1.0 / np.sqrt(L)), 'bk': jnp.zeros((E,), dtype=jnp.float32), 'Wv': jax.random.normal(ks[4], (L, E), dtype=jnp.float32) * (1.0 / np.sqrt(L)), 'bv': jnp.zeros((E,), dtype=jnp.float32), 'gamma': jnp.ones((E,), dtype=jnp.float32), 'beta': jnp.zeros((E,), dtype=jnp.float32)}
    _L1_xattn_all = _L1_xattn_setup()
    _L1_xattn_in = {k: v for k, v in _L1_xattn_all.items() if k in ('Wq', 'bq', 'Wk', 'bk', 'Wv', 'bv', 'gamma', 'beta')}
    del _L1_xattn_all

    def _L2_xattn_setup():
        import jax, jax.numpy as jnp
        import numpy as np
        B, ST, SS = (8, 64, 72)
        TD, SD = (128, 64)
        L, H, D, FF = (6, 16, 64, 512)

        def _ln(x, g, b, eps=1e-05):
            m = jnp.mean(x, axis=-1, keepdims=True)
            v = jnp.mean(jnp.square(x - m), axis=-1, keepdims=True)
            return (x - m) / jnp.sqrt(v + eps) * g + b

        def _heads(x):
            b, s, _ = x.shape
            return x.reshape(b, s, H, D).transpose(0, 2, 1, 3)

        def _mha(s, t, kv_w, q_w, o_w, o_b, mask):
            kv = s @ kv_w
            k, v = jnp.split(kv, 2, axis=-1)
            q = t @ q_w
            k, v, q = (_heads(k), _heads(v), _heads(q))
            scores = jnp.einsum('bhqd,bhkd->bhqk', q, k) * D ** (-0.5)
            scores = jnp.where(mask[:, None] == 0, jnp.float32(-1000000000.0), scores)
            attn = jax.nn.softmax(scores, axis=-1)
            o = jnp.einsum('bhqk,bhkd->bhqd', attn, v)
            o = o.transpose(0, 2, 1, 3).reshape(t.shape[0], t.shape[1], H * D)
            return o @ o_w + o_b
        key = jax.random.key(seed)
        ks = jax.random.split(key, 18)
        sc = 0.02
        inp = {'src': jax.random.normal(ks[0], (B, SS, SD), jnp.float32), 'tgt': jax.random.normal(ks[1], (B, ST, TD), jnp.float32), 'tgt_mask': jnp.broadcast_to(jnp.tril(jnp.ones((ST, ST), jnp.int32)), (B, ST, ST)), 'src_mask': jnp.ones((B, 1, SS), jnp.int32), 'norm_g': jnp.ones((TD,), jnp.float32), 'norm_b': jnp.zeros((TD,), jnp.float32), 'sa_kv': jax.random.normal(ks[2], (L, TD, 2 * H * D), jnp.float32) * sc, 'sa_q': jax.random.normal(ks[3], (L, TD, H * D), jnp.float32) * sc, 'sa_ow': jax.random.normal(ks[4], (L, H * D, TD), jnp.float32) * sc, 'sa_ob': jnp.zeros((L, TD), jnp.float32), 'ca_kv': jax.random.normal(ks[5], (L, SD, 2 * H * D), jnp.float32) * sc, 'ca_q': jax.random.normal(ks[6], (L, TD, H * D), jnp.float32) * sc, 'ca_ow': jax.random.normal(ks[7], (L, H * D, TD), jnp.float32) * sc, 'ca_ob': jnp.zeros((L, TD), jnp.float32), 'ff_w1': jax.random.normal(ks[8], (L, TD, FF), jnp.float32) * sc, 'ff_b1': jnp.zeros((L, FF), jnp.float32), 'ff_w2': jax.random.normal(ks[9], (L, FF, TD), jnp.float32) * sc, 'ff_b2': jnp.zeros((L, TD), jnp.float32), 'pre_g': jnp.ones((L, TD), jnp.float32), 'pre_b': jnp.zeros((L, TD), jnp.float32)}
        return inp
    _L2_xattn_all = _L2_xattn_setup()
    _L2_xattn_in = {k: v for k, v in _L2_xattn_all.items() if k in ('norm_g', 'norm_b', 'sa_kv', 'sa_q', 'sa_ow', 'sa_ob', 'ca_kv', 'ca_q', 'ca_ow', 'ca_ob', 'ff_w1', 'ff_b1', 'ff_w2', 'ff_b2', 'pre_g', 'pre_b')}
    del _L2_xattn_all

    def _L3_xattn_setup():
        import jax, jax.numpy as jnp
        import numpy as np
        QUERY_DIM = 128
        KEY_DIM = 64
        HIDDEN_DIM = 128
        B, LQ, LK = (8, 256, 256)
        key = jax.random.key(seed)
        ks = jax.random.split(key, 10)
        s_q = 1.0 / np.sqrt(QUERY_DIM)
        s_k = 1.0 / np.sqrt(KEY_DIM)
        s_h = 1.0 / np.sqrt(HIDDEN_DIM)
        return {'query': jax.random.normal(ks[0], (B, LQ, QUERY_DIM), jnp.float32), 'key': jax.random.normal(ks[1], (B, LK, KEY_DIM), jnp.float32), 'Wq': jax.random.uniform(ks[2], (QUERY_DIM, HIDDEN_DIM), jnp.float32, -s_q, s_q), 'bq': jax.random.uniform(ks[3], (HIDDEN_DIM,), jnp.float32, -s_q, s_q), 'Wk': jax.random.uniform(ks[4], (KEY_DIM, HIDDEN_DIM), jnp.float32, -s_k, s_k), 'bk': jax.random.uniform(ks[5], (HIDDEN_DIM,), jnp.float32, -s_k, s_k), 'Wv': jax.random.uniform(ks[6], (KEY_DIM, HIDDEN_DIM), jnp.float32, -s_k, s_k), 'bv': jax.random.uniform(ks[7], (HIDDEN_DIM,), jnp.float32, -s_k, s_k), 'Wo': jax.random.uniform(ks[8], (HIDDEN_DIM, QUERY_DIM), jnp.float32, -s_h, s_h), 'bo': jax.random.uniform(ks[9], (QUERY_DIM,), jnp.float32, -s_h, s_h)}
    _L3_xattn_all = _L3_xattn_setup()
    _L3_xattn_in = {k: v for k, v in _L3_xattn_all.items() if k in ('Wq', 'bq', 'Wk', 'bk', 'Wv', 'bv', 'Wo', 'bo')}
    del _L3_xattn_all
    return {'x': x, 'ctx_512': ctx_512, 'mask_BxSxS_ik0': mask_BxSxS_ik0, 'mask_Bx1xS2_if1': mask_Bx1xS2_if1, 'L0_xattn_Wq': _L0_xattn_in['Wq'], 'L0_xattn_bq': _L0_xattn_in['bq'], 'L0_xattn_Wk': _L0_xattn_in['Wk'], 'L0_xattn_bk': _L0_xattn_in['bk'], 'L0_xattn_Wv': _L0_xattn_in['Wv'], 'L0_xattn_bv': _L0_xattn_in['bv'], 'L0_xattn_Wo': _L0_xattn_in['Wo'], 'L0_xattn_bo': _L0_xattn_in['bo'], 'L1_xattn_Wq': _L1_xattn_in['Wq'], 'L1_xattn_bq': _L1_xattn_in['bq'], 'L1_xattn_Wk': _L1_xattn_in['Wk'], 'L1_xattn_bk': _L1_xattn_in['bk'], 'L1_xattn_Wv': _L1_xattn_in['Wv'], 'L1_xattn_bv': _L1_xattn_in['bv'], 'L1_xattn_gamma': _L1_xattn_in['gamma'], 'L1_xattn_beta': _L1_xattn_in['beta'], 'L2_xattn_norm_g': _L2_xattn_in['norm_g'], 'L2_xattn_norm_b': _L2_xattn_in['norm_b'], 'L2_xattn_sa_kv': _L2_xattn_in['sa_kv'], 'L2_xattn_sa_q': _L2_xattn_in['sa_q'], 'L2_xattn_sa_ow': _L2_xattn_in['sa_ow'], 'L2_xattn_sa_ob': _L2_xattn_in['sa_ob'], 'L2_xattn_ca_kv': _L2_xattn_in['ca_kv'], 'L2_xattn_ca_q': _L2_xattn_in['ca_q'], 'L2_xattn_ca_ow': _L2_xattn_in['ca_ow'], 'L2_xattn_ca_ob': _L2_xattn_in['ca_ob'], 'L2_xattn_ff_w1': _L2_xattn_in['ff_w1'], 'L2_xattn_ff_b1': _L2_xattn_in['ff_b1'], 'L2_xattn_ff_w2': _L2_xattn_in['ff_w2'], 'L2_xattn_ff_b2': _L2_xattn_in['ff_b2'], 'L2_xattn_pre_g': _L2_xattn_in['pre_g'], 'L2_xattn_pre_b': _L2_xattn_in['pre_b'], 'L3_xattn_Wq': _L3_xattn_in['Wq'], 'L3_xattn_bq': _L3_xattn_in['bq'], 'L3_xattn_Wk': _L3_xattn_in['Wk'], 'L3_xattn_bk': _L3_xattn_in['bk'], 'L3_xattn_Wv': _L3_xattn_in['Wv'], 'L3_xattn_bv': _L3_xattn_in['bv'], 'L3_xattn_Wo': _L3_xattn_in['Wo'], 'L3_xattn_bo': _L3_xattn_in['bo']}

def reference(x, ctx_512, mask_BxSxS_ik0, mask_Bx1xS2_if1, L0_xattn_Wq, L0_xattn_bq, L0_xattn_Wk, L0_xattn_bk, L0_xattn_Wv, L0_xattn_bv, L0_xattn_Wo, L0_xattn_bo, L1_xattn_Wq, L1_xattn_bq, L1_xattn_Wk, L1_xattn_bk, L1_xattn_Wv, L1_xattn_bv, L1_xattn_gamma, L1_xattn_beta, L2_xattn_norm_g, L2_xattn_norm_b, L2_xattn_sa_kv, L2_xattn_sa_q, L2_xattn_sa_ow, L2_xattn_sa_ob, L2_xattn_ca_kv, L2_xattn_ca_q, L2_xattn_ca_ow, L2_xattn_ca_ob, L2_xattn_ff_w1, L2_xattn_ff_b1, L2_xattn_ff_w2, L2_xattn_ff_b2, L2_xattn_pre_g, L2_xattn_pre_b, L3_xattn_Wq, L3_xattn_bq, L3_xattn_Wk, L3_xattn_bk, L3_xattn_Wv, L3_xattn_bv, L3_xattn_Wo, L3_xattn_bo):
    import jax
    import jax.numpy as jnp

    def _L0_xattn_ref(query, key, Wq, bq, Wk, bk, Wv, bv, Wo, bo):
        import jax, jax.numpy as jnp
        import numpy as np
        QUERY_DIM = 128
        KEY_DIM = 64
        HIDDEN_DIM = 128
        B, LQ, LK = (8, 256, 256)
        scale = HIDDEN_DIM ** (-0.5)
        Q = jnp.einsum('bqd,dh->bqh', query, Wq) + bq
        K = jnp.einsum('bkd,dh->bkh', key, Wk) + bk
        V = jnp.einsum('bkd,dh->bkh', key, Wv) + bv
        scores = jnp.einsum('bqh,bkh->bqk', Q, K) * scale
        weights = jax.nn.softmax(scores, axis=-1)
        attended = jnp.einsum('bqk,bkh->bqh', weights, V)
        out = jnp.einsum('bqh,hd->bqd', attended, Wo) + bo
        return query + out

    def _L1_xattn_ref(emb, latent, Wq, bq, Wk, bk, Wv, bv, gamma, beta):
        import jax, jax.numpy as jnp
        import numpy as np
        B, T, E = (8, 512, 128)
        M, L = (32, 64)
        EPS = 1e-06
        q = jnp.einsum('bte,ef->btf', emb, Wq) + bq
        k = jnp.einsum('bml,le->bme', latent, Wk) + bk
        v = jnp.einsum('bml,le->bme', latent, Wv) + bv
        scale = 1.0 / jnp.sqrt(jnp.asarray(E, dtype=q.dtype))
        w = jnp.einsum('bte,bme->btm', q, k) * scale
        w = jax.nn.softmax(w, axis=1)
        pred = jnp.einsum('btm,bme->bte', w, v)
        x = pred + emb
        mu = jnp.mean(x, axis=-1, keepdims=True)
        var = jnp.var(x, axis=-1, keepdims=True)
        return (x - mu) * jax.lax.rsqrt(var + EPS) * gamma + beta

    def _L2_xattn_ref(src, tgt, tgt_mask, src_mask, norm_g, norm_b, sa_kv, sa_q, sa_ow, sa_ob, ca_kv, ca_q, ca_ow, ca_ob, ff_w1, ff_b1, ff_w2, ff_b2, pre_g, pre_b):
        import jax, jax.numpy as jnp
        import numpy as np
        B, ST, SS = (8, 64, 72)
        TD, SD = (128, 64)
        L, H, D, FF = (6, 16, 64, 512)

        def _ln(x, g, b, eps=1e-05):
            m = jnp.mean(x, axis=-1, keepdims=True)
            v = jnp.mean(jnp.square(x - m), axis=-1, keepdims=True)
            return (x - m) / jnp.sqrt(v + eps) * g + b

        def _heads(x):
            b, s, _ = x.shape
            return x.reshape(b, s, H, D).transpose(0, 2, 1, 3)

        def _mha(s, t, kv_w, q_w, o_w, o_b, mask):
            kv = s @ kv_w
            k, v = jnp.split(kv, 2, axis=-1)
            q = t @ q_w
            k, v, q = (_heads(k), _heads(v), _heads(q))
            scores = jnp.einsum('bhqd,bhkd->bhqk', q, k) * D ** (-0.5)
            scores = jnp.where(mask[:, None] == 0, jnp.float32(-1000000000.0), scores)
            attn = jax.nn.softmax(scores, axis=-1)
            o = jnp.einsum('bhqk,bhkd->bhqd', attn, v)
            o = o.transpose(0, 2, 1, 3).reshape(t.shape[0], t.shape[1], H * D)
            return o @ o_w + o_b
        stacked = (sa_kv, sa_q, sa_ow, sa_ob, ca_kv, ca_q, ca_ow, ca_ob, ff_w1, ff_b1, ff_w2, ff_b2, pre_g, pre_b)

        def step(t, p):
            skv, sq, sow, sob, ckv, cq, cow, cob, w1, b1, w2, b2, pg, pb = p
            tn = _ln(t, norm_g, norm_b)
            t = _mha(tn, tn, skv, sq, sow, sob, tgt_mask) + t
            tn = _ln(t, norm_g, norm_b)
            t = _mha(src, tn, ckv, cq, cow, cob, src_mask) + t
            tn = _ln(t, pg, pb)
            t = t + (jax.nn.relu(tn @ w1 + b1) @ w2 + b2)
            return (t, None)
        out, _ = jax.lax.scan(step, tgt, stacked)
        return out

    def _L3_xattn_ref(query, key, Wq, bq, Wk, bk, Wv, bv, Wo, bo):
        import jax, jax.numpy as jnp
        import numpy as np
        QUERY_DIM = 128
        KEY_DIM = 64
        HIDDEN_DIM = 128
        B, LQ, LK = (8, 256, 256)
        scale = HIDDEN_DIM ** (-0.5)
        Q = jnp.einsum('bqd,dh->bqh', query, Wq) + bq
        K = jnp.einsum('bkd,dh->bkh', key, Wk) + bk
        V = jnp.einsum('bkd,dh->bkh', key, Wv) + bv
        scores = jnp.einsum('bqh,bkh->bqk', Q, K) * scale
        weights = jax.nn.softmax(scores, axis=-1)
        attended = jnp.einsum('bqk,bkh->bqh', weights, V)
        out = jnp.einsum('bqh,hd->bqd', attended, Wo) + bo
        return query + out
    x = _L0_xattn_ref(x, ctx_512, L0_xattn_Wq, L0_xattn_bq, L0_xattn_Wk, L0_xattn_bk, L0_xattn_Wv, L0_xattn_bv, L0_xattn_Wo, L0_xattn_bo)
    x = _L1_xattn_ref(x, ctx_512, L1_xattn_Wq, L1_xattn_bq, L1_xattn_Wk, L1_xattn_bk, L1_xattn_Wv, L1_xattn_bv, L1_xattn_gamma, L1_xattn_beta)
    x = _L2_xattn_ref(ctx_512, x, mask_BxSxS_ik0, mask_Bx1xS2_if1, L2_xattn_norm_g, L2_xattn_norm_b, L2_xattn_sa_kv, L2_xattn_sa_q, L2_xattn_sa_ow, L2_xattn_sa_ob, L2_xattn_ca_kv, L2_xattn_ca_q, L2_xattn_ca_ow, L2_xattn_ca_ob, L2_xattn_ff_w1, L2_xattn_ff_b1, L2_xattn_ff_w2, L2_xattn_ff_b2, L2_xattn_pre_g, L2_xattn_pre_b)
    x = _L3_xattn_ref(x, ctx_512, L3_xattn_Wq, L3_xattn_bq, L3_xattn_Wk, L3_xattn_bk, L3_xattn_Wv, L3_xattn_bv, L3_xattn_Wo, L3_xattn_bo)
    return x

_drawn_inputs = setup_inputs


def setup_inputs(seed=0):
    import zlib

    import numpy as np

    out = dict(_drawn_inputs(seed))
    spreads = {'L1_xattn_bq': (0.0, 2.0),
     'L1_xattn_bk': (0.0, 0.1),
     'L1_xattn_bv': (0.0, 0.1),
     'L1_xattn_gamma': (1.0, 0.2),
     'L1_xattn_beta': (0.0, 0.1),
     'L2_xattn_norm_g': (1.0, 0.2),
     'L2_xattn_norm_b': (0.0, 0.1),
     'L2_xattn_sa_ob': (0.0, 0.1),
     'L2_xattn_ca_ob': (0.0, 0.1),
     'L2_xattn_ff_b1': (0.0, 0.1),
     'L2_xattn_ff_b2': (0.0, 0.1),
     'L2_xattn_pre_g': (1.0, 0.2),
     'L2_xattn_pre_b': (0.0, 0.574)}
    factors = {'L0_xattn_Wq': 3.047,
     'L0_xattn_bq': 8.0,
     'L0_xattn_Wk': 3.046,
     'L0_xattn_bk': 64.0,
     'L2_xattn_sa_q': 8.0,
     'L2_xattn_ca_q': 33.34,
     'L3_xattn_bq': 36.215,
     'L3_xattn_bk': 64.0}
    for name, (base, spread) in spreads.items():
        noise = np.random.default_rng([zlib.crc32(name.encode()), seed]).standard_normal(out[name].shape)
        drawn = base * np.exp(spread * noise) if base else spread * noise
        out[name] = jnp.asarray(drawn.astype(out[name].dtype))
    for name, factor in factors.items():
        out[name] = (out[name] * factor).astype(out[name].dtype)
    return out
```

```python
from contextlib import ExitStack

import concourse.bass as bass
from concourse import mybir

F32 = mybir.dt.float32
I32 = mybir.dt.int32
ALU = mybir.AluOpType
ACT = mybir.ActivationFunctionType
AX = mybir.AxisListType

B, S, E = 16, 128, 128
SC, CD = 120, 64
L, H, D = 6, 16, 64
HD = H * D
FF = 512
NP = H // 2
NG = 4
GH = H // NG
NF = FF // 128
N = L * B
BG = 4
GROUPS = B // BG
MASKED = 1e30
LN_EPS, L1_EPS = 1e-5, 1e-6
SCALE1 = 128 ** -0.5


def wait(eng, sem, value):
    if isinstance(value, int) and value <= 0:
        return
    eng.wait_ge(sem, value)


def bcast(ap, shape):
    return ap.unsqueeze(2).to_broadcast(shape)


def pipeline(kinds, groups):
    return [(k, tick - k) for tick in range(kinds + groups - 1) for k in reversed(range(kinds))
            if 0 <= tick - k < groups]


def build(nc, a):
    with ExitStack() as ctx:
        def sb(name, shape, dt=F32, scope=ctx):
            return scope.enter_context(nc.sbuf_tensor(name, shape, dt))

        phase_sems = []

        def sem(name, scope=ctx):
            if scope is ctx:
                return ctx.enter_context(nc.semaphore(name))
            phase_sems.append(nc.alloc_semaphore(name=name))
            return phase_sems[-1]

        def next_phase():
            nc.clear_and_free_semaphores(phase_sems)
            phase_sems.clear()
            nc.all_engine_barrier()

        banks = [ctx.enter_context(nc.psum_tensor(f"bank{i}", [128, 512], F32)) for i in range(8)]

        t_all = sb("t_all", [128, B, E])
        ctxT = sb("ctxT", [128, B, SC])
        ctx_all = sb("ctx_all", [SC, B, CD])
        ident = sb("ident", [128, 128])
        started = sem("started")

        load_and_l0(nc, a, sb, sem, banks, t_all, ctxT, ctx_all, ident, started)
        next_phase()
        l1(nc, a, sb, sem, banks, t_all, ctxT, ident)
        next_phase()
        decoder(nc, a, sb, sem, banks, t_all, ctxT, ctx_all, ident, started, next_phase)
        next_phase()
        query_context(nc, a, "L3", sb, sem, banks, t_all, ctxT, ident, a["out"])


def load_and_l0(nc, a, sb, sem, banks, t_all, ctxT, ctx_all, ident, started):
    loaded, zeroed, made = sem("inputs_loaded"), sem("ident_zeroed"), sem("ident_made")
    with nc.Block() as block:
        @block.sync
        def _(sp):
            sp.dma_start(t_all[:, :, :], a["x"].rearrange("b s e -> s b e")).then_inc(loaded, 16)
            for half in range(2):
                sp.dma_start(ctxT[half * CD:(half + 1) * CD, :, :], a["ctxT"]).then_inc(loaded, 16)
            sp.dma_start(ctx_all[:, :, :], a["ctx_512"].rearrange("b k c -> k b c")).then_inc(loaded, 16)
            sp.wait_ge(loaded, 64)

        @block.gpsimd
        def _(pool):
            nc.gpsimd.memset(ident[:, :], 0.0).then_inc(zeroed, 1)
            pool.wait_ge(zeroed, 1)
            nc.gpsimd.affine_select(out=ident[:, :], in_=ident[:, :], compare_op=ALU.not_equal, fill=1.0,
                                    base=0, pattern=[[-1, 128]], channel_multiplier=1).then_inc(made, 1)
            pool.wait_ge(made, 1)
            pool.sem_inc(started, 1)
    query_context(nc, a, "L0", sb, sem, banks, t_all, ctxT, ident, None)


def query_context(nc, a, name, sb, sem, banks, t_all, ctxT, ident, out):
    with ExitStack() as ctx:
        def buf(what, shape):
            return sb(f"{name}_{what}", shape, F32, ctx)

        def ev(what):
            return sem(f"{name}_{what}", ctx)

        wq, wk, wv, wo = buf("wq", [E, 128]), buf("wk", [CD, 128]), buf("wv", [CD, 128]), buf("wo", [128, E])
        bq, bk = buf("bq", [128, 1]), buf("bk", [128, 1])
        bv, bo = buf("bv", [SC, 128]), buf("bo", [128, E])
        xT, qT = buf("xT", [E, B, S]), buf("qT", [128, B, S])
        kT, v = buf("kT", [128, B, SC]), buf("v", [SC, B, 128])
        probs, pT = buf("probs", [S, B, SC]), buf("pT", [SC, B, S])
        attT, tb = buf("attT", [128, B, S]), buf("tb", [S, B, E])
        top, bias, total, part = (buf(w, [S, B]) for w in ("top", "bias", "total", "part"))
        bx, bqp, bkp, bvp, bs, bt, ba, bo_p = banks
        w_in = ev("weights_loaded")
        x_done, xT_ready = ev("x_turned"), ev("xT_ready")
        q_done, k_done, v_done = ev("q_done"), ev("k_done"), ev("v_done")
        q_ready, k_ready, v_ready = ev("q_ready"), ev("k_ready"), ev("v_ready")
        s_done, top_done, bias_done = ev("scores_done"), ev("top_done"), ev("bias_done")
        exp_done, part_done, probs_ready = ev("exp_done"), ev("part_done"), ev("probs_ready")
        p_done, pT_ready = ev("probs_turned"), ev("pT_ready")
        att_done, att_ready = ev("attended_done"), ev("attended_ready")
        o_done, tb_ready, t_ready, stored = ev("o_done"), ev("tb_ready"), ev("t_ready"), ev("stored")
        order = pipeline(6, GROUPS)

        with nc.Block() as block:
            @block.sync
            def _(sp):
                for dst, src in ((wq, a[f"{name}_xattn_Wq"]), (wk, a[f"{name}_xattn_Wk"]),
                                 (wv, a[f"{name}_xattn_Wv"]), (wo, a[f"{name}_xattn_Wo"])):
                    sp.dma_start(dst[:, :], src).then_inc(w_in, 16)
                for dst, src in ((bq, a[f"{name}_xattn_bq"]), (bk, a[f"{name}_xattn_bk"])):
                    sp.dma_start(dst[:, :], src.rearrange("(p o) -> p o", o=1)).then_inc(w_in, 16)
                for dst, src, rows in ((bv, a[f"{name}_xattn_bv"], SC), (bo, a[f"{name}_xattn_bo"], 128)):
                    sp.dma_start(dst[:, :], src.rearrange("(o n) -> o n", o=1).to_broadcast([rows, 128])).then_inc(w_in, 16)
                if out is not None:
                    for g in range(GROUPS):
                        sp.wait_ge(t_ready, g + 1)
                        sp.dma_start(out[g * BG:(g + 1) * BG].rearrange("b s e -> s b e"),
                                     t_all[:, g * BG:(g + 1) * BG, :]).then_inc(stored, 16)
                    sp.wait_ge(stored, 16 * GROUPS)

            @block.gpsimd
            def _(pool):
                pool.wait_ge(w_in, 128)
                nc.gpsimd.tensor_tensor(tb[:, :, :], t_all[:, :, :], bo[:, :].unsqueeze(1).to_broadcast([S, B, E]),
                                        ALU.add).then_inc(tb_ready, 1)

            @block.tensor
            def _(pe):
                pe.wait_ge(w_in, 128)
                for step, g in order:
                    bs_ = range(g * BG, (g + 1) * BG)
                    if step == 0:
                        wait(pe, xT_ready, g)
                        for j, b in enumerate(bs_):
                            last = nc.tensor.transpose(bx[:, j * S:(j + 1) * S], t_all[:, b, :], ident[:, :])
                        last.then_inc(x_done, 1)
                    if step == 1:
                        wait(pe, k_ready, g)
                        nc.tensor.matmul(bkp[:, 0:BG * SC], wk[:, :], ctxT[0:CD, g * BG:(g + 1) * BG, :],
                                         start=True, stop=True).then_inc(k_done, 1)
                        wait(pe, v_ready, g)
                        for j, b in enumerate(bs_):
                            last = nc.tensor.matmul(bvp[0:SC, j * 128:(j + 1) * 128], ctxT[0:CD, b, :], wv[:, :],
                                                    start=True, stop=True)
                        last.then_inc(v_done, 1)
                        pe.wait_ge(xT_ready, g + 1)
                        wait(pe, q_ready, g)
                        nc.tensor.matmul(bqp[:, :], wq[:, :], xT[:, g * BG:(g + 1) * BG, :],
                                         start=True, stop=True).then_inc(q_done, 1)
                    if step == 2:
                        pe.wait_ge(q_ready, g + 1)
                        pe.wait_ge(k_ready, g + 1)
                        wait(pe, exp_done, BG * g)
                        for j, b in enumerate(bs_):
                            last = nc.tensor.matmul(bs[:, j * SC:(j + 1) * SC], qT[:, b, :], kT[:, b, :],
                                                    start=True, stop=True)
                        last.then_inc(s_done, 1)
                    if step == 3:
                        pe.wait_ge(probs_ready, g + 1)
                        wait(pe, pT_ready, g)
                        for j, b in enumerate(bs_):
                            last = nc.tensor.transpose(bt[0:SC, j * S:(j + 1) * S], probs[:, b, :], ident[:, :])
                        last.then_inc(p_done, 1)
                    if step == 4:
                        pe.wait_ge(pT_ready, g + 1)
                        pe.wait_ge(v_ready, g + 1)
                        wait(pe, att_ready, g)
                        for j, b in enumerate(bs_):
                            last = nc.tensor.matmul(ba[:, j * S:(j + 1) * S], v[:, b, :], pT[:, b, :],
                                                    start=True, stop=True)
                        last.then_inc(att_done, 1)
                    if step == 5:
                        pe.wait_ge(att_ready, g + 1)
                        wait(pe, t_ready, g)
                        for j, b in enumerate(bs_):
                            last = nc.tensor.matmul(bo_p[:, j * E:(j + 1) * E], attT[:, b, :], wo[:, :],
                                                    start=True, stop=True)
                        last.then_inc(o_done, 1)

            @block.scalar
            def _(act):
                act.wait_ge(w_in, 128)
                for step, g in order:
                    gs = slice(g * BG, (g + 1) * BG)
                    if step == 0:
                        act.wait_ge(x_done, g + 1)
                        nc.scalar.activation(xT[:, gs, :], bx[:, :], ACT.Copy).then_inc(xT_ready, 1)
                    if step == 1:
                        act.wait_ge(q_done, g + 1)
                        nc.scalar.activation(qT[:, gs, :], bqp[:, :], ACT.Identity, bias=bq[:, 0:1]).then_inc(q_ready, 1)
                    if step == 2:
                        act.wait_ge(bias_done, g + 1)
                        for j in range(BG):
                            b = g * BG + j
                            nc.scalar.activation(probs[:, b, :], bs[:, j * SC:(j + 1) * SC], ACT.Exp, bias=bias[:, b:b + 1],
                                                 scale=SCALE1, accum_out=total[:, b:b + 1]).then_inc(exp_done, 1)
                    if step == 4:
                        act.wait_ge(att_done, g + 1)
                        nc.scalar.activation(attT[:, gs, :], ba[:, :], ACT.Copy).then_inc(att_ready, 1)

            @block.vector
            def _(dve):
                dve.wait_ge(w_in, 128)
                for step, g in order:
                    gs = slice(g * BG, (g + 1) * BG)
                    if step == 1:
                        dve.wait_ge(k_done, g + 1)
                        nc.vector.tensor_scalar(kT[:, gs, :], bkp[:, 0:BG * SC].rearrange("p (b k) -> p b k", b=BG),
                                                bk[:, 0:1], None, ALU.add).then_inc(k_ready, 1)
                        dve.wait_ge(v_done, g + 1)
                        nc.vector.tensor_tensor(v[:, gs, :], bvp[0:SC, :].rearrange("p (b k) -> p b k", b=BG),
                                                bv[:, :].unsqueeze(1).to_broadcast([SC, BG, 128]), ALU.add).then_inc(v_ready, 1)
                    if step == 2:
                        dve.wait_ge(s_done, g + 1)
                        nc.vector.tensor_reduce(top[:, gs], bs[:, 0:BG * SC].rearrange("p (b k) -> p b k", b=BG),
                                                AX.X, ALU.max).then_inc(top_done, 1)
                        dve.wait_ge(top_done, g + 1)
                        nc.vector.tensor_scalar(bias[:, gs], top[:, gs], -SCALE1, None, ALU.mult).then_inc(bias_done, 1)
                    if step == 3:
                        dve.wait_ge(exp_done, BG * (g + 1))
                        nc.vector.reciprocal(part[:, gs], total[:, gs]).then_inc(part_done, 1)
                        dve.wait_ge(part_done, g + 1)
                        nc.vector.tensor_tensor(probs[:, gs, :], probs[:, gs, :], bcast(part[:, gs], [S, BG, SC]),
                                                ALU.mult).then_inc(probs_ready, 1)
                        dve.wait_ge(p_done, g + 1)
                        nc.vector.tensor_copy(pT[:, gs, :], bt[0:SC, :].rearrange("p (b k) -> p b k", b=BG)).then_inc(pT_ready, 1)
                    if step == 5:
                        if g == 0:
                            dve.wait_ge(tb_ready, 1)
                        dve.wait_ge(o_done, g + 1)
                        nc.vector.tensor_tensor(t_all[:, gs, :], bo_p[:, :].rearrange("p (b k) -> p b k", b=BG),
                                                tb[:, gs, :], ALU.add).then_inc(t_ready, 1)


def l1(nc, a, sb, sem, banks, t_all, ctxT, ident):
    with ExitStack() as ctx:
        def buf(what, shape):
            return sb(f"L1_{what}", shape, F32, ctx)

        def ev(what):
            return sem(f"L1_{what}", ctx)

        wq, wk, wv = buf("wq", [E, 128]), buf("wk", [CD, 128]), buf("wv", [CD, 128])
        bq, bk, bv = buf("bq", [128, 1]), buf("bk", [128, 1]), buf("bv", [SC, 128])
        gamma, beta = buf("gamma", [128, E]), buf("beta", [128, E])
        xT, qT, kT = buf("xT", [E, B, S]), buf("qT", [128, B, S]), buf("kT", [128, B, SC])
        v, w = buf("v", [SC, B, 128]), buf("w", [SC, B, S])
        x1, z1, z2 = buf("x1", [S, B, E]), buf("z1", [S, B, E]), buf("z2", [S, B, E])
        top, bias, total, part = (buf(k, [SC, B]) for k in ("top", "bias", "total", "part"))
        stats, mv = buf("stats", [S, B, 6]), buf("mv", [S, B, 2])
        ve, rstd, mhalf = buf("ve", [S, B]), buf("rstd", [S, B]), buf("mhalf", [S, BG])
        bx, bqp, bkp, bvp, bs, bp = banks[0:6]
        w_in, x_done, xT_ready = ev("weights_loaded"), ev("x_turned"), ev("xT_ready")
        q_done, k_done, v_done = ev("q_done"), ev("k_done"), ev("v_done")
        q_ready, k_ready, v_ready = ev("q_ready"), ev("k_ready"), ev("v_ready")
        s_done, top_done, bias_done = ev("scores_done"), ev("top_done"), ev("bias_done")
        exp_done, part_done, w_ready = ev("exp_done"), ev("part_done"), ev("w_ready")
        pred_done, x1_ready, stats_done, mv_done = ev("pred_done"), ev("x1_ready"), ev("stats_done"), ev("mv_done")
        const_done, ve_done, rstd_done = ev("const_done"), ev("ve_done"), ev("rstd_done")
        z1_done, z2_done, t_ready = ev("z1_done"), ev("z2_done"), ev("t_ready")
        order = pipeline(5, GROUPS)

        with nc.Block() as block:
            @block.sync
            def _(sp):
                for dst, src in ((wq, a["L1_xattn_Wq"]), (wk, a["L1_xattn_Wk"]), (wv, a["L1_xattn_Wv"])):
                    sp.dma_start(dst[:, :], src).then_inc(w_in, 16)
                for dst, src in ((bq, a["L1_xattn_bq"]), (bk, a["L1_xattn_bk"])):
                    sp.dma_start(dst[:, :], src.rearrange("(p o) -> p o", o=1)).then_inc(w_in, 16)
                for dst, src, rows in ((bv, a["L1_xattn_bv"], SC), (gamma, a["L1_xattn_gamma"], 128),
                                       (beta, a["L1_xattn_beta"], 128)):
                    sp.dma_start(dst[:, :], src.rearrange("(o n) -> o n", o=1).to_broadcast([rows, 128])).then_inc(w_in, 16)

            @block.tensor
            def _(pe):
                pe.wait_ge(w_in, 128)
                for step, g in order:
                    bs_ = range(g * BG, (g + 1) * BG)
                    if step == 0:
                        wait(pe, xT_ready, g)
                        for j, b in enumerate(bs_):
                            last = nc.tensor.transpose(bx[:, j * S:(j + 1) * S], t_all[:, b, :], ident[:, :])
                        last.then_inc(x_done, 1)
                    if step == 1:
                        wait(pe, k_ready, g)
                        nc.tensor.matmul(bkp[:, 0:BG * SC], wk[:, :], ctxT[0:CD, g * BG:(g + 1) * BG, :],
                                         start=True, stop=True).then_inc(k_done, 1)
                        wait(pe, v_ready, g)
                        for j, b in enumerate(bs_):
                            last = nc.tensor.matmul(bvp[0:SC, j * 128:(j + 1) * 128], ctxT[0:CD, b, :], wv[:, :],
                                                    start=True, stop=True)
                        last.then_inc(v_done, 1)
                        pe.wait_ge(xT_ready, g + 1)
                        wait(pe, q_ready, g)
                        nc.tensor.matmul(bqp[:, :], wq[:, :], xT[:, g * BG:(g + 1) * BG, :],
                                         start=True, stop=True).then_inc(q_done, 1)
                    if step == 2:
                        pe.wait_ge(q_ready, g + 1)
                        pe.wait_ge(k_ready, g + 1)
                        wait(pe, exp_done, BG * g)
                        for j, b in enumerate(bs_):
                            last = nc.tensor.matmul(bs[0:SC, j * S:(j + 1) * S], kT[:, b, :], qT[:, b, :],
                                                    start=True, stop=True)
                        last.then_inc(s_done, 1)
                    if step == 3:
                        pe.wait_ge(w_ready, g + 1)
                        pe.wait_ge(v_ready, g + 1)
                        wait(pe, x1_ready, g)
                        for j, b in enumerate(bs_):
                            last = nc.tensor.matmul(bp[:, j * E:(j + 1) * E], w[:, b, :], v[:, b, :],
                                                    start=True, stop=True)
                        last.then_inc(pred_done, 1)

            @block.scalar
            def _(act):
                act.wait_ge(w_in, 128)
                for step, g in order:
                    gs = slice(g * BG, (g + 1) * BG)
                    if step == 0:
                        act.wait_ge(x_done, g + 1)
                        nc.scalar.activation(xT[:, gs, :], bx[:, :], ACT.Copy).then_inc(xT_ready, 1)
                    if step == 1:
                        act.wait_ge(q_done, g + 1)
                        nc.scalar.activation(qT[:, gs, :], bqp[:, :], ACT.Identity, bias=bq[:, 0:1]).then_inc(q_ready, 1)
                    if step == 2:
                        act.wait_ge(bias_done, g + 1)
                        for j in range(BG):
                            b = g * BG + j
                            nc.scalar.activation(w[:, b, :], bs[0:SC, j * S:(j + 1) * S], ACT.Exp, bias=bias[:, b:b + 1],
                                                 scale=SCALE1, accum_out=total[:, b:b + 1]).then_inc(exp_done, 1)

            @block.gpsimd
            def _(pool):
                nc.gpsimd.memset(mhalf[:, :], -0.5).then_inc(const_done, 1)
                pool.wait_ge(w_in, 128)
                pool.wait_ge(const_done, 1)
                for g in range(GROUPS):
                    gs = slice(g * BG, (g + 1) * BG)
                    pool.wait_ge(mv_done, BG * (g + 1))
                    nc.gpsimd.tensor_scalar(ve[:, gs], mv[:, gs, 1], L1_EPS, None, ALU.add).then_inc(ve_done, 1)
                    pool.wait_ge(ve_done, g + 1)
                    nc.gpsimd.tensor_tensor(rstd[:, gs], ve[:, gs], mhalf[:, :], ALU.pow).then_inc(rstd_done, 1)
                    pool.wait_ge(z1_done, BG * (g + 1))
                    nc.gpsimd.tensor_tensor(z2[:, gs, :], z1[:, gs, :], gamma[:, :].unsqueeze(1).to_broadcast([S, BG, E]),
                                            ALU.mult).then_inc(z2_done, 1)
                    pool.wait_ge(z2_done, g + 1)
                    nc.gpsimd.tensor_tensor(t_all[:, gs, :], z2[:, gs, :], beta[:, :].unsqueeze(1).to_broadcast([S, BG, E]),
                                            ALU.add).then_inc(t_ready, 1)

            @block.vector
            def _(dve):
                dve.wait_ge(w_in, 128)
                for step, g in order:
                    gs = slice(g * BG, (g + 1) * BG)
                    if step == 1:
                        dve.wait_ge(k_done, g + 1)
                        nc.vector.tensor_scalar(kT[:, gs, :], bkp[:, 0:BG * SC].rearrange("p (b k) -> p b k", b=BG),
                                                bk[:, 0:1], None, ALU.add).then_inc(k_ready, 1)
                        dve.wait_ge(v_done, g + 1)
                        nc.vector.tensor_tensor(v[:, gs, :], bvp[0:SC, :].rearrange("p (b k) -> p b k", b=BG),
                                                bv[:, :].unsqueeze(1).to_broadcast([SC, BG, 128]), ALU.add).then_inc(v_ready, 1)
                    if step == 2:
                        dve.wait_ge(s_done, g + 1)
                        nc.vector.tensor_reduce(top[:, gs], bs[0:SC, :].rearrange("p (b k) -> p b k", b=BG),
                                                AX.X, ALU.max).then_inc(top_done, 1)
                        dve.wait_ge(top_done, g + 1)
                        nc.vector.tensor_scalar(bias[:, gs], top[:, gs], -SCALE1, None, ALU.mult).then_inc(bias_done, 1)
                        dve.wait_ge(exp_done, BG * (g + 1))
                        nc.vector.reciprocal(part[:, gs], total[:, gs]).then_inc(part_done, 1)
                        dve.wait_ge(part_done, g + 1)
                        nc.vector.tensor_tensor(w[:, gs, :], w[:, gs, :], bcast(part[:, gs], [SC, BG, S]),
                                                ALU.mult).then_inc(w_ready, 1)
                    if step == 3:
                        dve.wait_ge(pred_done, g + 1)
                        nc.vector.tensor_tensor(x1[:, gs, :], bp[:, :].rearrange("p (b k) -> p b k", b=BG),
                                                t_all[:, gs, :], ALU.add).then_inc(x1_ready, 1)
                        dve.wait_ge(x1_ready, g + 1)
                        for b in range(g * BG, (g + 1) * BG):
                            nc.vector.bn_stats(stats[:, b, :], x1[:, b, :]).then_inc(stats_done, 1)
                        for b in range(g * BG, (g + 1) * BG):
                            dve.wait_ge(stats_done, b + 1)
                            nc.vector.bn_aggr(mv[:, b, :], stats[:, b, :]).then_inc(mv_done, 1)
                    if step == 4:
                        dve.wait_ge(rstd_done, g + 1)
                        for b in range(g * BG, (g + 1) * BG):
                            nc.vector.tensor_scalar(z1[:, b, :], x1[:, b, :], mv[:, b, 0:1], rstd[:, b:b + 1],
                                                    ALU.subtract, ALU.mult).then_inc(z1_done, 1)


def decoder(nc, a, sb_, sem_, banks, t_all, ctxT, ctx_all, ident, started, next_phase):
    with ExitStack() as ctx:
        def buf(name, shape, dt=F32):
            return sb_(f"L2_{name}", shape, dt, ctx)

        cq_all = buf("cq_all", [E, L, HD])
        co_all = buf("co_all", [128, L, NP, E])
        combine_cross_weights(nc, a, sb_, sem_, banks, cq_all, co_all)
        next_phase()

        wq, wk, wv = buf("wq", [E, HD]), buf("wk", [E, HD]), buf("wv", [E, HD])
        sa_wo, sa_ob = buf("sa_wo", [128, NP, E]), buf("sa_ob", [128, E])
        cq, co, ca_ob = buf("cq", [E, HD]), buf("co", [128, NP, E]), buf("ca_ob", [128, E])
        w1, b1, w2, b2 = buf("w1", [E, FF]), buf("b1", [128, NF]), buf("w2", [128, NF, E]), buf("b2", [128, E])
        pre_g, pre_b = buf("pre_g", [E, 1]), buf("pre_b", [E, 1])
        norm_g, norm_b = buf("norm_g", [E, 1]), buf("norm_b", [E, 1])
        sa_mask, ca_mask = buf("sa_mask", [S, B, S]), buf("ca_mask", [S, B, SC])
        sa_mask_now, ca_mask_now = buf("sa_mask_now", [S, S]), buf("ca_mask_now", [S, SC])
        ctx_keys, ctx_vals = buf("ctx_keys", [128, 2, SC]), buf("ctx_vals", [SC, CD])
        own_half = buf("own_half", [128, 2])
        qT, kT = buf("qT", [128, NP, S]), buf("kT", [128, NP, 2, S])
        v = buf("v", [S, HD])
        oT, c_oT = buf("oT", [128, NP, S]), buf("c_oT", [128, NP, S])
        cqT = buf("cqT", [128, NP, S])
        masked = [buf(f"masked{i}", [S, GH, S]) for i in range(2)]
        probs = [buf(f"probs{i}", [S, GH, S]) for i in range(2)]
        pT = [buf(f"pT{i}", [S, GH, S]) for i in range(2)]
        c_masked = [buf(f"c_masked{i}", [S, GH, SC]) for i in range(2)]
        c_probs = [buf(f"c_probs{i}", [S, GH, SC]) for i in range(2)]
        c_pT = [buf(f"c_pT{i}", [SC, GH, S]) for i in range(2)]
        least, total, part = buf("least", [S, H]), buf("total", [S, H]), buf("part", [S, H])
        c_least, c_total, c_part = buf("c_least", [S, H]), buf("c_total", [S, H]), buf("c_part", [S, H])
        hid = buf("hid", [128, NF, S])
        mhalf = buf("mhalf", [S, 1])

        def sem(name):
            return sem_(f"L2_{name}", ctx)

        def group_sems(name):
            return [sem(f"{name}{g}") for g in range(NG)]

        class Norm:
            def __init__(self, name):
                self.stats, self.mv = buf(f"{name}_stats", [S, 6]), buf(f"{name}_mv", [S, 2])
                self.ve, self.rstd = buf(f"{name}_ve", [S, 1]), buf(f"{name}_rstd", [S, 1])
                self.z, self.tnT, self.tb = buf(f"{name}_z", [S, E]), buf(f"{name}_tnT", [E, S]), buf(f"{name}_tb", [S, E])
                self.stats_done, self.mv_done = sem(f"{name}_stats_done"), sem(f"{name}_mv_done")
                self.ve_done, self.rstd_done = sem(f"{name}_ve_done"), sem(f"{name}_rstd_done")
                self.z_done, self.turned = sem(f"{name}_z_done"), sem(f"{name}_z_turned")
                self.tnT_ready, self.tb_ready = sem(f"{name}_tnT_ready"), sem(f"{name}_tb_ready")

        sa, ca, ff = Norm("sa"), Norm("ca"), Norm("ff")
        w_qkv, w_so, w_cq, w_co, w_ff = (sem(f"weights_{k}") for k in ("qkv", "so", "cq", "co", "ff"))
        load = [sem(f"load_{k}") for k in ("qkv", "so", "cq", "co", "ff", "const")]
        mask_in, mask_eq, masks_ready = sem("mask_in"), sem("mask_eq"), sem("masks_ready")
        zeros_done, const_done = sem("zeros_done"), sem("const_done")
        sa_mask_set, ca_mask_set, keys_set, vals_set = (sem(k) for k in ("sa_mask_set", "ca_mask_set", "keys_set", "vals_set"))
        sc_done, masked_done, exp_done, part_done, probs_ready, pt_done, pT_ready, pv_done, oT_ready = (
            group_sems(f"sa_{k}") for k in ("scores_done", "masked_done", "exp_done", "part_done", "probs_ready",
                                            "probs_turned", "pT_ready", "pv_done", "oT_ready"))
        csc_done, cmasked_done, cexp_done, cpart_done, cprobs_ready, cpt_done, cpT_ready, cpv_done, coT_ready = (
            group_sems(f"ca_{k}") for k in ("scores_done", "masked_done", "exp_done", "part_done", "probs_ready",
                                            "probs_turned", "pT_ready", "pv_done", "oT_ready"))
        q_done, k_done, v_done, q_ready, k_ready, v_ready = (
            [sem(f"sa_{k}{i}") for i in range(2)] for k in ("q_done", "k_done", "v_done", "q_ready", "k_ready", "v_ready"))
        cq_done, cq_ready = ([sem(f"ca_{k}{i}") for i in range(2)] for k in ("q_done", "q_ready"))
        o_done, co_done = sem("sa_o_done"), sem("ca_o_done")
        sa_out, ca_out, ff_out = sem("sa_out"), sem("ca_out"), sem("ff_out")
        up_done, hid_ready, down_done = sem("ff_up_done"), sem("ff_hid_ready"), sem("ff_down_done")
        pj_free = [sem(f"projection_bank_free{i}") for i in range(2)]

        sc_b, csc_b, pt_b, cpt_b, pv_b, cpv_b = banks[0:6]
        pj = banks[6:8]
        PJ_FULL = 6

        def stages(n):
            if not isinstance(n, int):
                return True, True, True, True
            return n + 1 < N, 0 <= n < N, 0 <= n - 1 < N, 0 <= n - 2 < N

        def run(eng, body):
            for n in range(-1, 3):
                body(n)
            with eng.Fori(3, N - 1) as n:
                body(n)
            for n in range(N - 1, N + 2):
                body(n)

        def hold(eng, sem, value):
            if not isinstance(value, int):
                eng.wait_ge(started, 1)
            wait(eng, sem, value)

        def counted(eng, n):
            if isinstance(n, int):
                at = {k: n + k for k in range(-2, 3)}
            else:
                at = {k: eng.alloc_register(f"count{k}") for k in range(-2, 3)}
                for k, register in at.items():
                    eng.reg_mov(register, n + k)
            return (lambda sem, k: wait(eng, sem, at[k])), (lambda sem, k: hold(eng, sem, at[k]))

        with nc.Block() as block:
            @block.sync
            def _(sp):
                l_qkv, l_so, l_cq, l_co, l_ff, l_const = load

                def rows(src, l, n):
                    return src[bass.ds(l, 1), :].to_broadcast([n, 128])

                def cols(src, l):
                    return src[bass.ds(l, 1), :].rearrange("o (c p) -> p (o c)", p=128)

                def load_qkv(l):
                    sp.dma_start(wk[:, :], a["sa_k"][bass.ds(l, 1)].rearrange("o p n -> (o p) n")).then_inc(l_qkv, 16)
                    sp.dma_start(wq[:, :], a["L2_xattn_sa_q"][bass.ds(l, 1)].rearrange("o p n -> (o p) n")).then_inc(l_qkv, 16)
                    sp.dma_start(wv[:, :], a["sa_v"][bass.ds(l, 1)].rearrange("o p n -> (o p) n")).then_inc(l_qkv, 16)

                def load_so(l):
                    sp.dma_start(sa_wo[:, :, :], a["L2_xattn_sa_ow"][bass.ds(l, 1)].rearrange("o (j p) n -> p (o j) n", p=128)).then_inc(l_so, 16)
                    sp.dma_start(sa_ob[:, :], rows(a["L2_xattn_sa_ob"], l, 128)).then_inc(l_so, 16)

                def load_cq(l):
                    sp.dma_start(cq[:, :], cq_all[:, bass.ds(l, 1), :].rearrange("p o n -> p (o n)")).then_inc(l_cq, 16)

                def load_co(l):
                    sp.dma_start(co[:, :, :], co_all[:, bass.ds(l, 1), :, :].rearrange("p o j n -> p (o j) n")).then_inc(l_co, 16)
                    sp.dma_start(ca_ob[:, :], rows(a["L2_xattn_ca_ob"], l, 128)).then_inc(l_co, 16)

                def load_ff(l):
                    sp.dma_start(w1[:, :], a["L2_xattn_ff_w1"][bass.ds(l, 1)].rearrange("o p n -> (o p) n")).then_inc(l_ff, 16)
                    sp.dma_start(w2[:, :, :], a["L2_xattn_ff_w2"][bass.ds(l, 1)].rearrange("o (j p) n -> p (o j) n", p=128)).then_inc(l_ff, 16)
                    sp.dma_start(b2[:, :], rows(a["L2_xattn_ff_b2"], l, 128)).then_inc(l_ff, 16)
                    sp.dma_start(b1[:, :], a["ffb1T"][bass.ds(l, 1)].rearrange("o p c -> (o p) c")).then_inc(l_ff, 16)
                    sp.dma_start(pre_g[:, :], cols(a["L2_xattn_pre_g"], l)).then_inc(l_ff, 16)
                    sp.dma_start(pre_b[:, :], cols(a["L2_xattn_pre_b"], l)).then_inc(l_ff, 16)

                def landed(sem, each, l, ready):
                    hold(sp, sem, (l + 1) * 16 * each)
                    sp.sem_inc(ready, B)

                load_qkv(0)
                for dst, src in ((norm_g, "L2_xattn_norm_g"), (norm_b, "L2_xattn_norm_b")):
                    sp.dma_start(dst[:, :], a[src].rearrange("(p o) -> p o", o=1)).then_inc(l_const, 16)
                sp.dma_start(sa_mask[:, :, :].bitcast(I32), a["mask_BxSxS_ik0"].rearrange("b q k -> q b k")).then_inc(mask_in, 16)
                sp.dma_start(ca_mask[:, :, :].bitcast(I32), a["mask_Bx1xS2_if1"].rearrange("b o k -> o b k").to_broadcast([S, B, SC])).then_inc(mask_in, 16)
                load_so(0)
                load_cq(0)
                load_co(0)
                load_ff(0)
                landed(l_qkv, 3, 0, w_qkv)
                landed(l_so, 2, 0, w_so)
                landed(l_cq, 1, 0, w_cq)
                landed(l_co, 2, 0, w_co)
                landed(l_ff, 6, 0, w_ff)
                with sp.Fori(1, L) as l:
                    hold(sp, v_done[1], l * B)
                    load_qkv(l)
                    landed(l_qkv, 3, l, w_qkv)
                    hold(sp, o_done, l * B)
                    hold(sp, sa.tb_ready, l * B)
                    load_so(l)
                    landed(l_so, 2, l, w_so)
                    hold(sp, cq_done[1], l * B)
                    load_cq(l)
                    landed(l_cq, 1, l, w_cq)
                    hold(sp, co_done, l * B)
                    hold(sp, ca.tb_ready, l * B)
                    load_co(l)
                    landed(l_co, 2, l, w_co)
                    hold(sp, down_done, l * B)
                    hold(sp, ff.tb_ready, l * B)
                    load_ff(l)
                    landed(l_ff, 6, l, w_ff)

            @block.tensor
            def _(pe):
                pe.wait_ge(const_done, 1)

                def turn(need, st, now, bank):
                    need(st.z_done, now)
                    nc.tensor.transpose(bank[:, 0:S], st.z[:, :], ident[:, :]).then_inc(st.turned, 1)

                def body(n):
                    need, held = counted(pe, n)
                    run_qkv, run_sa, run_ca, run_ff = stages(n)
                    qkv_now, sa_now, ca_now, ff_now = 2, 1, 0, -1
                    edge = {-1: [0, 0], 0: [3, 3], 1: [7, 6], 2: [12, 11],
                            N: [PJ_FULL * N - 3, PJ_FULL * N - 4], N + 1: [PJ_FULL * N - 1, PJ_FULL * N - 1]}
                    used = edge[n] if isinstance(n, int) and n in edge else [PJ_FULL * n, PJ_FULL * n - 1]

                    def bank(i):
                        wait(pe, pj_free[i], used[i])
                        used[i] = used[i] + 1
                        return pj[i]

                    def project_T(weights, rhs, i, done, ready):
                        out = bank(i)
                        for j in range(4):
                            c = 4 * i + j
                            last = nc.tensor.matmul(out[:, j * S:(j + 1) * S], weights[:, c * 128:(c + 1) * 128], rhs,
                                                    start=True, stop=True)
                        last.then_inc(done, 1)

                    def sa_scores(g):
                        need(q_ready[g // 2], sa_now)
                        need(k_ready[g // 2], sa_now)
                        need(masked_done[(g - 1) % NG], sa_now if g else sa_now - 1)
                        for j in range(2):
                            p = 2 * g + j
                            last = nc.tensor.matmul(sc_b[:, j * 2 * S:(j + 1) * 2 * S], qT[:, p, :], kT[:, p, :, :],
                                                    start=True, stop=True)
                        last.then_inc(sc_done[g], 1)

                    def ca_scores(g):
                        need(cq_ready[g // 2], ca_now)
                        if g == 0:
                            need(keys_set, ca_now)
                        need(cmasked_done[(g - 1) % NG], ca_now if g else ca_now - 1)
                        for j in range(2):
                            p = 2 * g + j
                            last = nc.tensor.matmul(csc_b[:, j * 2 * SC:(j + 1) * 2 * SC], cqT[:, p, :], ctx_keys[:, :, :],
                                                    start=True, stop=True)
                        last.then_inc(csc_done[g], 1)

                    def sa_values(g):
                        need(probs_ready[g], sa_now)
                        need(pT_ready[(g - 1) % NG], sa_now if g else sa_now - 1)
                        if g == 3 and run_qkv:
                            need(sa.tnT_ready, qkv_now)
                        for j in range(GH):
                            last = nc.tensor.transpose(pt_b[:, j * S:(j + 1) * S], probs[g % 2][:, j, :], ident[:, :])
                        last.then_inc(pt_done[g], 1)

                    def sa_outputs(g):
                        need(pT_ready[g], sa_now)
                        need(v_ready[g // 2], sa_now)
                        need(oT_ready[(g - 1) % NG], sa_now if g else sa_now - 1)
                        for j in range(GH):
                            h, half = g * GH + j, j % 2
                            last = nc.tensor.matmul(pv_b[half * D:(half + 1) * D, (j // 2) * S:(j // 2 + 1) * S],
                                                    v[:, h * D:(h + 1) * D], pT[g % 2][:, j, :], start=True, stop=True)
                        last.then_inc(pv_done[g], 1)

                    def ca_values(g):
                        need(cprobs_ready[g], ca_now)
                        need(cpT_ready[(g - 1) % NG], ca_now if g else ca_now - 1)
                        for j in range(GH):
                            last = nc.tensor.transpose(cpt_b[0:SC, j * S:(j + 1) * S], c_probs[g % 2][:, j, :], ident[:, :])
                        last.then_inc(cpt_done[g], 1)

                    def ca_outputs(g):
                        need(cpT_ready[g], ca_now)
                        if g == 0:
                            need(vals_set, ca_now)
                            if run_ff:
                                need(ff.tnT_ready, ff_now)
                        need(coT_ready[(g - 1) % NG], ca_now if g else ca_now - 1)
                        pairs = c_pT[g % 2][:, :, :].rearrange("k (j e) q -> k j e q", e=2)
                        for half in range(2):
                            last = nc.tensor.matmul(cpv_b[half * D:(half + 1) * D, 0:2 * S], ctx_vals[:, :],
                                                    pairs[:, :, half, :], start=True, stop=True)
                        last.then_inc(cpv_done[g], 1)

                    def out_projection(oT, wo, i, done):
                        out = bank(i)
                        for p in range(NP):
                            last = nc.tensor.matmul(out[:, 0:E], oT[:, p, :], wo[:, p, :], start=(p == 0), stop=(p == NP - 1))
                        last.then_inc(done, 1)

                    if run_ca:
                        need(cpT_ready[NG - 1], ca_now - 1)
                        turn(need, ca, ca_now, cpt_b)
                    if run_sa:
                        sa_scores(0)
                    if run_ca:
                        need(ca.tnT_ready, ca_now)
                        need(w_cq, ca_now)
                        for i in range(2):
                            project_T(cq, ca.tnT[:, :], i, cq_done[i], cq_ready[i])
                    if run_sa:
                        sa_scores(1)
                    if run_ff:
                        need(coT_ready[NG - 1], ff_now)
                        turn(need, ff, ff_now, cpv_b)
                    if run_ca:
                        ca_scores(0)
                    if run_sa:
                        sa_values(0)
                    if run_ff:
                        need(ff.tnT_ready, ff_now)
                        need(w_ff, ff_now)
                        up = bank(0)
                        for c in range(NF):
                            last = nc.tensor.matmul(up[:, c * S:(c + 1) * S], w1[:, c * 128:(c + 1) * 128], ff.tnT[:, :],
                                                    start=True, stop=True)
                        last.then_inc(up_done, 1)
                    if run_sa:
                        sa_outputs(0)
                        sa_scores(2)
                    if run_ca:
                        ca_scores(1)
                    if run_sa:
                        sa_values(1)
                    if run_ca:
                        ca_values(0)
                    if run_sa:
                        sa_outputs(1)
                        sa_scores(3)
                    if run_ca:
                        ca_outputs(0)
                    if run_ff:
                        need(hid_ready, ff_now)
                        down = bank(1)
                        for c in range(NF):
                            last = nc.tensor.matmul(down[:, 0:E], hid[:, c, :], w2[:, c, :], start=(c == 0), stop=(c == NF - 1))
                        last.then_inc(down_done, 1)
                    if run_ca:
                        ca_scores(2)
                    if run_sa:
                        sa_values(2)
                    if run_ca:
                        ca_values(1)
                    if run_sa:
                        sa_outputs(2)
                    if run_qkv:
                        if run_sa:
                            need(pT_ready[2], sa_now)
                        turn(need, sa, qkv_now, pt_b)
                    if run_ca:
                        ca_outputs(1)
                        ca_scores(3)
                    if run_qkv:
                        need(sa.tnT_ready, qkv_now)
                        need(w_qkv, qkv_now)
                        for i in range(2):
                            project_T(wq, sa.tnT[:, :], i, q_done[i], q_ready[i])
                    if run_sa:
                        sa_values(3)
                    if run_qkv:
                        for i in range(2):
                            project_T(wk, sa.tnT[:, :], i, k_done[i], k_ready[i])
                    if run_ca:
                        ca_values(2)
                    if run_sa:
                        sa_outputs(3)
                    if run_qkv:
                        for i in range(2):
                            out = bank(i)
                            nc.tensor.matmul(out[:, :], sa.tnT[:, :], wv[:, i * 512:(i + 1) * 512],
                                             start=True, stop=True).then_inc(v_done[i], 1)
                    if run_ca:
                        ca_outputs(2)
                    if run_sa:
                        need(oT_ready[NG - 1], sa_now)
                        need(w_so, sa_now)
                        out_projection(oT, sa_wo, 0, o_done)
                    if run_ca:
                        ca_values(3)
                        ca_outputs(3)
                        need(coT_ready[NG - 1], ca_now)
                        need(w_co, ca_now)
                        out_projection(c_oT, co, 1, co_done)

                run(pe, body)

            @block.scalar
            def _(act):
                act.wait_ge(load[5], 32)

                def body(n):
                    need, held = counted(act, n)
                    run_qkv, run_sa, run_ca, run_ff = stages(n)
                    qkv_now, sa_now, ca_now, ff_now = 2, 1, 0, -1

                    def affine(st, now, bank, gain, offset, users):
                        need(st.turned, now)
                        for user in users:
                            need(user, now - 1)
                        nc.scalar.activation(st.tnT[:, :], bank[:, 0:S], ACT.Identity, bias=offset[:, 0:1],
                                             scale=gain[:, 0:1]).then_inc(st.tnT_ready, 1)

                    def exps(g, now, masked_d, masked, least, probs, total, turned, done, w):
                        need(masked_d[g], now)
                        need(turned[(g - 2) % NG], now if g >= 2 else now - 1)
                        for j in range(GH):
                            h = g * GH + j
                            last = nc.scalar.activation(probs[g % 2][:, j, :], masked[g % 2][:, j, :], ACT.Exp,
                                                        bias=least[:, h:h + 1], scale=-1.0, accum_out=total[:, h:h + 1])
                        last.then_inc(done[g], 1)

                    def sa_exps(g):
                        exps(g, sa_now, masked_done, masked, least, probs, total, pt_done, exp_done, S)

                    def ca_exps(g):
                        exps(g, ca_now, cmasked_done, c_masked, c_least, c_probs, c_total, cpt_done, cexp_done, SC)

                    if run_ca:
                        affine(ca, ca_now, cpt_b, norm_g, norm_b, [cq_done[1]])
                    if run_sa:
                        sa_exps(0)
                    if run_ca:
                        for i in range(2):
                            need(cq_done[i], ca_now)
                            need(csc_done[NG - 1], ca_now - 1)
                            nc.scalar.activation(cqT[:, 4 * i:4 * i + 4, :], pj[i][:, :], ACT.Copy).then_inc(cq_ready[i], 1)
                            need(cq_ready[i], ca_now)
                            act.sem_inc(pj_free[i], 1)
                    if run_sa:
                        sa_exps(1)
                    if run_ff:
                        need(w_ff, ff_now)
                        affine(ff, ff_now, cpv_b, pre_g, pre_b, [up_done])
                    if run_ca:
                        ca_exps(0)
                    if run_sa:
                        sa_exps(2)
                    if run_ca:
                        ca_exps(1)
                    if run_sa:
                        sa_exps(3)
                    if run_ca:
                        ca_exps(2)
                    if run_qkv:
                        affine(sa, qkv_now, pt_b, norm_g, norm_b, [v_done[1]])
                    if run_ca:
                        ca_exps(3)
                    if run_qkv:
                        for i in range(2):
                            need(q_done[i], qkv_now)
                            need(sc_done[NG - 1], qkv_now - 1)
                            nc.scalar.activation(qT[:, 4 * i:4 * i + 4, :], pj[i][:, :], ACT.Copy,
                                                 scale=-(D ** -0.5)).then_inc(q_ready[i], 1)
                            need(q_ready[i], qkv_now)
                            act.sem_inc(pj_free[i], 1)
                        for i in range(2):
                            need(k_done[i], qkv_now)
                            nc.scalar.activation(kT[0:D, 4 * i:4 * i + 4, 0, :], pj[i][0:D, :].rearrange("p (c k) -> p c k", c=4), ACT.Copy)
                            nc.scalar.activation(kT[D:128, 4 * i:4 * i + 4, 1, :], pj[i][D:128, :].rearrange("p (c k) -> p c k", c=4),
                                                 ACT.Copy).then_inc(k_ready[i], 1)
                            need(k_ready[i], qkv_now)
                            act.sem_inc(pj_free[i], 1)

                run(act, body)

            @block.gpsimd
            def _(pool):
                nc.gpsimd.memset(mhalf[:, :], -0.5).then_inc(zeros_done, 1)
                nc.gpsimd.memset(kT[:, :, :, :], 0.0).then_inc(zeros_done, 1)
                pool.wait_ge(zeros_done, 2)
                pool.sem_inc(const_done, 1)

                def body(n):
                    need, held = counted(pool, n)
                    run_qkv, run_sa, run_ca, run_ff = stages(n)
                    qkv_now, sa_now, ca_now, ff_now = 2, 1, 0, -1

                    def rstd(st, now):
                        held(st.mv_done, now)
                        nc.gpsimd.tensor_scalar(st.ve[:, :], st.mv[:, 1:2], LN_EPS, None, ALU.add).then_inc(st.ve_done, 1)
                        held(st.ve_done, now)
                        nc.gpsimd.tensor_tensor(st.rstd[:, :], st.ve[:, :], mhalf[:, :], ALU.pow).then_inc(st.rstd_done, 1)

                    def plus_bias(st, now, batch, bias, loaded, used):
                        held(loaded, now)
                        held(used, now - 1)
                        nc.gpsimd.tensor_tensor(st.tb[:, :], t_all[:, bass.ds(batch, 1), :].rearrange("p o e -> p (o e)"),
                                                bias[:, :], ALU.add).then_inc(st.tb_ready, 1)

                    def normalise(g, now, parts, probs, part, ready, w):
                        held(parts[g], now)
                        nc.gpsimd.tensor_tensor(probs[g % 2][:, :, :], probs[g % 2][:, :, :],
                                                bcast(part[:, g * GH:(g + 1) * GH], [S, GH, w]), ALU.mult).then_inc(ready[g], 1)

                    def sa_norm(g):
                        normalise(g, sa_now, part_done, probs, part, probs_ready, S)

                    def ca_norm(g):
                        normalise(g, ca_now, cpart_done, c_probs, c_part, cprobs_ready, SC)

                    if run_ff:
                        rstd(ff, ff_now)
                        plus_bias(ff, ff_now, (n - 2) % B, b2, w_ff, ff_out)
                    if run_ca:
                        b = (n - 1) % B
                        held(csc_done[NG - 1], ca_now - 1)
                        nc.gpsimd.tensor_tensor(ctx_keys[:, :, :], ctxT[:, bass.ds(b, 1), :].to_broadcast([128, 2, SC]),
                                                bcast(own_half[:, :], [128, 2, SC]), ALU.mult).then_inc(keys_set, 1)
                        held(cmasked_done[NG - 1], ca_now - 1)
                        nc.gpsimd.tensor_copy(ca_mask_now[:, :], ca_mask[:, bass.ds(b, 1), :].rearrange("p o k -> p (o k)")).then_inc(ca_mask_set, 1)
                    if run_sa:
                        sa_norm(0)
                    if run_ca:
                        held(cpv_done[NG - 1], ca_now - 1)
                        nc.gpsimd.tensor_copy(ctx_vals[:, :], ctx_all[:, bass.ds(b, 1), :].rearrange("p o k -> p (o k)")).then_inc(vals_set, 1)
                    if run_sa:
                        sa_norm(1)
                    if run_ca:
                        ca_norm(0)
                        plus_bias(ca, ca_now, (n - 1) % B, ca_ob, w_co, ca_out)
                    if run_sa:
                        sa_norm(2)
                    if run_ca:
                        ca_norm(1)
                    if run_qkv:
                        rstd(sa, qkv_now)
                    if run_sa:
                        plus_bias(sa, sa_now, n % B, sa_ob, w_so, sa_out)
                        sa_norm(3)
                    if run_qkv:
                        if run_sa:
                            held(masked_done[NG - 1], sa_now)
                        nc.gpsimd.tensor_copy(sa_mask_now[:, :], sa_mask[:, bass.ds((n + 1) % B, 1), :].rearrange("p o k -> p (o k)")).then_inc(sa_mask_set, 1)
                    if run_ca:
                        ca_norm(2)
                        ca_norm(3)
                    if run_sa:
                        rstd(ca, sa_now)

                pool.wait_ge(masks_ready, 5)
                run(pool, body)

            @block.vector
            def _(dve):
                nc.vector.memset(own_half[:, :], 0.0).then_inc(masks_ready, 1)
                dve.wait_ge(masks_ready, 1)
                for half in range(2):
                    nc.vector.memset(own_half[half * D:(half + 1) * D, half:half + 1], 1.0).then_inc(masks_ready, 1)
                dve.wait_ge(mask_in, 32)
                for m in (sa_mask, ca_mask):
                    nc.vector.tensor_scalar(m[:, :, :], m[:, :, :].bitcast(I32), 0.0, MASKED, ALU.is_equal, ALU.mult).then_inc(masks_ready, 1)

                def body(n):
                    need, held = counted(dve, n)
                    run_qkv, run_sa, run_ca, run_ff = stages(n)
                    qkv_now, sa_now, ca_now, ff_now = 2, 1, 0, -1

                    def rows_of(batch):
                        return t_all[:, bass.ds(batch, 1), :].rearrange("p o e -> p (o e)")

                    def stats(st, now, batch, written):
                        if written is not None:
                            held(*written)
                        nc.vector.bn_stats(st.stats[:, :], rows_of(batch)).then_inc(st.stats_done, 1)
                        held(st.stats_done, now)
                        held(st.ve_done, now - 1)
                        nc.vector.bn_aggr(st.mv[:, :], st.stats[:, :]).then_inc(st.mv_done, 1)

                    def centre(st, now, batch):
                        held(st.rstd_done, now)
                        held(st.turned, now - 1)
                        nc.vector.tensor_scalar(st.z[:, :], rows_of(batch), st.mv[:, 0:1], st.rstd[:, 0:1],
                                                ALU.subtract, ALU.mult).then_inc(st.z_done, 1)

                    def mask(g, now, done, bank, mask, mask_set, masked, least, exps, ready, w):
                        held(done[g], now)
                        held(mask_set, now)
                        held(exps[(g - 2) % NG], now if g >= 2 else now - 1)
                        for j in range(GH):
                            h = g * GH + j
                            last = nc.vector.tensor_tensor_reduce(out=masked[g % 2][:, j, :], in0=bank[:, j * w:(j + 1) * w], in1=mask[:, :],
                                                                  scale=1.0, scalar=3e38, op0=ALU.add, op1=ALU.min,
                                                                  accum_out=least[:, h:h + 1])
                        last.then_inc(ready[g], 1)

                    def sa_mask_(g):
                        mask(g, sa_now, sc_done, sc_b, sa_mask_now, sa_mask_set, masked, least, exp_done, masked_done, S)

                    def ca_mask_(g):
                        mask(g, ca_now, csc_done, csc_b, ca_mask_now, ca_mask_set, c_masked, c_least, cexp_done, cmasked_done, SC)

                    def over(g, now, exps, total, part, done):
                        need(exps[g], now)
                        nc.vector.reciprocal(part[:, g * GH:(g + 1) * GH], total[:, g * GH:(g + 1) * GH]).then_inc(done[g], 1)

                    def sa_over(g):
                        over(g, sa_now, exp_done, total, part, part_done)

                    def ca_over(g):
                        over(g, ca_now, cexp_done, c_total, c_part, cpart_done)

                    def take_pT(g, now, turned, bank, rows, pT, users, ready):
                        need(turned[g], now)
                        need(users[(g - 2) % NG], now if g >= 2 else now - 1)
                        nc.vector.tensor_copy(pT[g % 2][:, :, :], bank[0:rows, :].rearrange("p (j q) -> p j q", j=GH)).then_inc(ready[g], 1)

                    def sa_pT(g):
                        take_pT(g, sa_now, pt_done, pt_b, S, pT, pv_done, pT_ready)

                    def ca_pT(g):
                        take_pT(g, ca_now, cpt_done, cpt_b, SC, c_pT, cpv_done, cpT_ready)

                    def take_oT(g, now, done, bank, oT, projected, ready):
                        need(done[g], now)
                        need(projected, now - 1)
                        nc.vector.tensor_copy(oT[:, 2 * g:2 * g + 2, :], bank[:, 0:2 * S].rearrange("p (j q) -> p j q", j=2)).then_inc(ready[g], 1)

                    def sa_oT(g):
                        take_oT(g, sa_now, pv_done, pv_b, oT, o_done, oT_ready)

                    def ca_oT(g):
                        take_oT(g, ca_now, cpv_done, cpv_b, c_oT, co_done, coT_ready)

                    def add_out(st, now, batch, done, i, out):
                        held(st.tb_ready, now)
                        held(done, now)
                        nc.vector.tensor_tensor(rows_of(batch), pj[i][:, 0:E], st.tb[:, :], ALU.add).then_inc(out, 1)
                        need(out, now)
                        dve.sem_inc(pj_free[i], 1)

                    if run_ff:
                        stats(ff, ff_now, (n - 2) % B, (ca_out, ff_now))
                    if run_sa:
                        sa_mask_(0)
                    if run_ff:
                        centre(ff, ff_now, (n - 2) % B)
                    if run_sa:
                        sa_mask_(1)
                        sa_over(0)
                    if run_ca:
                        ca_mask_(0)
                    if run_sa:
                        sa_pT(0)
                        sa_over(1)
                    if run_ff:
                        need(up_done, ff_now)
                        need(down_done, ff_now - 1)
                        for c in range(NF):
                            last = nc.vector.tensor_scalar(hid[:, c, :], pj[0][:, c * S:(c + 1) * S], b1[:, c:c + 1], 0.0,
                                                           ALU.add, ALU.max)
                        last.then_inc(hid_ready, 1)
                        need(hid_ready, ff_now)
                        dve.sem_inc(pj_free[0], 1)
                    if run_sa:
                        sa_oT(0)
                        sa_mask_(2)
                    if run_ca:
                        ca_over(0)
                        ca_mask_(1)
                    if run_sa:
                        sa_pT(1)
                    if run_ca:
                        ca_pT(0)
                    if run_sa:
                        sa_oT(1)
                        sa_mask_(3)
                        sa_over(2)
                    if run_ca:
                        ca_oT(0)
                        ca_over(1)
                    if run_ff:
                        add_out(ff, ff_now, (n - 2) % B, down_done, 1, ff_out)
                    if run_qkv:
                        stats(sa, qkv_now, (n + 1) % B, None)
                    if run_ca:
                        ca_mask_(2)
                    if run_sa:
                        sa_pT(2)
                    if run_ca:
                        ca_pT(1)
                    if run_qkv:
                        centre(sa, qkv_now, (n + 1) % B)
                    if run_sa:
                        sa_oT(2)
                        sa_over(3)
                    if run_ca:
                        ca_oT(1)
                        ca_over(2)
                        ca_mask_(3)
                    if run_sa:
                        sa_pT(3)
                    if run_ca:
                        ca_pT(2)
                        ca_over(3)
                    if run_sa:
                        sa_oT(3)
                    if run_qkv:
                        for i in range(2):
                            need(v_done[i], qkv_now)
                            need(pv_done[NG - 1], qkv_now - 1)
                            nc.vector.tensor_copy(v[:, i * 512:(i + 1) * 512], pj[i][:, :]).then_inc(v_ready[i], 1)
                            need(v_ready[i], qkv_now)
                            dve.sem_inc(pj_free[i], 1)
                    if run_ca:
                        ca_oT(2)
                    if run_sa:
                        add_out(sa, sa_now, n % B, o_done, 0, sa_out)
                        stats(ca, sa_now, n % B, (sa_out, sa_now))
                    if run_ca:
                        ca_pT(3)
                        ca_oT(3)
                    if run_sa:
                        centre(ca, sa_now, n % B)
                    if run_ca:
                        add_out(ca, ca_now, (n - 1) % B, co_done, 1, ca_out)

                run(dve, body)


def combine_cross_weights(nc, a, sb, sem, banks, cq_all, co_all):
    with ExitStack() as ctx:
        def buf(what, shape):
            return sb(f"comb_{what}", shape, F32, ctx)

        qw, ow = ([buf(f"{k}{i}", [128, NP, 128]) for i in range(2)] for k in ("q", "o"))
        kw, vw = ([buf(f"{k}{i}", [128, NP, 2, CD]) for i in range(2)] for k in ("k", "v"))
        w_in = [sem(f"comb_loaded{i}", ctx) for i in range(2)]
        zeroed = sem("comb_zeroed", ctx)
        g_done, n_done, g_ready, n_ready = (
            [sem(f"comb_{k}{i}", ctx) for i in range(2)] for k in ("g_done", "n_done", "g_ready", "n_ready"))
        with nc.Block() as block:
            @block.sync
            def _(sp):
                sp.wait_ge(zeroed, 4)
                for l in range(L):
                    i = l % 2
                    if l >= 2:
                        sp.wait_ge(n_done[1], l - 1)
                    sp.dma_start(qw[i][:, :, :], a["caqT"][l].rearrange("(j p) n -> p j n", p=128)).then_inc(w_in[i], 16)
                    sp.dma_start(ow[i][:, :, :], a["L2_xattn_ca_ow"][l].rearrange("(j p) n -> p j n", p=128)).then_inc(w_in[i], 16)
                    for w, src in ((kw, a["cakT"]), (vw, a["cavT"])):
                        for half in range(2):
                            sp.dma_start(w[i][half * D:(half + 1) * D, :, half, :],
                                         src[l].rearrange("(j e p) n -> e p j n", e=2, p=D)[half]).then_inc(w_in[i], 16)

            @block.gpsimd
            def _(pool):
                for w in (*kw, *vw):
                    nc.gpsimd.memset(w[:, :, :, :], 0.0).then_inc(zeroed, 1)

            @block.tensor
            def _(pe):
                for l in range(L):
                    i = l % 2
                    pe.wait_ge(w_in[i], 96 * (l // 2 + 1))
                    for c in range(2):
                        wait(pe, g_ready[c], l)
                        for j in range(4):
                            p = 4 * c + j
                            last = nc.tensor.matmul(banks[c][:, j * 128:(j + 1) * 128], qw[i][:, p, :], kw[i][:, p, :, :],
                                                    start=True, stop=True)
                        last.then_inc(g_done[c], 1)
                    for c in range(2):
                        wait(pe, n_ready[c], l)
                        for j in range(4):
                            p = 4 * c + j
                            last = nc.tensor.matmul(banks[2 + c][:, j * 128:(j + 1) * 128], vw[i][:, p, :, :], ow[i][:, p, :],
                                                    start=True, stop=True)
                        last.then_inc(n_done[c], 1)

            @block.scalar
            def _(act):
                for l in range(L):
                    for c in range(2):
                        act.wait_ge(g_done[c], l + 1)
                        nc.scalar.activation(cq_all[:, l, c * 512:(c + 1) * 512], banks[c][:, :], ACT.Copy,
                                             scale=-(D ** -0.5)).then_inc(g_ready[c], 1)

            @block.vector
            def _(dve):
                for l in range(L):
                    for c in range(2):
                        dve.wait_ge(n_done[c], l + 1)
                        nc.vector.tensor_copy(co_all[:, l, 4 * c:4 * c + 4, :],
                                              banks[2 + c][:, :].rearrange("p (j n) -> p j n", j=4)).then_inc(n_ready[c], 1)


_AS_THEY_ARE = [f"{m}_xattn_{k}" for m in ("L0", "L3") for k in ("Wq", "bq", "Wk", "bk", "Wv", "bv", "Wo", "bo")] + \
    [f"L1_xattn_{k}" for k in ("Wq", "bq", "Wk", "bk", "Wv", "bv", "gamma", "beta")] + \
    [f"L2_xattn_{k}" for k in ("norm_g", "norm_b", "sa_q", "sa_ow", "sa_ob", "ca_ow", "ca_ob", "ff_w1",
                               "ff_w2", "ff_b2", "pre_g", "pre_b")] + \
    ["x", "ctx_512", "mask_BxSxS_ik0", "mask_Bx1xS2_if1"]


def kernel(**inputs):
    import numpy as np
    import concourse.bacc as bacc
    from concourse.bass_utils import run_bass_kernel_spmd

    laid = {k: inputs[k] for k in _AS_THEY_ARE}
    kv, ckv = np.asarray(inputs["L2_xattn_sa_kv"]), np.asarray(inputs["L2_xattn_ca_kv"])
    laid["sa_k"], laid["sa_v"] = kv[:, :, :HD], kv[:, :, HD:]
    laid["cakT"], laid["cavT"] = ckv[:, :, :HD].transpose(0, 2, 1), ckv[:, :, HD:].transpose(0, 2, 1)
    laid["caqT"] = np.asarray(inputs["L2_xattn_ca_q"]).transpose(0, 2, 1)
    laid["ffb1T"] = np.asarray(inputs["L2_xattn_ff_b1"]).reshape(L, NF, 128).transpose(0, 2, 1)
    laid["ctxT"] = np.asarray(inputs["ctx_512"]).transpose(2, 0, 1)

    nc = bacc.Bacc("TRN2", target_bir_lowering=False, num_devices=1)
    arrays, args = {}, {}
    for name, value in laid.items():
        value = np.ascontiguousarray(value)
        arrays[f"in_{name}"] = value
        args[name] = nc.dram_tensor(f"in_{name}", value.shape, mybir.dt.from_np(value.dtype), kind="ExternalInput").ap()
    args["out"] = nc.dram_tensor("out_t", (B, S, E), F32, kind="ExternalOutput").ap()
    build(nc, args)
    r = run_bass_kernel_spmd(nc, [arrays], core_ids=[0])
    return r.results[0]["out_t"]
```

```python
from contextlib import ExitStack

import concourse.bass as bass
from concourse import mybir

F32 = mybir.dt.float32
I32 = mybir.dt.int32
ALU = mybir.AluOpType
ACT = mybir.ActivationFunctionType
AX = mybir.AxisListType

B, S, E = 16, 128, 128
SC, CD = 120, 64
L, H, D = 6, 16, 64
HD = H * D
FF = 512
NP = H // 2
NG = 4
GH = H // NG
NF = FF // 128
N = L * B
BG = 4
GROUPS = B // BG
MASKED = 1e30
LN_EPS, L1_EPS = 1e-5, 1e-6
SCALE1 = 128 ** -0.5


def wait(eng, sem, value):
    if isinstance(value, int) and value <= 0:
        return
    eng.wait_ge(sem, value)


def bcast(ap, shape):
    return ap.unsqueeze(2).to_broadcast(shape)


def pipeline(kinds, groups):
    return [(k, tick - k) for tick in range(kinds + groups - 1) for k in reversed(range(kinds))
            if 0 <= tick - k < groups]


def build(nc, a):
    with ExitStack() as ctx:
        def sb(name, shape, dt=F32, scope=ctx):
            return scope.enter_context(nc.sbuf_tensor(name, shape, dt))

        phase_sems = []

        def sem(name, scope=ctx):
            if scope is ctx:
                return ctx.enter_context(nc.semaphore(name))
            phase_sems.append(nc.alloc_semaphore(name=name))
            return phase_sems[-1]

        def next_phase():
            nc.clear_and_free_semaphores(phase_sems)
            phase_sems.clear()
            nc.all_engine_barrier()

        banks = [ctx.enter_context(nc.psum_tensor(f"bank{i}", [128, 512], F32)) for i in range(8)]

        t_all = sb("t_all", [128, B, E])
        ctxT = sb("ctxT", [128, B, SC])
        ctx_all = sb("ctx_all", [SC, B, CD])
        ident = sb("ident", [128, 128])
        started = sem("started")

        load_and_l0(nc, a, sb, sem, banks, t_all, ctxT, ctx_all, ident, started)
        next_phase()
        l1(nc, a, sb, sem, banks, t_all, ctxT, ident)
        next_phase()
        decoder(nc, a, sb, sem, banks, t_all, ctxT, ctx_all, ident, started, next_phase)
        next_phase()
        query_context(nc, a, "L3", sb, sem, banks, t_all, ctxT, ident, a["out"])


def load_and_l0(nc, a, sb, sem, banks, t_all, ctxT, ctx_all, ident, started):
    loaded, zeroed, made = sem("inputs_loaded"), sem("ident_zeroed"), sem("ident_made")
    with nc.Block() as block:
        @block.sync
        def _(sp):
            sp.dma_start(t_all[:, :, :], a["x"].rearrange("b s e -> s b e")).then_inc(loaded, 16)
            for half in range(2):
                sp.dma_start(ctxT[half * CD:(half + 1) * CD, :, :], a["ctxT"]).then_inc(loaded, 16)
            sp.dma_start(ctx_all[:, :, :], a["ctx_512"].rearrange("b k c -> k b c")).then_inc(loaded, 16)
            sp.wait_ge(loaded, 64)

        @block.gpsimd
        def _(pool):
            nc.gpsimd.memset(ident[:, :], 0.0).then_inc(zeroed, 1)
            pool.wait_ge(zeroed, 1)
            nc.gpsimd.affine_select(out=ident[:, :], in_=ident[:, :], compare_op=ALU.not_equal, fill=1.0,
                                    base=0, pattern=[[-1, 128]], channel_multiplier=1).then_inc(made, 1)
            pool.wait_ge(made, 1)
            pool.sem_inc(started, 1)
    query_context(nc, a, "L0", sb, sem, banks, t_all, ctxT, ident, None)


def query_context(nc, a, name, sb, sem, banks, t_all, ctxT, ident, out):
    with ExitStack() as ctx:
        def buf(what, shape):
            return sb(f"{name}_{what}", shape, F32, ctx)

        def ev(what):
            return sem(f"{name}_{what}", ctx)

        wq, wk, wv, wo = buf("wq", [E, 128]), buf("wk", [CD, 128]), buf("wv", [CD, 128]), buf("wo", [128, E])
        bq, bk = buf("bq", [128, 1]), buf("bk", [128, 1])
        bv, bo = buf("bv", [SC, 128]), buf("bo", [128, E])
        xT, qT = buf("xT", [E, B, S]), buf("qT", [128, B, S])
        kT, v = buf("kT", [128, B, SC]), buf("v", [SC, B, 128])
        probs, pT = buf("probs", [S, B, SC]), buf("pT", [SC, B, S])
        attT, tb = buf("attT", [128, B, S]), buf("tb", [S, B, E])
        top, bias, total, part = (buf(w, [S, B]) for w in ("top", "bias", "total", "part"))
        bx, bqp, bkp, bvp, bs, bt, ba, bo_p = banks
        w_in = ev("weights_loaded")
        x_done, xT_ready = ev("x_turned"), ev("xT_ready")
        q_done, k_done, v_done = ev("q_done"), ev("k_done"), ev("v_done")
        q_ready, k_ready, v_ready = ev("q_ready"), ev("k_ready"), ev("v_ready")
        s_done, top_done, bias_done = ev("scores_done"), ev("top_done"), ev("bias_done")
        exp_done, part_done, probs_ready = ev("exp_done"), ev("part_done"), ev("probs_ready")
        p_done, pT_ready = ev("probs_turned"), ev("pT_ready")
        att_done, att_ready = ev("attended_done"), ev("attended_ready")
        o_done, tb_ready, t_ready, stored = ev("o_done"), ev("tb_ready"), ev("t_ready"), ev("stored")
        order = pipeline(6, GROUPS)

        with nc.Block() as block:
            @block.sync
            def _(sp):
                for dst, src in ((wq, a[f"{name}_xattn_Wq"]), (wk, a[f"{name}_xattn_Wk"]),
                                 (wv, a[f"{name}_xattn_Wv"]), (wo, a[f"{name}_xattn_Wo"])):
                    sp.dma_start(dst[:, :], src).then_inc(w_in, 16)
                for dst, src in ((bq, a[f"{name}_xattn_bq"]), (bk, a[f"{name}_xattn_bk"])):
                    sp.dma_start(dst[:, :], src.rearrange("(p o) -> p o", o=1)).then_inc(w_in, 16)
                for dst, src, rows in ((bv, a[f"{name}_xattn_bv"], SC), (bo, a[f"{name}_xattn_bo"], 128)):
                    sp.dma_start(dst[:, :], src.rearrange("(o n) -> o n", o=1).to_broadcast([rows, 128])).then_inc(w_in, 16)
                if out is not None:
                    for g in range(GROUPS):
                        sp.wait_ge(t_ready, g + 1)
                        sp.dma_start(out[g * BG:(g + 1) * BG].rearrange("b s e -> s b e"),
                                     t_all[:, g * BG:(g + 1) * BG, :]).then_inc(stored, 16)
                    sp.wait_ge(stored, 16 * GROUPS)

            @block.gpsimd
            def _(pool):
                pool.wait_ge(w_in, 128)
                nc.gpsimd.tensor_tensor(tb[:, :, :], t_all[:, :, :], bo[:, :].unsqueeze(1).to_broadcast([S, B, E]),
                                        ALU.add).then_inc(tb_ready, 1)

            @block.tensor
            def _(pe):
                pe.wait_ge(w_in, 128)
                for step, g in order:
                    bs_ = range(g * BG, (g + 1) * BG)
                    if step == 0:
                        wait(pe, xT_ready, g)
                        for j, b in enumerate(bs_):
                            last = nc.tensor.transpose(bx[:, j * S:(j + 1) * S], t_all[:, b, :], ident[:, :])
                        last.then_inc(x_done, 1)
                    if step == 1:
                        wait(pe, k_ready, g)
                        nc.tensor.matmul(bkp[:, 0:BG * SC], wk[:, :], ctxT[0:CD, g * BG:(g + 1) * BG, :],
                                         start=True, stop=True).then_inc(k_done, 1)
                        wait(pe, v_ready, g)
                        for j, b in enumerate(bs_):
                            last = nc.tensor.matmul(bvp[0:SC, j * 128:(j + 1) * 128], ctxT[0:CD, b, :], wv[:, :],
                                                    start=True, stop=True)
                        last.then_inc(v_done, 1)
                        pe.wait_ge(xT_ready, g + 1)
                        wait(pe, q_ready, g)
                        nc.tensor.matmul(bqp[:, :], wq[:, :], xT[:, g * BG:(g + 1) * BG, :],
                                         start=True, stop=True).then_inc(q_done, 1)
                    if step == 2:
                        pe.wait_ge(q_ready, g + 1)
                        pe.wait_ge(k_ready, g + 1)
                        wait(pe, exp_done, BG * g)
                        for j, b in enumerate(bs_):
                            last = nc.tensor.matmul(bs[:, j * SC:(j + 1) * SC], qT[:, b, :], kT[:, b, :],
                                                    start=True, stop=True)
                        last.then_inc(s_done, 1)
                    if step == 3:
                        pe.wait_ge(probs_ready, g + 1)
                        wait(pe, pT_ready, g)
                        for j, b in enumerate(bs_):
                            last = nc.tensor.transpose(bt[0:SC, j * S:(j + 1) * S], probs[:, b, :], ident[:, :])
                        last.then_inc(p_done, 1)
                    if step == 4:
                        pe.wait_ge(pT_ready, g + 1)
                        pe.wait_ge(v_ready, g + 1)
                        wait(pe, att_ready, g)
                        for j, b in enumerate(bs_):
                            last = nc.tensor.matmul(ba[:, j * S:(j + 1) * S], v[:, b, :], pT[:, b, :],
                                                    start=True, stop=True)
                        last.then_inc(att_done, 1)
                    if step == 5:
                        pe.wait_ge(att_ready, g + 1)
                        wait(pe, t_ready, g)
                        for j, b in enumerate(bs_):
                            last = nc.tensor.matmul(bo_p[:, j * E:(j + 1) * E], attT[:, b, :], wo[:, :],
                                                    start=True, stop=True)
                        last.then_inc(o_done, 1)

            @block.scalar
            def _(act):
                act.wait_ge(w_in, 128)
                for step, g in order:
                    gs = slice(g * BG, (g + 1) * BG)
                    if step == 0:
                        act.wait_ge(x_done, g + 1)
                        nc.scalar.activation(xT[:, gs, :], bx[:, :], ACT.Copy).then_inc(xT_ready, 1)
                    if step == 1:
                        act.wait_ge(q_done, g + 1)
                        nc.scalar.activation(qT[:, gs, :], bqp[:, :], ACT.Identity, bias=bq[:, 0:1]).then_inc(q_ready, 1)
                    if step == 2:
                        act.wait_ge(bias_done, g + 1)
                        for j in range(BG):
                            b = g * BG + j
                            nc.scalar.activation(probs[:, b, :], bs[:, j * SC:(j + 1) * SC], ACT.Exp, bias=bias[:, b:b + 1],
                                                 scale=SCALE1, accum_out=total[:, b:b + 1]).then_inc(exp_done, 1)
                    if step == 4:
                        act.wait_ge(att_done, g + 1)
                        nc.scalar.activation(attT[:, gs, :], ba[:, :], ACT.Copy).then_inc(att_ready, 1)

            @block.vector
            def _(dve):
                dve.wait_ge(w_in, 128)
                for step, g in order:
                    gs = slice(g * BG, (g + 1) * BG)
                    if step == 1:
                        dve.wait_ge(k_done, g + 1)
                        nc.vector.tensor_scalar(kT[:, gs, :], bkp[:, 0:BG * SC].rearrange("p (b k) -> p b k", b=BG),
                                                bk[:, 0:1], None, ALU.add).then_inc(k_ready, 1)
                        dve.wait_ge(v_done, g + 1)
                        nc.vector.tensor_tensor(v[:, gs, :], bvp[0:SC, :].rearrange("p (b k) -> p b k", b=BG),
                                                bv[:, :].unsqueeze(1).to_broadcast([SC, BG, 128]), ALU.add).then_inc(v_ready, 1)
                    if step == 2:
                        dve.wait_ge(s_done, g + 1)
                        nc.vector.tensor_reduce(top[:, gs], bs[:, 0:BG * SC].rearrange("p (b k) -> p b k", b=BG),
                                                AX.X, ALU.max).then_inc(top_done, 1)
                        dve.wait_ge(top_done, g + 1)
                        nc.vector.tensor_scalar(bias[:, gs], top[:, gs], -SCALE1, None, ALU.mult).then_inc(bias_done, 1)
                    if step == 3:
                        dve.wait_ge(exp_done, BG * (g + 1))
                        nc.vector.reciprocal(part[:, gs], total[:, gs]).then_inc(part_done, 1)
                        dve.wait_ge(part_done, g + 1)
                        nc.vector.tensor_tensor(probs[:, gs, :], probs[:, gs, :], bcast(part[:, gs], [S, BG, SC]),
                                                ALU.mult).then_inc(probs_ready, 1)
                        dve.wait_ge(p_done, g + 1)
                        nc.vector.tensor_copy(pT[:, gs, :], bt[0:SC, :].rearrange("p (b k) -> p b k", b=BG)).then_inc(pT_ready, 1)
                    if step == 5:
                        if g == 0:
                            dve.wait_ge(tb_ready, 1)
                        dve.wait_ge(o_done, g + 1)
                        nc.vector.tensor_tensor(t_all[:, gs, :], bo_p[:, :].rearrange("p (b k) -> p b k", b=BG),
                                                tb[:, gs, :], ALU.add).then_inc(t_ready, 1)


def l1(nc, a, sb, sem, banks, t_all, ctxT, ident):
    with ExitStack() as ctx:
        def buf(what, shape):
            return sb(f"L1_{what}", shape, F32, ctx)

        def ev(what):
            return sem(f"L1_{what}", ctx)

        wq, wk, wv = buf("wq", [E, 128]), buf("wk", [CD, 128]), buf("wv", [CD, 128])
        bq, bk, bv = buf("bq", [128, 1]), buf("bk", [128, 1]), buf("bv", [SC, 128])
        gamma, beta = buf("gamma", [128, E]), buf("beta", [128, E])
        xT, qT, kT = buf("xT", [E, B, S]), buf("qT", [128, B, S]), buf("kT", [128, B, SC])
        v, w = buf("v", [SC, B, 128]), buf("w", [SC, B, S])
        x1, z1, z2 = buf("x1", [S, B, E]), buf("z1", [S, B, E]), buf("z2", [S, B, E])
        top, bias, total, part = (buf(k, [SC, B]) for k in ("top", "bias", "total", "part"))
        stats, mv = buf("stats", [S, B, 6]), buf("mv", [S, B, 2])
        ve, rstd, mhalf = buf("ve", [S, B]), buf("rstd", [S, B]), buf("mhalf", [S, BG])
        bx, bqp, bkp, bvp, bs, bp = banks[0:6]
        w_in, x_done, xT_ready = ev("weights_loaded"), ev("x_turned"), ev("xT_ready")
        q_done, k_done, v_done = ev("q_done"), ev("k_done"), ev("v_done")
        q_ready, k_ready, v_ready = ev("q_ready"), ev("k_ready"), ev("v_ready")
        s_done, top_done, bias_done = ev("scores_done"), ev("top_done"), ev("bias_done")
        exp_done, part_done, w_ready = ev("exp_done"), ev("part_done"), ev("w_ready")
        pred_done, x1_ready, stats_done, mv_done = ev("pred_done"), ev("x1_ready"), ev("stats_done"), ev("mv_done")
        const_done, ve_done, rstd_done = ev("const_done"), ev("ve_done"), ev("rstd_done")
        z1_done, z2_done, t_ready = ev("z1_done"), ev("z2_done"), ev("t_ready")
        order = pipeline(5, GROUPS)

        with nc.Block() as block:
            @block.sync
            def _(sp):
                for dst, src in ((wq, a["L1_xattn_Wq"]), (wk, a["L1_xattn_Wk"]), (wv, a["L1_xattn_Wv"])):
                    sp.dma_start(dst[:, :], src).then_inc(w_in, 16)
                for dst, src in ((bq, a["L1_xattn_bq"]), (bk, a["L1_xattn_bk"])):
                    sp.dma_start(dst[:, :], src.rearrange("(p o) -> p o", o=1)).then_inc(w_in, 16)
                for dst, src, rows in ((bv, a["L1_xattn_bv"], SC), (gamma, a["L1_xattn_gamma"], 128),
                                       (beta, a["L1_xattn_beta"], 128)):
                    sp.dma_start(dst[:, :], src.rearrange("(o n) -> o n", o=1).to_broadcast([rows, 128])).then_inc(w_in, 16)

            @block.tensor
            def _(pe):
                pe.wait_ge(w_in, 128)
                for step, g in order:
                    bs_ = range(g * BG, (g + 1) * BG)
                    if step == 0:
                        wait(pe, xT_ready, g)
                        for j, b in enumerate(bs_):
                            last = nc.tensor.transpose(bx[:, j * S:(j + 1) * S], t_all[:, b, :], ident[:, :])
                        last.then_inc(x_done, 1)
                    if step == 1:
                        wait(pe, k_ready, g)
                        nc.tensor.matmul(bkp[:, 0:BG * SC], wk[:, :], ctxT[0:CD, g * BG:(g + 1) * BG, :],
                                         start=True, stop=True).then_inc(k_done, 1)
                        wait(pe, v_ready, g)
                        for j, b in enumerate(bs_):
                            last = nc.tensor.matmul(bvp[0:SC, j * 128:(j + 1) * 128], ctxT[0:CD, b, :], wv[:, :],
                                                    start=True, stop=True)
                        last.then_inc(v_done, 1)
                        pe.wait_ge(xT_ready, g + 1)
                        wait(pe, q_ready, g)
                        nc.tensor.matmul(bqp[:, :], wq[:, :], xT[:, g * BG:(g + 1) * BG, :],
                                         start=True, stop=True).then_inc(q_done, 1)
                    if step == 2:
                        pe.wait_ge(q_ready, g + 1)
                        pe.wait_ge(k_ready, g + 1)
                        wait(pe, exp_done, BG * g)
                        for j, b in enumerate(bs_):
                            last = nc.tensor.matmul(bs[0:SC, j * S:(j + 1) * S], kT[:, b, :], qT[:, b, :],
                                                    start=True, stop=True)
                        last.then_inc(s_done, 1)
                    if step == 3:
                        pe.wait_ge(w_ready, g + 1)
                        pe.wait_ge(v_ready, g + 1)
                        wait(pe, x1_ready, g)
                        for j, b in enumerate(bs_):
                            last = nc.tensor.matmul(bp[:, j * E:(j + 1) * E], w[:, b, :], v[:, b, :],
                                                    start=True, stop=True)
                        last.then_inc(pred_done, 1)

            @block.scalar
            def _(act):
                act.wait_ge(w_in, 128)
                for step, g in order:
                    gs = slice(g * BG, (g + 1) * BG)
                    if step == 0:
                        act.wait_ge(x_done, g + 1)
                        nc.scalar.activation(xT[:, gs, :], bx[:, :], ACT.Copy).then_inc(xT_ready, 1)
                    if step == 1:
                        act.wait_ge(q_done, g + 1)
                        nc.scalar.activation(qT[:, gs, :], bqp[:, :], ACT.Identity, bias=bq[:, 0:1]).then_inc(q_ready, 1)
                    if step == 2:
                        act.wait_ge(bias_done, g + 1)
                        for j in range(BG):
                            b = g * BG + j
                            nc.scalar.activation(w[:, b, :], bs[0:SC, j * S:(j + 1) * S], ACT.Exp, bias=bias[:, b:b + 1],
                                                 scale=SCALE1, accum_out=total[:, b:b + 1]).then_inc(exp_done, 1)

            @block.gpsimd
            def _(pool):
                nc.gpsimd.memset(mhalf[:, :], -0.5).then_inc(const_done, 1)
                pool.wait_ge(w_in, 128)
                pool.wait_ge(const_done, 1)
                for g in range(GROUPS):
                    gs = slice(g * BG, (g + 1) * BG)
                    pool.wait_ge(mv_done, BG * (g + 1))
                    nc.gpsimd.tensor_scalar(ve[:, gs], mv[:, gs, 1], L1_EPS, None, ALU.add).then_inc(ve_done, 1)
                    pool.wait_ge(ve_done, g + 1)
                    nc.gpsimd.tensor_tensor(rstd[:, gs], ve[:, gs], mhalf[:, :], ALU.pow).then_inc(rstd_done, 1)
                    pool.wait_ge(z1_done, BG * (g + 1))
                    nc.gpsimd.tensor_tensor(z2[:, gs, :], z1[:, gs, :], gamma[:, :].unsqueeze(1).to_broadcast([S, BG, E]),
                                            ALU.mult).then_inc(z2_done, 1)
                    pool.wait_ge(z2_done, g + 1)
                    nc.gpsimd.tensor_tensor(t_all[:, gs, :], z2[:, gs, :], beta[:, :].unsqueeze(1).to_broadcast([S, BG, E]),
                                            ALU.add).then_inc(t_ready, 1)

            @block.vector
            def _(dve):
                dve.wait_ge(w_in, 128)
                for step, g in order:
                    gs = slice(g * BG, (g + 1) * BG)
                    if step == 1:
                        dve.wait_ge(k_done, g + 1)
                        nc.vector.tensor_scalar(kT[:, gs, :], bkp[:, 0:BG * SC].rearrange("p (b k) -> p b k", b=BG),
                                                bk[:, 0:1], None, ALU.add).then_inc(k_ready, 1)
                        dve.wait_ge(v_done, g + 1)
                        nc.vector.tensor_tensor(v[:, gs, :], bvp[0:SC, :].rearrange("p (b k) -> p b k", b=BG),
                                                bv[:, :].unsqueeze(1).to_broadcast([SC, BG, 128]), ALU.add).then_inc(v_ready, 1)
                    if step == 2:
                        dve.wait_ge(s_done, g + 1)
                        nc.vector.tensor_reduce(top[:, gs], bs[0:SC, :].rearrange("p (b k) -> p b k", b=BG),
                                                AX.X, ALU.max).then_inc(top_done, 1)
                        dve.wait_ge(top_done, g + 1)
                        nc.vector.tensor_scalar(bias[:, gs], top[:, gs], -SCALE1, None, ALU.mult).then_inc(bias_done, 1)
                        dve.wait_ge(exp_done, BG * (g + 1))
                        nc.vector.reciprocal(part[:, gs], total[:, gs]).then_inc(part_done, 1)
                        dve.wait_ge(part_done, g + 1)
                        nc.vector.tensor_tensor(w[:, gs, :], w[:, gs, :], bcast(part[:, gs], [SC, BG, S]),
                                                ALU.mult).then_inc(w_ready, 1)
                    if step == 3:
                        dve.wait_ge(pred_done, g + 1)
                        nc.vector.tensor_tensor(x1[:, gs, :], bp[:, :].rearrange("p (b k) -> p b k", b=BG),
                                                t_all[:, gs, :], ALU.add).then_inc(x1_ready, 1)
                        dve.wait_ge(x1_ready, g + 1)
                        for b in range(g * BG, (g + 1) * BG):
                            nc.vector.bn_stats(stats[:, b, :], x1[:, b, :]).then_inc(stats_done, 1)
                        for b in range(g * BG, (g + 1) * BG):
                            dve.wait_ge(stats_done, b + 1)
                            nc.vector.bn_aggr(mv[:, b, :], stats[:, b, :]).then_inc(mv_done, 1)
                    if step == 4:
                        dve.wait_ge(rstd_done, g + 1)
                        for b in range(g * BG, (g + 1) * BG):
                            nc.vector.tensor_scalar(z1[:, b, :], x1[:, b, :], mv[:, b, 0:1], rstd[:, b:b + 1],
                                                    ALU.subtract, ALU.mult).then_inc(z1_done, 1)


def decoder(nc, a, sb_, sem_, banks, t_all, ctxT, ctx_all, ident, started, next_phase):
    with ExitStack() as ctx:
        def buf(name, shape, dt=F32):
            return sb_(f"L2_{name}", shape, dt, ctx)

        cq_all = buf("cq_all", [E, L, HD])
        co_all = buf("co_all", [128, L, NP, E])
        combine_cross_weights(nc, a, sb_, sem_, banks, cq_all, co_all)
        next_phase()

        wq, wk, wv = buf("wq", [E, HD]), buf("wk", [E, HD]), buf("wv", [E, HD])
        sa_wo, sa_ob = buf("sa_wo", [128, NP, E]), buf("sa_ob", [128, E])
        cq, co, ca_ob = buf("cq", [E, HD]), buf("co", [128, NP, E]), buf("ca_ob", [128, E])
        w1, b1, w2, b2 = buf("w1", [E, FF]), buf("b1", [128, NF]), buf("w2", [128, NF, E]), buf("b2", [128, E])
        pre_g, pre_b = buf("pre_g", [E, 1]), buf("pre_b", [E, 1])
        norm_g, norm_b = buf("norm_g", [E, 1]), buf("norm_b", [E, 1])
        sa_mask, ca_mask = buf("sa_mask", [S, B, S]), buf("ca_mask", [S, B, SC])
        sa_mask_now, ca_mask_now = buf("sa_mask_now", [S, S]), buf("ca_mask_now", [S, SC])
        ctx_keys, ctx_vals = buf("ctx_keys", [128, 2, SC]), buf("ctx_vals", [SC, CD])
        own_half = buf("own_half", [128, 2])
        qT, kT = buf("qT", [128, NP, S]), buf("kT", [128, NP, 2, S])
        v = buf("v", [S, HD])
        oT, c_oT = buf("oT", [128, NP, S]), buf("c_oT", [128, NP, S])
        cqT = buf("cqT", [128, NP, S])
        masked = [buf(f"masked{i}", [S, GH, S]) for i in range(2)]
        probs = [buf(f"probs{i}", [S, GH, S]) for i in range(2)]
        pT = [buf(f"pT{i}", [S, GH, S]) for i in range(2)]
        c_masked = [buf(f"c_masked{i}", [S, GH, SC]) for i in range(2)]
        c_probs = [buf(f"c_probs{i}", [S, GH, SC]) for i in range(2)]
        c_pT = [buf(f"c_pT{i}", [SC, GH, S]) for i in range(2)]
        least, total, part = buf("least", [S, H]), buf("total", [S, H]), buf("part", [S, H])
        c_least, c_total, c_part = buf("c_least", [S, H]), buf("c_total", [S, H]), buf("c_part", [S, H])
        hid = buf("hid", [128, NF, S])
        mhalf = buf("mhalf", [S, 1])

        def sem(name):
            return sem_(f"L2_{name}", ctx)

        def group_sems(name):
            return [sem(f"{name}{g}") for g in range(NG)]

        class Norm:
            def __init__(self, name):
                self.stats, self.mv = buf(f"{name}_stats", [S, 6]), buf(f"{name}_mv", [S, 2])
                self.ve, self.rstd = buf(f"{name}_ve", [S, 1]), buf(f"{name}_rstd", [S, 1])
                self.z, self.tnT, self.tb = buf(f"{name}_z", [S, E]), buf(f"{name}_tnT", [E, S]), buf(f"{name}_tb", [S, E])
                self.stats_done, self.mv_done = sem(f"{name}_stats_done"), sem(f"{name}_mv_done")
                self.ve_done, self.rstd_done = sem(f"{name}_ve_done"), sem(f"{name}_rstd_done")
                self.z_done, self.turned = sem(f"{name}_z_done"), sem(f"{name}_z_turned")
                self.tnT_ready, self.tb_ready = sem(f"{name}_tnT_ready"), sem(f"{name}_tb_ready")

        sa, ca, ff = Norm("sa"), Norm("ca"), Norm("ff")
        w_qkv, w_so, w_cq, w_co, w_ff = (sem(f"weights_{k}") for k in ("qkv", "so", "cq", "co", "ff"))
        load = [sem(f"load_{k}") for k in ("qkv", "so", "cq", "co", "ff", "const")]
        mask_in, mask_eq, masks_ready = sem("mask_in"), sem("mask_eq"), sem("masks_ready")
        zeros_done, const_done = sem("zeros_done"), sem("const_done")
        sa_mask_set, ca_mask_set, keys_set, vals_set = (sem(k) for k in ("sa_mask_set", "ca_mask_set", "keys_set", "vals_set"))
        sc_done, masked_done, exp_done, part_done, probs_ready, pt_done, pT_ready, pv_done, oT_ready = (
            group_sems(f"sa_{k}") for k in ("scores_done", "masked_done", "exp_done", "part_done", "probs_ready",
                                            "probs_turned", "pT_ready", "pv_done", "oT_ready"))
        csc_done, cmasked_done, cexp_done, cpart_done, cprobs_ready, cpt_done, cpT_ready, cpv_done, coT_ready = (
            group_sems(f"ca_{k}") for k in ("scores_done", "masked_done", "exp_done", "part_done", "probs_ready",
                                            "probs_turned", "pT_ready", "pv_done", "oT_ready"))
        q_done, k_done, v_done, q_ready, v_ready = (
            [sem(f"sa_{k}{i}") for i in range(2)] for k in ("q_done", "k_done", "v_done", "q_ready", "v_ready"))
        k_ready = [[sem(f"sa_k_ready{i}_{half}") for half in range(2)] for i in range(2)]
        cq_done, cq_ready = ([sem(f"ca_{k}{i}") for i in range(2)] for k in ("q_done", "q_ready"))
        o_done, co_done = sem("sa_o_done"), sem("ca_o_done")
        sa_out, ca_out, ff_out = sem("sa_out"), sem("ca_out"), sem("ff_out")
        up_done, hid_ready, down_done = sem("ff_up_done"), sem("ff_hid_ready"), sem("ff_down_done")

        sc_b, csc_b, pt_b, cpt_b, pv_b, cpv_b = banks[0:6]
        pj = banks[6:8]
        bank_users = (
            (("ca_query", (cq_ready[0],), 0),
             ("up", (hid_ready,), -1),
             ("value", (v_ready[0],), 2),
             ("key", (k_ready[0][0], k_ready[0][1]), 2),
             ("sa_project", (sa_out,), 1),
             ("query", (q_ready[0],), 2)),
            (("ca_project", (ca_out,), -1),
             ("ca_query", (cq_ready[1],), 0),
             ("down", (ff_out,), -1),
             ("key", (k_ready[1][0], k_ready[1][1]), 2),
             ("query", (q_ready[1],), 2),
             ("value", (v_ready[1],), 2)),
        )

        def stages(n):
            if not isinstance(n, int):
                return True, True, True, True
            return n + 1 < N, 0 <= n < N, 0 <= n - 1 < N, 0 <= n - 2 < N

        def run(eng, body):
            for n in range(-1, 3):
                body(n)
            with eng.Fori(3, N - 1) as n:
                body(n)
            for n in range(N - 1, N + 2):
                body(n)

        def hold(eng, sem, value):
            if not isinstance(value, int):
                eng.wait_ge(started, 1)
            wait(eng, sem, value)

        def counted(eng, n):
            if isinstance(n, int):
                at = {k: n + k for k in range(-2, 3)}
            else:
                at = {k: eng.alloc_register(f"count{k}") for k in range(-2, 3)}
                for k, register in at.items():
                    eng.reg_mov(register, n + k)
            return (lambda sem, k: wait(eng, sem, at[k])), (lambda sem, k: hold(eng, sem, at[k]))

        with nc.Block() as block:
            @block.sync
            def _(sp):
                l_qkv, l_so, l_cq, l_co, l_ff, l_const = load

                def rows(src, l, n):
                    return src[bass.ds(l, 1), :].to_broadcast([n, 128])

                def cols(src, l):
                    return src[bass.ds(l, 1), :].rearrange("o (c p) -> p (o c)", p=128)

                def load_qkv(l):
                    sp.dma_start(wk[:, :], a["sa_k"][bass.ds(l, 1)].rearrange("o p n -> (o p) n")).then_inc(l_qkv, 16)
                    sp.dma_start(wq[:, :], a["L2_xattn_sa_q"][bass.ds(l, 1)].rearrange("o p n -> (o p) n")).then_inc(l_qkv, 16)
                    sp.dma_start(wv[:, :], a["sa_v"][bass.ds(l, 1)].rearrange("o p n -> (o p) n")).then_inc(l_qkv, 16)

                def load_so(l):
                    sp.dma_start(sa_wo[:, :, :], a["L2_xattn_sa_ow"][bass.ds(l, 1)].rearrange("o (j p) n -> p (o j) n", p=128)).then_inc(l_so, 16)
                    sp.dma_start(sa_ob[:, :], rows(a["L2_xattn_sa_ob"], l, 128)).then_inc(l_so, 16)

                def load_cq(l):
                    sp.dma_start(cq[:, :], cq_all[:, bass.ds(l, 1), :].rearrange("p o n -> p (o n)")).then_inc(l_cq, 16)

                def load_co(l):
                    sp.dma_start(co[:, :, :], co_all[:, bass.ds(l, 1), :, :].rearrange("p o j n -> p (o j) n")).then_inc(l_co, 16)
                    sp.dma_start(ca_ob[:, :], rows(a["L2_xattn_ca_ob"], l, 128)).then_inc(l_co, 16)

                def load_ff(l):
                    sp.dma_start(w1[:, :], a["L2_xattn_ff_w1"][bass.ds(l, 1)].rearrange("o p n -> (o p) n")).then_inc(l_ff, 16)
                    sp.dma_start(w2[:, :, :], a["L2_xattn_ff_w2"][bass.ds(l, 1)].rearrange("o (j p) n -> p (o j) n", p=128)).then_inc(l_ff, 16)
                    sp.dma_start(b2[:, :], rows(a["L2_xattn_ff_b2"], l, 128)).then_inc(l_ff, 16)
                    sp.dma_start(b1[:, :], a["ffb1T"][bass.ds(l, 1)].rearrange("o p c -> (o p) c")).then_inc(l_ff, 16)
                    sp.dma_start(pre_g[:, :], cols(a["L2_xattn_pre_g"], l)).then_inc(l_ff, 16)
                    sp.dma_start(pre_b[:, :], cols(a["L2_xattn_pre_b"], l)).then_inc(l_ff, 16)

                def landed(sem, each, l, ready):
                    hold(sp, sem, (l + 1) * 16 * each)
                    sp.sem_inc(ready, B)

                load_qkv(0)
                for dst, src in ((norm_g, "L2_xattn_norm_g"), (norm_b, "L2_xattn_norm_b")):
                    sp.dma_start(dst[:, :], a[src].rearrange("(p o) -> p o", o=1)).then_inc(l_const, 16)
                sp.dma_start(sa_mask[:, :, :].bitcast(I32), a["mask_BxSxS_ik0"].rearrange("b q k -> q b k")).then_inc(mask_in, 16)
                sp.dma_start(ca_mask[:, :, :].bitcast(I32), a["mask_Bx1xS2_if1"].rearrange("b o k -> o b k").to_broadcast([S, B, SC])).then_inc(mask_in, 16)
                load_so(0)
                load_cq(0)
                load_co(0)
                load_ff(0)
                landed(l_qkv, 3, 0, w_qkv)
                landed(l_so, 2, 0, w_so)
                landed(l_cq, 1, 0, w_cq)
                landed(l_co, 2, 0, w_co)
                landed(l_ff, 6, 0, w_ff)
                with sp.Fori(1, L) as l:
                    hold(sp, v_done[1], l * B)
                    load_qkv(l)
                    landed(l_qkv, 3, l, w_qkv)
                    hold(sp, o_done, l * B)
                    hold(sp, sa.tb_ready, l * B)
                    load_so(l)
                    landed(l_so, 2, l, w_so)
                    hold(sp, cq_done[1], l * B)
                    load_cq(l)
                    landed(l_cq, 1, l, w_cq)
                    hold(sp, co_done, l * B)
                    hold(sp, ca.tb_ready, l * B)
                    load_co(l)
                    landed(l_co, 2, l, w_co)
                    hold(sp, down_done, l * B)
                    hold(sp, ff.tb_ready, l * B)
                    load_ff(l)
                    landed(l_ff, 6, l, w_ff)

            @block.tensor
            def _(pe):
                pe.wait_ge(const_done, 1)

                def body(n):
                    need, held = counted(pe, n)
                    run_qkv, run_sa, run_ca, run_ff = stages(n)
                    qkv_now, sa_now, ca_now, ff_now = 2, 1, 0, -1

                    def bank(i, name):
                        users = bank_users[i]
                        at = [u[0] for u in users].index(name)
                        if isinstance(n, int):
                            for k, (_, copied, offset) in enumerate(users):
                                for s in copied:
                                    wait(pe, s, min(n + offset - (k >= at), N))
                        else:
                            _, copied, offset = users[at - 1]
                            for s in copied:
                                need(s, offset - (at == 0))
                        return pj[i]

                    def turn(st, now, bank, copied):
                        need(st.z_done, now)
                        need(copied, now - 1)
                        nc.tensor.transpose(bank[:, 0:S], st.z[:, :], ident[:, :]).then_inc(st.turned, 1)

                    def project_T(weights, rhs, i, name, done):
                        out = bank(i, name)
                        for j in range(4):
                            c = 4 * i + j
                            last = nc.tensor.matmul(out[:, j * S:(j + 1) * S], weights[:, c * 128:(c + 1) * 128], rhs,
                                                    start=True, stop=True)
                        last.then_inc(done, 1)

                    def query(i):
                        need(sa.tnT_ready, qkv_now)
                        need(w_qkv, qkv_now)
                        project_T(wq, sa.tnT[:, :], i, "query", q_done[i])

                    def key(i):
                        need(sa.tnT_ready, qkv_now)
                        need(w_qkv, qkv_now)
                        project_T(wk, sa.tnT[:, :], i, "key", k_done[i])

                    def value(i):
                        need(sa.tnT_ready, qkv_now)
                        need(w_qkv, qkv_now)
                        nc.tensor.matmul(bank(i, "value")[:, :], sa.tnT[:, :], wv[:, i * 512:(i + 1) * 512],
                                         start=True, stop=True).then_inc(v_done[i], 1)

                    def ca_query(i):
                        need(ca.tnT_ready, ca_now)
                        need(w_cq, ca_now)
                        project_T(cq, ca.tnT[:, :], i, "ca_query", cq_done[i])

                    def sa_scores(g):
                        need(q_ready[g // 2], sa_now)
                        need(k_ready[g // 2][0], sa_now)
                        need(k_ready[g // 2][1], sa_now)
                        need(masked_done[(g - 1) % NG], sa_now if g else sa_now - 1)
                        for j in range(2):
                            p = 2 * g + j
                            last = nc.tensor.matmul(sc_b[:, j * 2 * S:(j + 1) * 2 * S], qT[:, p, :], kT[:, p, :, :],
                                                    start=True, stop=True)
                        last.then_inc(sc_done[g], 1)

                    def ca_scores(g):
                        need(cq_ready[g // 2], ca_now)
                        need(keys_set, ca_now)
                        need(cmasked_done[(g - 1) % NG], ca_now if g else ca_now - 1)
                        for j in range(2):
                            p = 2 * g + j
                            last = nc.tensor.matmul(csc_b[:, j * 2 * SC:(j + 1) * 2 * SC], cqT[:, p, :], ctx_keys[:, :, :],
                                                    start=True, stop=True)
                        last.then_inc(csc_done[g], 1)

                    def sa_values(g):
                        need(probs_ready[g], sa_now)
                        need(pT_ready[(g - 1) % NG], sa_now if g else sa_now - 1)
                        if g == NG - 1 and run_qkv:
                            need(sa.tnT_ready, qkv_now)
                        for j in range(GH):
                            last = nc.tensor.transpose(pt_b[:, j * S:(j + 1) * S], probs[g % 2][:, j, :], ident[:, :])
                        last.then_inc(pt_done[g], 1)

                    def sa_outputs(g):
                        need(pT_ready[g], sa_now)
                        need(v_ready[g // 2], sa_now)
                        need(oT_ready[(g - 1) % NG], sa_now if g else sa_now - 1)
                        for j in range(GH):
                            h, half = g * GH + j, j % 2
                            last = nc.tensor.matmul(pv_b[half * D:(half + 1) * D, (j // 2) * S:(j // 2 + 1) * S],
                                                    v[:, h * D:(h + 1) * D], pT[g % 2][:, j, :], start=True, stop=True)
                        last.then_inc(pv_done[g], 1)

                    def ca_values(g):
                        need(cprobs_ready[g], ca_now)
                        need(cpT_ready[(g - 1) % NG], ca_now if g else ca_now - 1)
                        if g == 0:
                            need(ca.tnT_ready, ca_now)
                        for j in range(GH):
                            last = nc.tensor.transpose(cpt_b[0:SC, j * S:(j + 1) * S], c_probs[g % 2][:, j, :], ident[:, :])
                        last.then_inc(cpt_done[g], 1)

                    def ca_outputs(g):
                        need(cpT_ready[g], ca_now)
                        need(vals_set, ca_now)
                        if g == 0 and run_ff:
                            need(ff.tnT_ready, ff_now)
                        need(coT_ready[(g - 1) % NG], ca_now if g else ca_now - 1)
                        pairs = c_pT[g % 2][:, :, :].rearrange("k (j e) q -> k j e q", e=2)
                        for half in range(2):
                            last = nc.tensor.matmul(cpv_b[half * D:(half + 1) * D, 0:2 * S], ctx_vals[:, :],
                                                    pairs[:, :, half, :], start=True, stop=True)
                        last.then_inc(cpv_done[g], 1)

                    def out_projection(oT, oT_ready, wo, loaded, now, i, name, done):
                        for ready in oT_ready:
                            need(ready, now)
                        need(loaded, now)
                        out = bank(i, name)
                        for p in range(NP):
                            last = nc.tensor.matmul(out[:, 0:E], oT[:, p, :], wo[:, p, :], start=(p == 0), stop=(p == NP - 1))
                        last.then_inc(done, 1)

                    def sa_project():
                        out_projection(oT, oT_ready, sa_wo, w_so, sa_now, 0, "sa_project", o_done)

                    def ca_project():
                        out_projection(c_oT, coT_ready, co, w_co, ff_now, 1, "ca_project", co_done)

                    def feed_up():
                        need(ff.tnT_ready, ff_now)
                        need(w_ff, ff_now)
                        out = bank(0, "up")
                        for c in range(NF):
                            last = nc.tensor.matmul(out[:, c * S:(c + 1) * S], w1[:, c * 128:(c + 1) * 128], ff.tnT[:, :],
                                                    start=True, stop=True)
                        last.then_inc(up_done, 1)

                    def feed_down():
                        need(hid_ready, ff_now)
                        out = bank(1, "down")
                        for c in range(NF):
                            last = nc.tensor.matmul(out[:, 0:E], hid[:, c, :], w2[:, c, :], start=(c == 0), stop=(c == NF - 1))
                        last.then_inc(down_done, 1)

                    if run_sa:
                        sa_scores(0)
                    if run_ca:
                        turn(ca, ca_now, cpt_b, cpT_ready[NG - 1])
                    if run_ff:
                        ca_project()
                    if run_sa:
                        sa_scores(1)
                    if run_ca:
                        ca_query(0)
                        ca_query(1)
                        ca_scores(0)
                    if run_ff:
                        turn(ff, ff_now, cpv_b, coT_ready[NG - 1])
                    if run_sa:
                        sa_scores(2)
                        sa_values(0)
                    if run_ca:
                        ca_scores(1)
                    if run_sa:
                        sa_scores(3)
                        sa_outputs(0)
                        sa_values(1)
                    if run_ff:
                        feed_up()
                    if run_ca:
                        ca_scores(2)
                        ca_values(0)
                    if run_sa:
                        sa_outputs(1)
                        sa_values(2)
                    if run_ff:
                        feed_down()
                    if run_ca:
                        ca_outputs(0)
                    if run_qkv:
                        turn(sa, qkv_now, pt_b, pT_ready[NG - 2])
                    if run_sa:
                        sa_outputs(2)
                    if run_ca:
                        ca_values(1)
                        ca_scores(3)
                    if run_qkv:
                        value(0)
                        key(1)
                    if run_sa:
                        sa_values(3)
                    if run_qkv:
                        key(0)
                    if run_ca:
                        ca_outputs(1)
                        ca_values(2)
                    if run_sa:
                        sa_outputs(3)
                    if run_qkv:
                        query(1)
                    if run_sa:
                        sa_project()
                    if run_ca:
                        ca_outputs(2)
                        ca_values(3)
                    if run_qkv:
                        query(0)
                        value(1)
                    if run_ca:
                        ca_outputs(3)

                run(pe, body)

            def copies_out(need, copy):
                qkv_now, ca_now = 2, 0

                def take_pT(g, now, turned, bank, rows, pT, users, ready):
                    need(turned[g], now)
                    need(users[(g - 2) % NG], now if g >= 2 else now - 1)
                    copy(pT[g % 2][:, :, :], bank[0:rows, :].rearrange("p (j q) -> p j q", j=GH)).then_inc(ready[g], 1)

                def take_oT(g, now, done, bank, oT, projected, ready):
                    need(done[g], now)
                    need(projected, now - 1)
                    copy(oT[:, 2 * g:2 * g + 2, :], bank[:, 0:2 * S].rearrange("p (j q) -> p j q", j=2)).then_inc(ready[g], 1)

                def take_ca_query(i):
                    need(cq_done[i], ca_now)
                    need(csc_done[2 * i + 1], ca_now - 1)
                    copy(cqT[:, 4 * i:4 * i + 4, :], pj[i][:, :].rearrange("p (c q) -> p c q", c=4)).then_inc(cq_ready[i], 1)

                def take_query(i):
                    need(q_done[i], qkv_now)
                    need(sc_done[2 * i + 1], qkv_now - 1)
                    copy(qT[:, 4 * i:4 * i + 4, :], pj[i][:, :].rearrange("p (c q) -> p c q", c=4), -(D ** -0.5)).then_inc(q_ready[i], 1)

                def take_key(i, half):
                    need(k_done[i], qkv_now)
                    need(sc_done[2 * i + 1], qkv_now - 1)
                    rows = slice(half * D, (half + 1) * D)
                    copy(kT[rows, 4 * i:4 * i + 4, half, :], pj[i][rows, :].rearrange("p (c k) -> p c k", c=4)).then_inc(k_ready[i][half], 1)

                def take_value(i):
                    need(v_done[i], qkv_now)
                    need(pv_done[2 * i + 1], qkv_now - 1)
                    copy(v[:, i * 512:(i + 1) * 512], pj[i][:, :]).then_inc(v_ready[i], 1)

                return take_pT, take_oT, take_ca_query, take_query, take_key, take_value

            @block.scalar
            def _(act):
                act.wait_ge(load[5], 32)
                act.wait_ge(const_done, 1)

                def body(n):
                    need, held = counted(act, n)
                    run_qkv, run_sa, run_ca, run_ff = stages(n)
                    qkv_now, sa_now, ca_now, ff_now = 2, 1, 0, -1
                    take_pT, take_oT, take_ca_query, take_query, take_key, take_value = copies_out(
                        need, lambda out, in_, scale=1.0: nc.scalar.activation(out, in_, ACT.Copy, scale=scale))

                    def affine(st, now, bank, gain, offset, user):
                        need(st.turned, now)
                        if st is ff:
                            need(w_ff, now)
                        need(user, now - 1)
                        nc.scalar.activation(st.tnT[:, :], bank[:, 0:S], ACT.Identity, bias=offset[:, 0:1],
                                             scale=gain[:, 0:1]).then_inc(st.tnT_ready, 1)

                    def exps(g, now, masked_done, masked, least, probs, total, turned, done):
                        need(masked_done[g], now)
                        need(turned[(g - 2) % NG], now if g >= 2 else now - 1)
                        for j in range(GH):
                            h = g * GH + j
                            last = nc.scalar.activation(probs[g % 2][:, j, :], masked[g % 2][:, j, :], ACT.Exp,
                                                        bias=least[:, h:h + 1], scale=-1.0, accum_out=total[:, h:h + 1])
                        last.then_inc(done[g], 1)

                    def sa_exps(g):
                        exps(g, sa_now, masked_done, masked, least, probs, total, pt_done, exp_done)

                    def ca_exps(g):
                        exps(g, ca_now, cmasked_done, c_masked, c_least, c_probs, c_total, cpt_done, cexp_done)

                    if run_ca:
                        affine(ca, ca_now, cpt_b, norm_g, norm_b, cq_done[1])
                    if run_sa:
                        sa_exps(0)
                    if run_ca:
                        take_ca_query(0)
                    if run_sa:
                        sa_exps(1)
                    if run_ff:
                        affine(ff, ff_now, cpv_b, pre_g, pre_b, up_done)
                    if run_ca:
                        ca_exps(0)
                    if run_sa:
                        sa_exps(2)
                        take_oT(0, sa_now, pv_done, pv_b, oT, o_done, oT_ready)
                    if run_ca:
                        ca_exps(1)
                        take_pT(0, ca_now, cpt_done, cpt_b, SC, c_pT, cpv_done, cpT_ready)
                    if run_sa:
                        take_oT(1, sa_now, pv_done, pv_b, oT, o_done, oT_ready)
                        sa_exps(3)
                    if run_qkv:
                        affine(sa, qkv_now, pt_b, norm_g, norm_b, v_done[1])
                    if run_ca:
                        ca_exps(2)
                    if run_qkv:
                        take_value(0)
                        take_key(1, 1)
                    if run_sa:
                        take_oT(2, sa_now, pv_done, pv_b, oT, o_done, oT_ready)
                    if run_ca:
                        ca_exps(3)
                    if run_sa:
                        take_oT(3, sa_now, pv_done, pv_b, oT, o_done, oT_ready)
                    if run_ca:
                        take_oT(1, ca_now, cpv_done, cpv_b, c_oT, co_done, coT_ready)
                    if run_qkv:
                        take_query(1)
                    if run_ca:
                        take_pT(3, ca_now, cpt_done, cpt_b, SC, c_pT, cpv_done, cpT_ready)
                        take_oT(3, ca_now, cpv_done, cpv_b, c_oT, co_done, coT_ready)

                run(act, body)

            @block.gpsimd
            def _(pool):
                nc.gpsimd.memset(mhalf[:, :], -0.5).then_inc(zeros_done, 1)
                nc.gpsimd.memset(kT[:, :, :, :], 0.0).then_inc(zeros_done, 1)
                pool.wait_ge(zeros_done, 2)
                pool.sem_inc(const_done, 1)

                def body(n):
                    need, held = counted(pool, n)
                    run_qkv, run_sa, run_ca, run_ff = stages(n)
                    qkv_now, sa_now, ca_now, ff_now = 2, 1, 0, -1

                    def rows_of(batch, what=t_all):
                        return what[:, bass.ds(batch, 1), :].rearrange("p o e -> p (o e)")

                    def rstd(st, now):
                        held(st.mv_done, now)
                        nc.gpsimd.tensor_scalar(st.ve[:, :], st.mv[:, 1:2], LN_EPS, None, ALU.add).then_inc(st.ve_done, 1)
                        held(st.ve_done, now)
                        nc.gpsimd.tensor_tensor(st.rstd[:, :], st.ve[:, :], mhalf[:, :], ALU.pow).then_inc(st.rstd_done, 1)

                    def plus_bias(st, now, batch, bias, loaded, used):
                        held(loaded, now)
                        held(used, now - 1)
                        nc.gpsimd.tensor_tensor(st.tb[:, :], rows_of(batch), bias[:, :], ALU.add).then_inc(st.tb_ready, 1)

                    def normalise(g, now, parts, probs, part, ready, w):
                        held(parts[g], now)
                        nc.gpsimd.tensor_tensor(probs[g % 2][:, :, :], probs[g % 2][:, :, :],
                                                bcast(part[:, g * GH:(g + 1) * GH], [S, GH, w]), ALU.mult).then_inc(ready[g], 1)

                    def sa_norm(g):
                        normalise(g, sa_now, part_done, probs, part, probs_ready, S)

                    def ca_norm(g):
                        normalise(g, ca_now, cpart_done, c_probs, c_part, cprobs_ready, SC)

                    def set_keys():
                        held(csc_done[NG - 1], ca_now - 1)
                        nc.gpsimd.tensor_tensor(ctx_keys[:, :, :], ctxT[:, bass.ds((n - 1) % B, 1), :].to_broadcast([128, 2, SC]),
                                                bcast(own_half[:, :], [128, 2, SC]), ALU.mult).then_inc(keys_set, 1)

                    def set_ca_mask():
                        held(cmasked_done[NG - 1], ca_now - 1)
                        nc.gpsimd.tensor_copy(ca_mask_now[:, :], rows_of((n - 1) % B, ca_mask)).then_inc(ca_mask_set, 1)

                    def set_vals():
                        held(cpv_done[NG - 1], ca_now - 1)
                        nc.gpsimd.tensor_copy(ctx_vals[:, :], rows_of((n - 1) % B, ctx_all)).then_inc(vals_set, 1)

                    def set_sa_mask():
                        held(masked_done[NG - 1], qkv_now - 1)
                        nc.gpsimd.tensor_copy(sa_mask_now[:, :], rows_of((n + 1) % B, sa_mask)).then_inc(sa_mask_set, 1)

                    if run_qkv:
                        rstd(sa, qkv_now)
                    if run_ca:
                        set_vals()
                        set_keys()
                        set_ca_mask()
                    if run_ff:
                        rstd(ff, ff_now)
                        plus_bias(ff, ff_now, (n - 2) % B, b2, w_ff, ff_out)
                    if run_sa:
                        sa_norm(0)
                        sa_norm(1)
                    if run_ca:
                        ca_norm(0)
                    if run_sa:
                        sa_norm(2)
                    if run_ca:
                        ca_norm(1)
                    if run_sa:
                        sa_norm(3)
                    if run_ca:
                        ca_norm(2)
                        plus_bias(ca, ca_now, (n - 1) % B, ca_ob, w_co, ca_out)
                    if run_qkv:
                        set_sa_mask()
                    if run_ca:
                        ca_norm(3)
                    if run_sa:
                        plus_bias(sa, sa_now, n % B, sa_ob, w_so, sa_out)
                        rstd(ca, sa_now)

                pool.wait_ge(masks_ready, 5)
                run(pool, body)

            @block.vector
            def _(dve):
                nc.vector.memset(own_half[:, :], 0.0).then_inc(masks_ready, 1)
                dve.wait_ge(masks_ready, 1)
                for half in range(2):
                    nc.vector.memset(own_half[half * D:(half + 1) * D, half:half + 1], 1.0).then_inc(masks_ready, 1)
                dve.wait_ge(mask_in, 32)
                for m in (sa_mask, ca_mask):
                    nc.vector.tensor_scalar(m[:, :, :], m[:, :, :].bitcast(I32), 0.0, MASKED, ALU.is_equal, ALU.mult).then_inc(masks_ready, 1)
                dve.wait_ge(const_done, 1)

                def body(n):
                    need, held = counted(dve, n)
                    run_qkv, run_sa, run_ca, run_ff = stages(n)
                    qkv_now, sa_now, ca_now, ff_now = 2, 1, 0, -1

                    def copy(out, in_, scale=1.0):
                        if scale == 1.0:
                            return nc.vector.tensor_copy(out, in_)
                        return nc.vector.tensor_scalar(out, in_, scale, None, ALU.mult)

                    take_pT, take_oT, take_ca_query, take_query, take_key, take_value = copies_out(need, copy)

                    def rows_of(batch):
                        return t_all[:, bass.ds(batch, 1), :].rearrange("p o e -> p (o e)")

                    def stats(st, now, batch, written):
                        if written is not None:
                            held(written, now)
                        nc.vector.bn_stats(st.stats[:, :], rows_of(batch)).then_inc(st.stats_done, 1)
                        held(st.stats_done, now)
                        held(st.ve_done, now - 1)
                        nc.vector.bn_aggr(st.mv[:, :], st.stats[:, :]).then_inc(st.mv_done, 1)

                    def centre(st, now, batch):
                        held(st.rstd_done, now)
                        held(st.turned, now - 1)
                        nc.vector.tensor_scalar(st.z[:, :], rows_of(batch), st.mv[:, 0:1], st.rstd[:, 0:1],
                                                ALU.subtract, ALU.mult).then_inc(st.z_done, 1)

                    def mask(g, now, done, bank, mask, mask_set, masked, least, exps, ready, w):
                        held(done[g], now)
                        held(mask_set, now)
                        held(exps[(g - 2) % NG], now if g >= 2 else now - 1)
                        for j in range(GH):
                            h = g * GH + j
                            last = nc.vector.tensor_tensor_reduce(out=masked[g % 2][:, j, :], in0=bank[:, j * w:(j + 1) * w], in1=mask[:, :],
                                                                  scale=1.0, scalar=3e38, op0=ALU.add, op1=ALU.min,
                                                                  accum_out=least[:, h:h + 1])
                        last.then_inc(ready[g], 1)

                    def sa_mask_(g):
                        mask(g, sa_now, sc_done, sc_b, sa_mask_now, sa_mask_set, masked, least, exp_done, masked_done, S)

                    def ca_mask_(g):
                        mask(g, ca_now, csc_done, csc_b, ca_mask_now, ca_mask_set, c_masked, c_least, cexp_done, cmasked_done, SC)

                    def over(g, now, exps, total, part, done):
                        need(exps[g], now)
                        nc.vector.reciprocal(part[:, g * GH:(g + 1) * GH], total[:, g * GH:(g + 1) * GH]).then_inc(done[g], 1)

                    def sa_over(g):
                        over(g, sa_now, exp_done, total, part, part_done)

                    def ca_over(g):
                        over(g, ca_now, cexp_done, c_total, c_part, cpart_done)

                    def relu_up():
                        need(up_done, ff_now)
                        need(down_done, ff_now - 1)
                        for c in range(NF):
                            last = nc.vector.tensor_scalar(hid[:, c, :], pj[0][:, c * S:(c + 1) * S], b1[:, c:c + 1], 0.0,
                                                           ALU.add, ALU.max)
                        last.then_inc(hid_ready, 1)

                    def add_out(st, now, batch, done, bank, out):
                        held(st.tb_ready, now)
                        held(done, now)
                        nc.vector.tensor_tensor(rows_of(batch), bank[:, 0:E], st.tb[:, :], ALU.add).then_inc(out, 1)

                    if run_qkv:
                        stats(sa, qkv_now, (n + 1) % B, None)
                    if run_sa:
                        sa_mask_(0)
                    if run_ff:
                        add_out(ca, ff_now, (n - 2) % B, co_done, pj[1], ca_out)
                        stats(ff, ff_now, (n - 2) % B, ca_out)
                    if run_sa:
                        sa_over(0)
                        sa_mask_(1)
                    if run_ff:
                        centre(ff, ff_now, (n - 2) % B)
                    if run_ca:
                        take_ca_query(1)
                        ca_mask_(0)
                    if run_sa:
                        sa_over(1)
                        sa_mask_(2)
                        take_pT(0, sa_now, pt_done, pt_b, S, pT, pv_done, pT_ready)
                    if run_ca:
                        ca_mask_(1)
                        ca_over(0)
                    if run_sa:
                        sa_mask_(3)
                        sa_over(2)
                        take_pT(1, sa_now, pt_done, pt_b, S, pT, pv_done, pT_ready)
                    if run_ff:
                        relu_up()
                    if run_qkv:
                        centre(sa, qkv_now, (n + 1) % B)
                    if run_ca:
                        ca_over(1)
                    if run_sa:
                        take_pT(2, sa_now, pt_done, pt_b, S, pT, pv_done, pT_ready)
                    if run_ca:
                        ca_mask_(2)
                        take_oT(0, ca_now, cpv_done, cpv_b, c_oT, co_done, coT_ready)
                    if run_ff:
                        add_out(ff, ff_now, (n - 2) % B, down_done, pj[1], ff_out)
                    if run_sa:
                        sa_over(3)
                    if run_ca:
                        take_pT(1, ca_now, cpt_done, cpt_b, SC, c_pT, cpv_done, cpT_ready)
                        ca_over(2)
                        ca_mask_(3)
                    if run_qkv:
                        take_key(1, 0)
                    if run_sa:
                        take_pT(3, sa_now, pt_done, pt_b, S, pT, pv_done, pT_ready)
                    if run_qkv:
                        take_key(0, 1)
                        take_key(0, 0)
                    if run_ca:
                        ca_over(3)
                        take_pT(2, ca_now, cpt_done, cpt_b, SC, c_pT, cpv_done, cpT_ready)
                    if run_sa:
                        add_out(sa, sa_now, n % B, o_done, pj[0], sa_out)
                        stats(ca, sa_now, n % B, sa_out)
                    if run_ca:
                        take_oT(2, ca_now, cpv_done, cpv_b, c_oT, co_done, coT_ready)
                    if run_qkv:
                        take_query(0)
                    if run_sa:
                        centre(ca, sa_now, n % B)
                    if run_qkv:
                        take_value(1)

                run(dve, body)


def combine_cross_weights(nc, a, sb, sem, banks, cq_all, co_all):
    with ExitStack() as ctx:
        def buf(what, shape):
            return sb(f"comb_{what}", shape, F32, ctx)

        qw, ow = ([buf(f"{k}{i}", [128, NP, 128]) for i in range(2)] for k in ("q", "o"))
        kw, vw = ([buf(f"{k}{i}", [128, NP, 2, CD]) for i in range(2)] for k in ("k", "v"))
        w_in = [sem(f"comb_loaded{i}", ctx) for i in range(2)]
        zeroed = sem("comb_zeroed", ctx)
        g_done, n_done, g_ready, n_ready = (
            [sem(f"comb_{k}{i}", ctx) for i in range(2)] for k in ("g_done", "n_done", "g_ready", "n_ready"))
        with nc.Block() as block:
            @block.sync
            def _(sp):
                sp.wait_ge(zeroed, 4)
                for l in range(L):
                    i = l % 2
                    if l >= 2:
                        sp.wait_ge(n_done[1], l - 1)
                    sp.dma_start(qw[i][:, :, :], a["caqT"][l].rearrange("(j p) n -> p j n", p=128)).then_inc(w_in[i], 16)
                    sp.dma_start(ow[i][:, :, :], a["L2_xattn_ca_ow"][l].rearrange("(j p) n -> p j n", p=128)).then_inc(w_in[i], 16)
                    for w, src in ((kw, a["cakT"]), (vw, a["cavT"])):
                        for half in range(2):
                            sp.dma_start(w[i][half * D:(half + 1) * D, :, half, :],
                                         src[l].rearrange("(j e p) n -> e p j n", e=2, p=D)[half]).then_inc(w_in[i], 16)

            @block.gpsimd
            def _(pool):
                for w in (*kw, *vw):
                    nc.gpsimd.memset(w[:, :, :, :], 0.0).then_inc(zeroed, 1)

            @block.tensor
            def _(pe):
                for l in range(L):
                    i = l % 2
                    pe.wait_ge(w_in[i], 96 * (l // 2 + 1))
                    for c in range(2):
                        wait(pe, g_ready[c], l)
                        for j in range(4):
                            p = 4 * c + j
                            last = nc.tensor.matmul(banks[c][:, j * 128:(j + 1) * 128], qw[i][:, p, :], kw[i][:, p, :, :],
                                                    start=True, stop=True)
                        last.then_inc(g_done[c], 1)
                    for c in range(2):
                        wait(pe, n_ready[c], l)
                        for j in range(4):
                            p = 4 * c + j
                            last = nc.tensor.matmul(banks[2 + c][:, j * 128:(j + 1) * 128], vw[i][:, p, :, :], ow[i][:, p, :],
                                                    start=True, stop=True)
                        last.then_inc(n_done[c], 1)

            @block.scalar
            def _(act):
                for l in range(L):
                    for c in range(2):
                        act.wait_ge(g_done[c], l + 1)
                        nc.scalar.activation(cq_all[:, l, c * 512:(c + 1) * 512], banks[c][:, :], ACT.Copy,
                                             scale=-(D ** -0.5)).then_inc(g_ready[c], 1)

            @block.vector
            def _(dve):
                for l in range(L):
                    for c in range(2):
                        dve.wait_ge(n_done[c], l + 1)
                        nc.vector.tensor_copy(co_all[:, l, 4 * c:4 * c + 4, :],
                                              banks[2 + c][:, :].rearrange("p (j n) -> p j n", j=4)).then_inc(n_ready[c], 1)


_AS_THEY_ARE = [f"{m}_xattn_{k}" for m in ("L0", "L3") for k in ("Wq", "bq", "Wk", "bk", "Wv", "bv", "Wo", "bo")] + \
    [f"L1_xattn_{k}" for k in ("Wq", "bq", "Wk", "bk", "Wv", "bv", "gamma", "beta")] + \
    [f"L2_xattn_{k}" for k in ("norm_g", "norm_b", "sa_q", "sa_ow", "sa_ob", "ca_ow", "ca_ob", "ff_w1",
                               "ff_w2", "ff_b2", "pre_g", "pre_b")] + \
    ["x", "ctx_512", "mask_BxSxS_ik0", "mask_Bx1xS2_if1"]


def kernel(**inputs):
    import numpy as np
    import concourse.bacc as bacc
    from concourse.bass_utils import run_bass_kernel_spmd

    laid = {k: inputs[k] for k in _AS_THEY_ARE}
    kv, ckv = np.asarray(inputs["L2_xattn_sa_kv"]), np.asarray(inputs["L2_xattn_ca_kv"])
    laid["sa_k"], laid["sa_v"] = kv[:, :, :HD], kv[:, :, HD:]
    laid["cakT"], laid["cavT"] = ckv[:, :, :HD].transpose(0, 2, 1), ckv[:, :, HD:].transpose(0, 2, 1)
    laid["caqT"] = np.asarray(inputs["L2_xattn_ca_q"]).transpose(0, 2, 1)
    laid["ffb1T"] = np.asarray(inputs["L2_xattn_ff_b1"]).reshape(L, NF, 128).transpose(0, 2, 1)
    laid["ctxT"] = np.asarray(inputs["ctx_512"]).transpose(2, 0, 1)

    nc = bacc.Bacc("TRN2", target_bir_lowering=False, num_devices=1)
    arrays, args = {}, {}
    for name, value in laid.items():
        value = np.ascontiguousarray(value)
        arrays[f"in_{name}"] = value
        args[name] = nc.dram_tensor(f"in_{name}", value.shape, mybir.dt.from_np(value.dtype), kind="ExternalInput").ap()
    args["out"] = nc.dram_tensor("out_t", (B, S, E), F32, kind="ExternalOutput").ap()
    build(nc, args)
    r = run_bass_kernel_spmd(nc, [arrays], core_ids=[0])
    return r.results[0]["out_t"]
```

```python
from contextlib import ExitStack

import concourse.bass as bass
from concourse import mybir

F32 = mybir.dt.float32
F32R = mybir.dt.float32r
I32 = mybir.dt.int32
ALU = mybir.AluOpType
ACT = mybir.ActivationFunctionType
AX = mybir.AxisListType

B, S, E = 16, 128, 128
SC, CD = 120, 64
L, H, D = 6, 16, 64
HD = H * D
FF = 512
NP = H // 2
NG = 4
GH = H // NG
NF = FF // 128
N = L * B
BG = 4
GROUPS = B // BG
MASKED = 1e30
LN_EPS, L1_EPS = 1e-5, 1e-6
SCALE1 = 128 ** -0.5


def wait(eng, sem, value):
    if isinstance(value, int) and value <= 0:
        return
    eng.wait_ge(sem, value)


def bcast(ap, shape):
    return ap.unsqueeze(2).to_broadcast(shape)


def build(nc, a):
    with ExitStack() as ctx:
        def sb(name, shape, dt=F32, scope=ctx):
            return scope.enter_context(nc.sbuf_tensor(name, shape, dt))

        phase_sems = []

        def sem(name, scope=ctx):
            if scope is ctx:
                return ctx.enter_context(nc.semaphore(name))
            phase_sems.append(nc.alloc_semaphore(name=name))
            return phase_sems[-1]

        def next_phase():
            nc.clear_and_free_semaphores(phase_sems)
            phase_sems.clear()
            nc.all_engine_barrier()

        banks = [ctx.enter_context(nc.psum_tensor(f"bank{i}", [128, 512], F32)) for i in range(8)]

        t_all = sb("t_all", [128, B, E])
        ctxT = sb("ctxT", [128, B, SC])
        ctx_all = sb("ctx_all", [SC, B, CD])
        ident = sb("ident", [128, 128])
        started = sem("started")
        ahead = Ahead(sb)

        front(nc, a, sb, sem, banks, t_all, ctxT, ctx_all, ident, started, ahead)
        next_phase()
        l3_weights = ContextWeights(sb, "L3")
        decoder(nc, a, sb, sem, banks, t_all, ctxT, ctx_all, ident, started, ahead, l3_weights)
        next_phase()
        l3(nc, a, sb, sem, banks, t_all, ctxT, ident, l3_weights)


class Ahead:
    def __init__(self, sb):
        self.wq, self.wk, self.wv = sb("L2_wq", [E, HD]), sb("L2_wk", [E, HD]), sb("L2_wv", [E, HD])
        self.ctxT_low = sb("L2_ctxT_low", [128, B, SC])
        self.norm_g, self.norm_b = sb("L2_norm_g", [E, 1]), sb("L2_norm_b", [E, 1])
        self.sa_mask, self.ca_mask = sb("L2_sa_mask", [S, B, S]), sb("L2_ca_mask", [S, B, SC])
        self.cq_all = sb("L2_cq_all", [E, L, HD])
        self.co_all = sb("L2_co_all", [128, L, NP, E])


class ContextWeights:
    COUNT = 16 * 8

    def __init__(self, sb, name):
        self.name = name
        self.wq, self.wk, self.wv, self.wo = (sb(f"{name}_{k}", shape) for k, shape in (
            ("wq", [E, 128]), ("wk", [CD, 128]), ("wv", [CD, 128]), ("wo", [128, E])))
        self.bq, self.bk, self.bv, self.bo = (sb(f"{name}_{k}", shape) for k, shape in (
            ("bq", [128, 1]), ("bk", [128, 1]), ("bv", [SC, 128]), ("bo", [128, E])))

    def load(self, eng, a, loaded):
        src = {k: a[f"{self.name}_xattn_{k}"] for k in ("Wq", "Wk", "Wv", "Wo", "bq", "bk", "bv", "bo")}
        for dst, w in ((self.wk, "Wk"), (self.wq, "Wq"), (self.wv, "Wv"), (self.wo, "Wo")):
            eng.dma_start(dst[:, :], src[w]).then_inc(loaded, 16)
        for dst, w in ((self.bk, "bk"), (self.bq, "bq")):
            eng.dma_start(dst[:, :], src[w].rearrange("(p o) -> p o", o=1)).then_inc(loaded, 16)
        for dst, w, rows in ((self.bv, "bv", SC), (self.bo, "bo", 128)):
            eng.dma_start(dst[:, :], src[w].rearrange("(o n) -> o n", o=1).to_broadcast([rows, 128])).then_inc(loaded, 16)


class Work:
    def __init__(self, sb, name, scope):
        def buf(what):
            return sb(f"{name}_{what}", [128, B, 128], F32, scope)

        self.xT, self.qT, self.kT, self.v, self.probs = (buf(k) for k in ("xT", "qT", "kT", "v", "probs"))
        self.pT, self.attT, self.tb = buf("pT_x1"), buf("attT_z1"), buf("tb_z2")
        self.x1, self.z1, self.z2 = self.pT, self.attT, self.tb


class QueryContext:
    STAGES = 6

    def __init__(self, nc, sb, sem, name, scope, banks, w, work, bg, t_all, ctxT, ident):
        self.nc, self.w, self.k, self.bg, self.t_all, self.ctxT, self.ident = nc, w, work, bg, t_all, ctxT, ident
        self.bank_x, self.bank_q, self.bank_k, self.bank_v, self.bank_s, self.bank_p, self.bank_a, self.bank_o = banks
        self.top, self.bias, self.total, self.part = (
            sb(f"{name}_{k}", [S, B], F32, scope) for k in ("top", "bias", "total", "part"))
        (self.x_done, self.xT_ready, self.q_done, self.k_done, self.v_done, self.q_ready, self.k_ready, self.v_ready,
         self.s_done, self.top_done, self.bias_done, self.exp_done, self.part_done, self.probs_ready, self.p_done,
         self.pT_ready, self.att_done, self.att_ready, self.o_done, self.tb_ready, self.t_ready) = (
            sem(f"{name}_{k}", scope) for k in (
                "x_turned", "xT_ready", "q_done", "k_done", "v_done", "q_ready", "k_ready", "v_ready",
                "scores_done", "top_done", "bias_done", "exp_done", "part_done", "probs_ready", "probs_turned",
                "pT_ready", "attended_done", "attended_ready", "o_done", "tb_ready", "t_ready"))

    def tensor(self, pe, stage, g):
        nc, w, k, bg, ctxT = self.nc, self.w, self.k, self.bg, self.ctxT
        batches = list(enumerate(range(g * bg, (g + 1) * bg)))
        if stage == 0:
            wait(pe, self.xT_ready, g)
            for j, b in batches:
                last = nc.tensor.transpose(self.bank_x[:, j * S:(j + 1) * S], self.t_all[:, b, :], self.ident[:, :])
            last.then_inc(self.x_done, 1)
        if stage == 1:
            wait(pe, self.k_ready, g)
            nc.tensor.matmul(self.bank_k[:, 0:bg * SC], w.wk[:, :], ctxT[0:CD, g * bg:(g + 1) * bg, :],
                             start=True, stop=True).then_inc(self.k_done, 1)
            wait(pe, self.v_ready, g)
            for j, b in batches:
                last = nc.tensor.matmul(self.bank_v[0:SC, j * 128:(j + 1) * 128], ctxT[0:CD, b, :], w.wv[:, :],
                                        start=True, stop=True)
            last.then_inc(self.v_done, 1)
            pe.wait_ge(self.xT_ready, g + 1)
            wait(pe, self.q_ready, g)
            nc.tensor.matmul(self.bank_q[:, 0:bg * S], w.wq[:, :], k.xT[:, g * bg:(g + 1) * bg, :],
                             start=True, stop=True).then_inc(self.q_done, 1)
        if stage == 2:
            pe.wait_ge(self.q_ready, g + 1)
            pe.wait_ge(self.k_ready, g + 1)
            wait(pe, self.exp_done, bg * g)
            for j, b in batches:
                last = nc.tensor.matmul(self.bank_s[:, j * SC:(j + 1) * SC], k.qT[:, b, :], k.kT[:, b, 0:SC],
                                        start=True, stop=True)
            last.then_inc(self.s_done, 1)
        if stage == 3:
            pe.wait_ge(self.probs_ready, g + 1)
            wait(pe, self.pT_ready, g)
            for j, b in batches:
                last = nc.tensor.transpose(self.bank_p[0:SC, j * S:(j + 1) * S], k.probs[:, b, 0:SC], self.ident[:, :])
            last.then_inc(self.p_done, 1)
        if stage == 4:
            pe.wait_ge(self.pT_ready, g + 1)
            pe.wait_ge(self.v_ready, g + 1)
            wait(pe, self.att_ready, g)
            for j, b in batches:
                last = nc.tensor.matmul(self.bank_a[:, j * S:(j + 1) * S], k.v[0:SC, b, :], k.pT[0:SC, b, :],
                                        start=True, stop=True)
            last.then_inc(self.att_done, 1)
        if stage == 5:
            pe.wait_ge(self.att_ready, g + 1)
            wait(pe, self.t_ready, g)
            for j, b in batches:
                last = nc.tensor.matmul(self.bank_o[:, j * E:(j + 1) * E], k.attT[:, b, :], w.wo[:, :],
                                        start=True, stop=True)
            last.then_inc(self.o_done, 1)

    def scalar(self, act, stage, g):
        nc, k, bg = self.nc, self.k, self.bg
        gs = slice(g * bg, (g + 1) * bg)
        if stage == 0:
            act.wait_ge(self.x_done, g + 1)
            nc.scalar.activation(k.xT[:, gs, :], self.bank_x[:, 0:bg * S], ACT.Copy).then_inc(self.xT_ready, 1)
        if stage == 1:
            act.wait_ge(self.q_done, g + 1)
            nc.scalar.activation(k.qT[:, gs, :], self.bank_q[:, 0:bg * S], ACT.Identity, bias=self.w.bq[:, 0:1]).then_inc(self.q_ready, 1)
        if stage == 2:
            act.wait_ge(self.bias_done, g + 1)
            for j in range(bg):
                b = g * bg + j
                nc.scalar.activation(k.probs[:, b, 0:SC], self.bank_s[:, j * SC:(j + 1) * SC], ACT.Exp, bias=self.bias[:, b:b + 1],
                                     scale=SCALE1, accum_out=self.total[:, b:b + 1]).then_inc(self.exp_done, 1)
        if stage == 4:
            act.wait_ge(self.att_done, g + 1)
            nc.scalar.activation(k.attT[:, gs, :], self.bank_a[:, 0:bg * S], ACT.Copy).then_inc(self.att_ready, 1)

    def vector(self, dve, stage, g):
        nc, k, w, bg = self.nc, self.k, self.w, self.bg
        gs = slice(g * bg, (g + 1) * bg)
        if stage == 1:
            dve.wait_ge(self.k_done, g + 1)
            nc.vector.tensor_scalar(k.kT[:, gs, 0:SC], self.bank_k[:, 0:bg * SC].rearrange("p (b k) -> p b k", b=bg),
                                    w.bk[:, 0:1], None, ALU.add).then_inc(self.k_ready, 1)
            dve.wait_ge(self.v_done, g + 1)
            nc.vector.tensor_tensor(k.v[0:SC, gs, :], self.bank_v[0:SC, 0:bg * 128].rearrange("p (b k) -> p b k", b=bg),
                                    w.bv[:, :].unsqueeze(1).to_broadcast([SC, bg, 128]), ALU.add).then_inc(self.v_ready, 1)
        if stage == 2:
            dve.wait_ge(self.s_done, g + 1)
            nc.vector.tensor_reduce(self.top[:, gs], self.bank_s[:, 0:bg * SC].rearrange("p (b k) -> p b k", b=bg),
                                    AX.X, ALU.max).then_inc(self.top_done, 1)
            dve.wait_ge(self.top_done, g + 1)
            nc.vector.tensor_scalar(self.bias[:, gs], self.top[:, gs], -SCALE1, None, ALU.mult).then_inc(self.bias_done, 1)
        if stage == 3:
            dve.wait_ge(self.p_done, g + 1)
            nc.vector.tensor_copy(k.pT[0:SC, gs, :], self.bank_p[0:SC, 0:bg * S].rearrange("p (b k) -> p b k", b=bg)).then_inc(self.pT_ready, 1)
        if stage == 5:
            dve.wait_ge(self.tb_ready, g + 1)
            dve.wait_ge(self.o_done, g + 1)
            nc.vector.tensor_tensor(self.t_all[:, gs, :], self.bank_o[:, 0:bg * E].rearrange("p (b k) -> p b k", b=bg),
                                    k.tb[:, gs, :], ALU.add).then_inc(self.t_ready, 1)

    def normalise(self, dve, g):
        nc, k, bg = self.nc, self.k, self.bg
        gs = slice(g * bg, (g + 1) * bg)
        dve.wait_ge(self.exp_done, bg * (g + 1))
        nc.vector.reciprocal(self.part[:, gs], self.total[:, gs]).then_inc(self.part_done, 1)
        dve.wait_ge(self.part_done, g + 1)
        nc.vector.tensor_tensor(k.probs[:, gs, 0:SC], k.probs[:, gs, 0:SC], bcast(self.part[:, gs], [S, bg, SC]),
                                ALU.mult).then_inc(self.probs_ready, 1)

    def gpsimd(self, pool, g):
        nc, bg = self.nc, self.bg
        gs = slice(g * bg, (g + 1) * bg)
        nc.gpsimd.tensor_tensor(self.k.tb[:, gs, :], self.t_all[:, gs, :], self.w.bo[:, :].unsqueeze(1).to_broadcast([S, bg, E]),
                                ALU.add).then_inc(self.tb_ready, 1)


class TokenSoftmax:
    STAGES = 5
    COUNT = 16 * 8

    def __init__(self, nc, sb, sem, scope, banks, work, t_all, ctxT, ident):
        self.nc, self.k, self.t_all, self.ctxT, self.ident = nc, work, t_all, ctxT, ident
        self.bank_x, self.bank_q, self.bank_k, self.bank_v, self.bank_s, self.bank_p = banks

        def buf(what, shape):
            return sb(f"L1_{what}", shape, F32, scope)

        self.wq, self.wk, self.wv = buf("wq", [E, 128]), buf("wk", [CD, 128]), buf("wv", [CD, 128])
        self.bq, self.bk, self.bv = buf("bq", [128, 1]), buf("bk", [128, 1]), buf("bv", [SC, 128])
        self.gamma, self.beta = buf("gamma", [128, E]), buf("beta", [128, E])
        self.top, self.bias, self.total, self.part = (buf(k, [SC, B]) for k in ("top", "bias", "total", "part"))
        self.stats, self.mv = buf("stats", [S, B, 6]), buf("mv", [S, B, 2])
        self.ve, self.rstd, self.mhalf = buf("ve", [S, B]), buf("rstd", [S, B]), buf("mhalf", [S, BG])
        (self.x_done, self.xT_ready, self.q_done, self.k_done, self.v_done, self.q_ready, self.k_ready, self.v_ready,
         self.s_done, self.top_done, self.bias_done, self.exp_done, self.part_done, self.w_ready, self.pred_done,
         self.x1_ready, self.stats_done, self.mv_done, self.const_done, self.ve_done, self.rstd_done, self.z1_done,
         self.z2_done, self.t_ready) = (
            sem(f"L1_{k}", scope) for k in (
                "x_turned", "xT_ready", "q_done", "k_done", "v_done", "q_ready", "k_ready", "v_ready",
                "scores_done", "top_done", "bias_done", "exp_done", "part_done", "w_ready", "pred_done",
                "x1_ready", "stats_done", "mv_done", "const_done", "ve_done", "rstd_done", "z1_done",
                "z2_done", "t_ready"))

    def load(self, eng, a, loaded):
        for dst, w in ((self.wq, "Wq"), (self.wk, "Wk"), (self.wv, "Wv")):
            eng.dma_start(dst[:, :], a[f"L1_xattn_{w}"]).then_inc(loaded, 16)
        for dst, w in ((self.bq, "bq"), (self.bk, "bk")):
            eng.dma_start(dst[:, :], a[f"L1_xattn_{w}"].rearrange("(p o) -> p o", o=1)).then_inc(loaded, 16)
        for dst, w, rows in ((self.bv, "bv", SC), (self.gamma, "gamma", 128), (self.beta, "beta", 128)):
            eng.dma_start(dst[:, :], a[f"L1_xattn_{w}"].rearrange("(o n) -> o n", o=1).to_broadcast([rows, 128])).then_inc(loaded, 16)

    def tensor(self, pe, stage, g):
        nc, k, ctxT = self.nc, self.k, self.ctxT
        batches = list(enumerate(range(g * BG, (g + 1) * BG)))
        if stage == 0:
            wait(pe, self.xT_ready, g)
            for j, b in batches:
                last = nc.tensor.transpose(self.bank_x[:, j * S:(j + 1) * S], self.t_all[:, b, :], self.ident[:, :])
            last.then_inc(self.x_done, 1)
        if stage == 1:
            wait(pe, self.k_ready, g)
            nc.tensor.matmul(self.bank_k[:, 0:BG * SC], self.wk[:, :], ctxT[0:CD, g * BG:(g + 1) * BG, :],
                             start=True, stop=True).then_inc(self.k_done, 1)
            wait(pe, self.v_ready, g)
            for j, b in batches:
                last = nc.tensor.matmul(self.bank_v[0:SC, j * 128:(j + 1) * 128], ctxT[0:CD, b, :], self.wv[:, :],
                                        start=True, stop=True)
            last.then_inc(self.v_done, 1)
            pe.wait_ge(self.xT_ready, g + 1)
            wait(pe, self.q_ready, g)
            nc.tensor.matmul(self.bank_q[:, :], self.wq[:, :], k.xT[:, g * BG:(g + 1) * BG, :],
                             start=True, stop=True).then_inc(self.q_done, 1)
        if stage == 2:
            pe.wait_ge(self.q_ready, g + 1)
            pe.wait_ge(self.k_ready, g + 1)
            wait(pe, self.exp_done, BG * g)
            for j, b in batches:
                last = nc.tensor.matmul(self.bank_s[0:SC, j * S:(j + 1) * S], k.kT[:, b, 0:SC], k.qT[:, b, :],
                                        start=True, stop=True)
            last.then_inc(self.s_done, 1)
        if stage == 3:
            pe.wait_ge(self.w_ready, g + 1)
            pe.wait_ge(self.v_ready, g + 1)
            wait(pe, self.x1_ready, g)
            for j, b in batches:
                last = nc.tensor.matmul(self.bank_p[:, j * E:(j + 1) * E], k.probs[0:SC, b, :], k.v[0:SC, b, :],
                                        start=True, stop=True)
            last.then_inc(self.pred_done, 1)

    def scalar(self, act, stage, g):
        nc, k = self.nc, self.k
        gs = slice(g * BG, (g + 1) * BG)
        if stage == 0:
            act.wait_ge(self.x_done, g + 1)
            nc.scalar.activation(k.xT[:, gs, :], self.bank_x[:, :], ACT.Copy).then_inc(self.xT_ready, 1)
        if stage == 1:
            act.wait_ge(self.q_done, g + 1)
            nc.scalar.activation(k.qT[:, gs, :], self.bank_q[:, :], ACT.Identity, bias=self.bq[:, 0:1]).then_inc(self.q_ready, 1)
        if stage == 2:
            act.wait_ge(self.bias_done, g + 1)
            for j in range(BG):
                b = g * BG + j
                nc.scalar.activation(k.probs[0:SC, b, :], self.bank_s[0:SC, j * S:(j + 1) * S], ACT.Exp, bias=self.bias[:, b:b + 1],
                                     scale=SCALE1, accum_out=self.total[:, b:b + 1]).then_inc(self.exp_done, 1)

    def vector(self, dve, stage, g):
        nc, k = self.nc, self.k
        gs = slice(g * BG, (g + 1) * BG)
        if stage == 1:
            dve.wait_ge(self.k_done, g + 1)
            nc.vector.tensor_scalar(k.kT[:, gs, 0:SC], self.bank_k[:, 0:BG * SC].rearrange("p (b k) -> p b k", b=BG),
                                    self.bk[:, 0:1], None, ALU.add).then_inc(self.k_ready, 1)
            dve.wait_ge(self.v_done, g + 1)
            nc.vector.tensor_tensor(k.v[0:SC, gs, :], self.bank_v[0:SC, :].rearrange("p (b k) -> p b k", b=BG),
                                    self.bv[:, :].unsqueeze(1).to_broadcast([SC, BG, 128]), ALU.add).then_inc(self.v_ready, 1)
        if stage == 2:
            dve.wait_ge(self.s_done, g + 1)
            nc.vector.tensor_reduce(self.top[:, gs], self.bank_s[0:SC, :].rearrange("p (b k) -> p b k", b=BG),
                                    AX.X, ALU.max).then_inc(self.top_done, 1)
            dve.wait_ge(self.top_done, g + 1)
            nc.vector.tensor_scalar(self.bias[:, gs], self.top[:, gs], -SCALE1, None, ALU.mult).then_inc(self.bias_done, 1)
        if stage == 3:
            dve.wait_ge(self.pred_done, g + 1)
            nc.vector.tensor_tensor(k.x1[:, gs, :], self.bank_p[:, :].rearrange("p (b k) -> p b k", b=BG),
                                    self.t_all[:, gs, :], ALU.add).then_inc(self.x1_ready, 1)
            dve.wait_ge(self.x1_ready, g + 1)
            for b in range(g * BG, (g + 1) * BG):
                nc.vector.bn_stats(self.stats[:, b, :], k.x1[:, b, :]).then_inc(self.stats_done, 1)
            for b in range(g * BG, (g + 1) * BG):
                dve.wait_ge(self.stats_done, b + 1)
                nc.vector.bn_aggr(self.mv[:, b, :], self.stats[:, b, :]).then_inc(self.mv_done, 1)
        if stage == 4:
            dve.wait_ge(self.rstd_done, g + 1)
            for b in range(g * BG, (g + 1) * BG):
                nc.vector.tensor_scalar(k.z1[:, b, :], k.x1[:, b, :], self.mv[:, b, 0:1], self.rstd[:, b:b + 1],
                                        ALU.subtract, ALU.mult).then_inc(self.z1_done, 1)

    def normalise(self, dve, g):
        nc, k = self.nc, self.k
        gs = slice(g * BG, (g + 1) * BG)
        dve.wait_ge(self.exp_done, BG * (g + 1))
        nc.vector.reciprocal(self.part[:, gs], self.total[:, gs]).then_inc(self.part_done, 1)
        dve.wait_ge(self.part_done, g + 1)
        nc.vector.tensor_tensor(k.probs[0:SC, gs, :], k.probs[0:SC, gs, :], bcast(self.part[:, gs], [SC, BG, S]),
                                ALU.mult).then_inc(self.w_ready, 1)

    def gpsimd(self, pool, g):
        nc, k = self.nc, self.k
        gs = slice(g * BG, (g + 1) * BG)
        pool.wait_ge(self.mv_done, BG * (g + 1))
        nc.gpsimd.tensor_scalar(self.ve[:, gs], self.mv[:, gs, 1], L1_EPS, None, ALU.add).then_inc(self.ve_done, 1)
        pool.wait_ge(self.ve_done, g + 1)
        nc.gpsimd.tensor_tensor(self.rstd[:, gs], self.ve[:, gs], self.mhalf[:, :], ALU.pow).then_inc(self.rstd_done, 1)
        pool.wait_ge(self.z1_done, BG * (g + 1))
        nc.gpsimd.tensor_tensor(k.z2[:, gs, :], k.z1[:, gs, :], self.gamma[:, :].unsqueeze(1).to_broadcast([S, BG, E]),
                                ALU.mult).then_inc(self.z2_done, 1)
        pool.wait_ge(self.z2_done, g + 1)
        nc.gpsimd.tensor_tensor(self.t_all[:, gs, :], k.z2[:, gs, :], self.beta[:, :].unsqueeze(1).to_broadcast([S, BG, E]),
                                ALU.add).then_inc(self.t_ready, 1)


class CrossWeights:
    UNITS = 2 * L

    def __init__(self, nc, sb, sem, scope, banks, ahead):
        self.nc, self.ahead = nc, ahead
        self.bank_g, self.bank_n = banks

        def buf(what, shape):
            return sb(f"comb_{what}", shape, F32, scope)

        self.qw, self.ow = ([buf(f"{k}{i}", [128, NP, 128]) for i in range(2)] for k in ("q", "o"))
        self.kw, self.vw = ([buf(f"{k}{i}", [128, NP, 2, CD]) for i in range(2)] for k in ("k", "v"))
        self.loaded = [sem(f"comb_loaded{i}", scope) for i in range(2)]
        self.zeroed = sem("comb_zeroed", scope)
        self.g_done, self.n_done, self.g_ready, self.n_ready = (
            sem(f"comb_{k}", scope) for k in ("g_done", "n_done", "g_ready", "n_ready"))

    def load(self, sp, a, l):
        i = l % 2
        if l < 2:
            sp.wait_ge(self.zeroed, 2 * (l + 1))
        else:
            sp.wait_ge(self.n_done, 2 * (l - 1))
        for w, src in ((self.qw, a["caqT"]), (self.ow, a["L2_xattn_ca_ow"])):
            sp.dma_start(w[i][:, :, :], src[l].rearrange("(j p) n -> p j n", p=128)).then_inc(self.loaded[i], 16)
        for w, src in ((self.kw, a["cakT"]), (self.vw, a["cavT"])):
            for half in range(2):
                sp.dma_start(w[i][half * D:(half + 1) * D, :, half, :],
                             src[l].rearrange("(j e p) n -> e p j n", e=2, p=D)[half]).then_inc(self.loaded[i], 16)

    def zero(self):
        for i in range(2):
            for w in (self.kw[i], self.vw[i]):
                self.nc.gpsimd.memset(w[:, :, :, :], 0.0).then_inc(self.zeroed, 1)

    def tensor_g(self, pe, u):
        l, half = u // 2, u % 2
        i = l % 2
        if half == 0:
            pe.wait_ge(self.loaded[i], 96 * (l // 2 + 1))
        wait(pe, self.g_ready, u)
        for j in range(4):
            p = 4 * half + j
            last = self.nc.tensor.matmul(self.bank_g[:, j * 128:(j + 1) * 128], self.qw[i][:, p, :], self.kw[i][:, p, :, :],
                                         start=True, stop=True)
        last.then_inc(self.g_done, 1)

    def tensor_n(self, pe, u):
        i, half = u // 2 % 2, u % 2
        wait(pe, self.n_ready, u)
        for j in range(4):
            p = 4 * half + j
            last = self.nc.tensor.matmul(self.bank_n[:, j * 128:(j + 1) * 128], self.vw[i][:, p, :, :], self.ow[i][:, p, :],
                                         start=True, stop=True)
        last.then_inc(self.n_done, 1)

    def scalar(self, act, u):
        l, half = u // 2, u % 2
        act.wait_ge(self.g_done, u + 1)
        self.nc.scalar.activation(self.ahead.cq_all[:, l, half * 512:(half + 1) * 512], self.bank_g[:, :], ACT.Copy,
                                  scale=-(D ** -0.5)).then_inc(self.g_ready, 1)

    def vector(self, dve, u):
        l, half = u // 2, u % 2
        dve.wait_ge(self.n_done, u + 1)
        self.nc.vector.tensor_copy(self.ahead.co_all[:, l, 4 * half:4 * half + 4, :],
                                   self.bank_n[:, :].rearrange("p (j n) -> p j n", j=4)).then_inc(self.n_ready, 1)


def front(nc, a, sb, sem, banks, t_all, ctxT, ctx_all, ident, started, ahead):
    with ExitStack() as ctx:
        work = Work(sb, "front", ctx)
        w0 = ContextWeights(lambda name, shape: sb(name, shape, F32, ctx), "L0")
        l0 = QueryContext(nc, sb, sem, "L0", ctx, [banks[i] for i in (0, 1, 2, 5, 3, 4, 0, 1)], w0, work, BG, t_all, ctxT, ident)
        l1 = TokenSoftmax(nc, sb, sem, ctx, [banks[i] for i in (2, 3, 4, 5, 0, 1)], work, t_all, ctxT, ident)
        cross = CrossWeights(nc, sb, sem, ctx, banks[6:8], ahead)
        x_in = [sem(f"x_loaded{g}", ctx) for g in range(GROUPS)]
        ctx_in, l0_in, l1_in, mask_in, rest_in = (
            sem(k, ctx) for k in ("context_loaded", "L0_loaded", "L1_loaded", "masks_loaded", "decoder_loaded"))
        zeroed, made, masks_ready = sem("ident_zeroed", ctx), sem("ident_made", ctx), sem("masks_ready", ctx)
        upper_in, high_done, low_done = sem("upper_context_loaded", ctx), sem("high_done", ctx), sem("low_done", ctx)
        NS = l0.STAGES + l1.STAGES
        units_in = (0, 0, 1, 1, 1, 0, 0, 1, 1, 1, 2, 2, 1, 1)

        def ticks():
            return [(t, [(k, t - k) for k in reversed(range(NS)) if 0 <= t - k < GROUPS],
                     range(sum(units_in[:t]), sum(units_in[:t + 1]))) for t in range(NS + GROUPS - 1)]

        def load_x(eng, g):
            gs = slice(g * BG, (g + 1) * BG)
            eng.dma_start(t_all[:, gs, :], a["x"][gs].rearrange("b s e -> s b e")).then_inc(x_in[g], 16)

        with nc.Block() as block:
            @block.sync
            def _(sp):
                load_x(sp, 0)
                w0.load(sp, a, l0_in)
                for g in range(1, GROUPS):
                    load_x(sp, g)
                cross.load(sp, a, 0)
                cross.load(sp, a, 1)
                sp.dma_start(ctxT[CD:2 * CD, :, :], a["ctxT"]).then_inc(upper_in, 16)
                l1.load(sp, a, l1_in)
                for dst, src in ((ahead.norm_g, "L2_xattn_norm_g"), (ahead.norm_b, "L2_xattn_norm_b")):
                    sp.dma_start(dst[:, :], a[src].rearrange("(p o) -> p o", o=1)).then_inc(rest_in, 16)
                sp.dma_start(ahead.sa_mask[:, :, :].bitcast(I32), a["mask_BxSxS_ik0"].rearrange("b q k -> q b k")).then_inc(mask_in, 16)
                sp.dma_start(ahead.ca_mask[:, :, :].bitcast(I32), a["mask_Bx1xS2_if1"].rearrange("b o k -> o b k").to_broadcast([S, B, SC])).then_inc(mask_in, 16)
                for l in range(2, L):
                    cross.load(sp, a, l)
                for dst, src in ((ahead.wk, a["sa_k"]), (ahead.wq, a["L2_xattn_sa_q"]), (ahead.wv, a["sa_v"])):
                    sp.dma_start(dst[:, :], src[0]).then_inc(rest_in, 16)
                sp.dma_start(ctx_all[:, :, :], a["ctx_512"].rearrange("b k c -> k b c")).then_inc(rest_in, 16)
                sp.wait_ge(rest_in, 16 * 6)

            @block.gpsimd
            def _(pool):
                nc.gpsimd.memset(ident[:, :], 0.0).then_inc(zeroed, 1)
                pool.wait_ge(zeroed, 1)
                nc.gpsimd.affine_select(out=ident[:, :], in_=ident[:, :], compare_op=ALU.not_equal, fill=1.0,
                                        base=0, pattern=[[-1, 128]], channel_multiplier=1).then_inc(made, 1)
                pool.wait_ge(made, 1)
                pool.sem_inc(started, 1)
                cross.zero()
                nc.gpsimd.memset(l1.mhalf[:, :], -0.5).then_inc(l1.const_done, 1)
                pool.wait_ge(l0_in, ContextWeights.COUNT)
                for g in range(GROUPS):
                    pool.wait_ge(x_in[g], 16)
                    l0.gpsimd(pool, g)
                pool.wait_ge(ctx_in, 16)
                pool.wait_ge(upper_in, 16)
                low = ahead.ctxT_low
                nc.gpsimd.tensor_copy(low[:, :, :].bitcast(F32R), ctxT[:, :, :]).then_inc(high_done, 1)
                pool.wait_ge(high_done, 1)
                nc.gpsimd.tensor_tensor(low[:, :, :], ctxT[:, :, :], low[:, :, :], ALU.subtract).then_inc(low_done, 1)
                pool.wait_ge(l1.const_done, 1)
                pool.wait_ge(l1_in, l1.COUNT)
                for g in range(GROUPS):
                    l1.gpsimd(pool, g)

            @block.tensor
            def _(pe):
                pe.wait_ge(made, 1)
                free = {4: (l0.xT_ready, GROUPS), 5: (l0.q_ready, GROUPS), 6: (l0.k_ready, GROUPS),
                        8: (l0.att_ready, GROUPS), 9: (l0.t_ready, GROUPS)}
                for t, stages, units in ticks():
                    for u in units[:1]:
                        cross.tensor_g(pe, u)
                    for k, g in stages:
                        if g == 0 and k in free:
                            pe.wait_ge(*free[k])
                        if k == 0:
                            pe.wait_ge(x_in[g], 16)
                        if k == 1 and g == 0:
                            pe.wait_ge(l0_in, ContextWeights.COUNT)
                            pe.wait_ge(ctx_in, 16)
                        if k == l0.STAGES:
                            pe.wait_ge(l0.t_ready, g + 1)
                        if k == l0.STAGES + 1 and g == 0:
                            pe.wait_ge(l1_in, l1.COUNT)
                            pe.wait_ge(l0.exp_done, B)
                            pe.wait_ge(l0.pT_ready, GROUPS)
                            pe.wait_ge(l0.v_ready, GROUPS)
                        if k < l0.STAGES:
                            l0.tensor(pe, k, g)
                        else:
                            l1.tensor(pe, k - l0.STAGES, g)
                    for u in units[:1]:
                        cross.tensor_n(pe, u)
                    for u in units[1:]:
                        cross.tensor_g(pe, u)
                        cross.tensor_n(pe, u)

            @block.scalar
            def _(act):
                act.dma_start(ctxT[0:CD, :, :], a["ctxT"]).then_inc(ctx_in, 16)
                act.wait_ge(l0_in, ContextWeights.COUNT)
                for t, stages, units in ticks():
                    for k, g in stages:
                        if k == l0.STAGES + 1 and g == 0:
                            act.wait_ge(l1_in, l1.COUNT)
                        if k < l0.STAGES:
                            l0.scalar(act, k, g)
                        else:
                            l1.scalar(act, k - l0.STAGES, g)
                    for u in units:
                        cross.scalar(act, u)

            @block.vector
            def _(dve):
                dve.wait_ge(l0_in, ContextWeights.COUNT)
                for t, stages, units in ticks():
                    for k, g in stages:
                        if k == l0.STAGES + 1 and g == 0:
                            dve.wait_ge(l1_in, l1.COUNT)
                        if k < l0.STAGES:
                            l0.vector(dve, k, g)
                        else:
                            l1.vector(dve, k - l0.STAGES, g)
                    for u in units:
                        cross.vector(dve, u)
                    for k, g in stages:
                        if k == 2:
                            l0.normalise(dve, g)
                        if k == l0.STAGES + 2:
                            l1.normalise(dve, g)
                    if t == NS - 2:
                        dve.wait_ge(mask_in, 32)
                        for m in (ahead.sa_mask, ahead.ca_mask):
                            nc.vector.tensor_scalar(m[:, :, :], m[:, :, :].bitcast(I32), 0.0, MASKED, ALU.is_equal,
                                                    ALU.mult).then_inc(masks_ready, 1)


def l3(nc, a, sb, sem, banks, t_all, ctxT, ident, weights):
    with ExitStack() as ctx:
        bg = 2
        groups = B // bg
        work = Work(sb, "L3", ctx)
        q = QueryContext(nc, sb, sem, "L3", ctx, banks, weights, work, bg, t_all, ctxT, ident)
        stored = sem("L3_stored", ctx)
        ticks = [[(k, t - k) for k in reversed(range(q.STAGES)) if 0 <= t - k < groups] for t in range(q.STAGES + groups - 1)]
        with nc.Block() as block:
            @block.sync
            def _(sp):
                for g in range(groups):
                    sp.wait_ge(q.t_ready, g + 1)
                    sp.dma_start(a["out"][g * bg:(g + 1) * bg].rearrange("b s e -> s b e"),
                                 t_all[:, g * bg:(g + 1) * bg, :]).then_inc(stored, 16)
                sp.wait_ge(stored, 16 * groups)

            @block.gpsimd
            def _(pool):
                for g in range(groups):
                    q.gpsimd(pool, g)

            @block.tensor
            def _(pe):
                for stages in ticks:
                    for k, g in stages:
                        q.tensor(pe, k, g)

            @block.scalar
            def _(act):
                for stages in ticks:
                    for k, g in stages:
                        q.scalar(act, k, g)

            @block.vector
            def _(dve):
                for stages in ticks:
                    for k, g in stages:
                        q.vector(dve, k, g)
                    for k, g in stages:
                        if k == 2:
                            q.normalise(dve, g)


def decoder(nc, a, sb_, sem_, banks, t_all, ctxT, ctx_all, ident, started, ahead, l3_weights):
    with ExitStack() as ctx:
        def buf(name, shape, dt=F32):
            return sb_(f"L2_{name}", shape, dt, ctx)

        wq, wk, wv, norm_g, norm_b = ahead.wq, ahead.wk, ahead.wv, ahead.norm_g, ahead.norm_b
        sa_mask, ca_mask = ahead.sa_mask, ahead.ca_mask
        cq_all, co_all = ahead.cq_all, ahead.co_all
        ctxT_low = ahead.ctxT_low
        sa_wo, sa_ob = buf("sa_wo", [128, NP, E]), buf("sa_ob", [128, E])
        cq, co, ca_ob = buf("cq", [E, HD]), buf("co", [128, NP, E]), buf("ca_ob", [128, E])
        w1, b1, w2, b2 = buf("w1", [E, FF]), buf("b1", [128, NF]), buf("w2", [128, NF, E]), buf("b2", [128, E])
        pre_g, pre_b = buf("pre_g", [E, 1]), buf("pre_b", [E, 1])
        sa_mask_now, ca_mask_now = buf("sa_mask_now", [S, S]), buf("ca_mask_now", [S, SC])
        keys_high, keys_low = (buf(f"keys_{k}", [128, 2, SC], F32R) for k in ("high", "low"))
        ctx_vals = buf("ctx_vals", [SC, CD])
        own_half = buf("own_half", [128, 2])
        qT, kT = buf("qT", [128, NP, S]), buf("kT", [128, NP, 2, S])
        v = buf("v", [S, HD])
        oT, c_oT = buf("oT", [128, NP, S]), buf("c_oT", [128, NP, S])
        cqT_high, cqT_low = (buf(f"cqT_{k}", [128, NP, S], F32R) for k in ("high", "low"))
        masked = [buf(f"masked{i}", [S, GH, S]) for i in range(2)]
        probs = [buf(f"probs{i}", [S, GH, S]) for i in range(2)]
        pT = [buf(f"pT{i}", [S, GH, S]) for i in range(2)]
        c_masked = [buf(f"c_masked{i}", [S, GH, SC]) for i in range(2)]
        c_probs = [buf(f"c_probs{i}", [S, GH, SC]) for i in range(2)]
        c_pT = [buf(f"c_pT{i}", [SC, GH, S]) for i in range(2)]
        least, total, part = buf("least", [S, H]), buf("total", [S, H]), buf("part", [S, H])
        c_least, c_total, c_part = buf("c_least", [S, H]), buf("c_total", [S, H]), buf("c_part", [S, H])
        hid = buf("hid", [128, NF, S])
        mhalf = buf("mhalf", [S, 1])

        def sem(name):
            return sem_(f"L2_{name}", ctx)

        def group_sems(name):
            return [sem(f"{name}{g}") for g in range(NG)]

        class Norm:
            def __init__(self, name):
                self.stats, self.mv = buf(f"{name}_stats", [S, 6]), buf(f"{name}_mv", [S, 2])
                self.ve, self.rstd = buf(f"{name}_ve", [S, 1]), buf(f"{name}_rstd", [S, 1])
                self.z, self.tnT, self.tb = buf(f"{name}_z", [S, E]), buf(f"{name}_tnT", [E, S]), buf(f"{name}_tb", [S, E])
                self.stats_done, self.mv_done = sem(f"{name}_stats_done"), sem(f"{name}_mv_done")
                self.ve_done, self.rstd_done = sem(f"{name}_ve_done"), sem(f"{name}_rstd_done")
                self.z_done, self.turned = sem(f"{name}_z_done"), sem(f"{name}_z_turned")
                self.tnT_ready, self.tb_ready = sem(f"{name}_tnT_ready"), sem(f"{name}_tb_ready")

        sa, ca, ff = Norm("sa"), Norm("ca"), Norm("ff")
        w_qkv, w_so, w_cq, w_co, w_ff = (sem(f"weights_{k}") for k in ("qkv", "so", "cq", "co", "ff"))
        load = [sem(f"load_{k}") for k in ("qkv", "so", "cq", "co", "ff")]
        halves_ready = sem("halves_ready")
        zeros_done, const_done, l3_in = sem("zeros_done"), sem("const_done"), sem("l3_loaded")
        sa_mask_set, ca_mask_set, keys_set, vals_set = (sem(k) for k in ("sa_mask_set", "ca_mask_set", "keys_set", "vals_set"))
        sc_done, masked_done, exp_done, part_done, probs_ready, pt_done, pT_ready, pv_done, oT_ready = (
            group_sems(f"sa_{k}") for k in ("scores_done", "masked_done", "exp_done", "part_done", "probs_ready",
                                            "probs_turned", "pT_ready", "pv_done", "oT_ready"))
        csc_done, cmasked_done, cexp_done, cpart_done, cprobs_ready, cpt_done, cpT_ready, cpv_done, coT_ready = (
            group_sems(f"ca_{k}") for k in ("scores_done", "masked_done", "exp_done", "part_done", "probs_ready",
                                            "probs_turned", "pT_ready", "pv_done", "oT_ready"))
        q_done, k_done, v_done, q_ready, v_ready = (
            [sem(f"sa_{k}{i}") for i in range(2)] for k in ("q_done", "k_done", "v_done", "q_ready", "v_ready"))
        k_ready = [[sem(f"sa_k_ready{i}_{half}") for half in range(2)] for i in range(2)]
        cq_done, cq_high_ready, cq_ready = (
            [sem(f"ca_{k}{i}") for i in range(2)] for k in ("q_done", "q_high_ready", "q_ready"))
        o_done, co_done = sem("sa_o_done"), sem("ca_o_done")
        sa_out, ca_out, ff_out = sem("sa_out"), sem("ca_out"), sem("ff_out")
        up_done, hid_ready, down_done = sem("ff_up_done"), sem("ff_hid_ready"), sem("ff_down_done")

        sc_b, csc_b, pt_b, cpt_b, pv_b, cpv_b = banks[0:6]
        pj = banks[6:8]
        bank_users = (
            (("ca_query", (cq_ready[0],), 0),
             ("up", (hid_ready,), -1),
             ("key", (k_ready[0][0], k_ready[0][1]), 2),
             ("sa_project", (sa_out,), 1),
             ("query", (q_ready[0],), 2),
             ("value", (v_ready[0],), 2)),
            (("ca_project", (ca_out,), -1),
             ("ca_query", (cq_ready[1],), 0),
             ("down", (ff_out,), -1),
             ("query", (q_ready[1],), 2),
             ("key", (k_ready[1][0], k_ready[1][1]), 2),
             ("value", (v_ready[1],), 2)),
        )

        def stages(n):
            if not isinstance(n, int):
                return True, True, True, True
            return n + 1 < N, 0 <= n < N, 0 <= n - 1 < N, 0 <= n - 2 < N

        def counts(eng, n):
            at = {k: eng.alloc_register(f"count{k}") for k in range(-2, 3)}
            for k, register in at.items():
                eng.reg_mov(register, n + k)
            return at

        def run(eng, body):
            for n in range(-1, 3):
                body(n, {k: n + k for k in range(-2, 3)})
            with eng.Fori(3, N - 1) as n:
                body(n, counts(eng, n))
            for n in range(N - 1, N + 2):
                body(n, {k: n + k for k in range(-2, 3)})

        def hold(eng, sem, value):
            if not isinstance(value, int):
                eng.wait_ge(started, 1)
            wait(eng, sem, value)

        def counted(eng, at):
            made = set()

            def first(sem, k):
                before = (sem.name, k) in made
                made.add((sem.name, k))
                return not before

            def need(sem, k):
                if first(sem, k):
                    wait(eng, sem, at[k])

            def held(sem, k):
                if first(sem, k):
                    hold(eng, sem, at[k])

            return need, held

        with nc.Block() as block:
            @block.sync
            def _(sp):
                l_qkv, l_so, l_cq, l_co, l_ff = load

                def rows(src, l, n):
                    return src[bass.ds(l, 1), :].to_broadcast([n, 128])

                def cols(src, l):
                    return src[bass.ds(l, 1), :].rearrange("o (c p) -> p (o c)", p=128)

                def load_qkv(l):
                    sp.dma_start(wk[:, :], a["sa_k"][bass.ds(l, 1)].rearrange("o p n -> (o p) n")).then_inc(l_qkv, 16)
                    sp.dma_start(wq[:, :], a["L2_xattn_sa_q"][bass.ds(l, 1)].rearrange("o p n -> (o p) n")).then_inc(l_qkv, 16)
                    sp.dma_start(wv[:, :], a["sa_v"][bass.ds(l, 1)].rearrange("o p n -> (o p) n")).then_inc(l_qkv, 16)

                def load_so(l):
                    sp.dma_start(sa_wo[:, :, :], a["L2_xattn_sa_ow"][bass.ds(l, 1)].rearrange("o (j p) n -> p (o j) n", p=128)).then_inc(l_so, 16)
                    sp.dma_start(sa_ob[:, :], rows(a["L2_xattn_sa_ob"], l, 128)).then_inc(l_so, 16)

                def load_cq(l):
                    sp.dma_start(cq[:, :], cq_all[:, bass.ds(l, 1), :].rearrange("p o n -> p (o n)")).then_inc(l_cq, 16)

                def load_co(l):
                    sp.dma_start(co[:, :, :], co_all[:, bass.ds(l, 1), :, :].rearrange("p o j n -> p (o j) n")).then_inc(l_co, 16)
                    sp.dma_start(ca_ob[:, :], rows(a["L2_xattn_ca_ob"], l, 128)).then_inc(l_co, 16)

                def load_ff(l):
                    sp.dma_start(w1[:, :], a["L2_xattn_ff_w1"][bass.ds(l, 1)].rearrange("o p n -> (o p) n")).then_inc(l_ff, 16)
                    sp.dma_start(w2[:, :, :], a["L2_xattn_ff_w2"][bass.ds(l, 1)].rearrange("o (j p) n -> p (o j) n", p=128)).then_inc(l_ff, 16)
                    sp.dma_start(b2[:, :], rows(a["L2_xattn_ff_b2"], l, 128)).then_inc(l_ff, 16)
                    sp.dma_start(b1[:, :], a["ffb1T"][bass.ds(l, 1)].rearrange("o p c -> (o p) c")).then_inc(l_ff, 16)
                    sp.dma_start(pre_g[:, :], cols(a["L2_xattn_pre_g"], l)).then_inc(l_ff, 16)
                    sp.dma_start(pre_b[:, :], cols(a["L2_xattn_pre_b"], l)).then_inc(l_ff, 16)

                def landed(sem, each, before, ready):
                    hold(sp, sem, (before + 1) * 16 * each)
                    sp.sem_inc(ready, B)

                sp.sem_inc(w_qkv, B)
                load_so(0)
                load_cq(0)
                load_co(0)
                load_ff(0)
                landed(l_so, 2, 0, w_so)
                landed(l_cq, 1, 0, w_cq)
                landed(l_co, 2, 0, w_co)
                landed(l_ff, 6, 0, w_ff)
                l3_weights.load(sp, a, l3_in)
                sp.wait_ge(l3_in, l3_weights.COUNT)
                with sp.Fori(1, L) as l:
                    hold(sp, v_done[0], l * B)
                    load_qkv(l)
                    landed(l_qkv, 3, l - 1, w_qkv)
                    hold(sp, o_done, l * B)
                    hold(sp, sa.tb_ready, l * B)
                    load_so(l)
                    landed(l_so, 2, l, w_so)
                    hold(sp, cq_done[1], l * B)
                    load_cq(l)
                    landed(l_cq, 1, l, w_cq)
                    hold(sp, co_done, l * B)
                    hold(sp, ca.tb_ready, l * B)
                    load_co(l)
                    landed(l_co, 2, l, w_co)
                    hold(sp, down_done, l * B)
                    hold(sp, ff.tb_ready, l * B)
                    load_ff(l)
                    landed(l_ff, 6, l, w_ff)

            @block.tensor
            def _(pe):
                pe.wait_ge(const_done, 1)

                def body(n, at):
                    need, held = counted(pe, at)
                    run_qkv, run_sa, run_ca, run_ff = stages(n)
                    qkv_now, sa_now, ca_now, ff_now = 2, 1, 0, -1

                    def bank(i, name):
                        users = bank_users[i]
                        at = [u[0] for u in users].index(name)
                        if isinstance(n, int):
                            for k, (_, copied, offset) in enumerate(users):
                                for s in copied:
                                    wait(pe, s, min(n + offset - (k >= at), N))
                        else:
                            _, copied, offset = users[at - 1]
                            for s in copied:
                                need(s, offset - (at == 0))
                        return pj[i]

                    def turn(st, now, bank, copied):
                        need(st.z_done, now)
                        need(copied, now - 1)
                        nc.tensor.transpose(bank[:, 0:S], st.z[:, :], ident[:, :]).then_inc(st.turned, 1)

                    def project_T(weights, rhs, i, name, done):
                        out = bank(i, name)
                        for j in range(4):
                            c = 4 * i + j
                            last = nc.tensor.matmul(out[:, j * S:(j + 1) * S], weights[:, c * 128:(c + 1) * 128], rhs,
                                                    start=True, stop=True)
                        last.then_inc(done, 1)

                    def query(i):
                        need(sa.tnT_ready, qkv_now)
                        need(w_qkv, qkv_now)
                        project_T(wq, sa.tnT[:, :], i, "query", q_done[i])

                    def key(i):
                        need(sa.tnT_ready, qkv_now)
                        need(w_qkv, qkv_now)
                        project_T(wk, sa.tnT[:, :], i, "key", k_done[i])

                    def value(i):
                        need(sa.tnT_ready, qkv_now)
                        need(w_qkv, qkv_now)
                        nc.tensor.matmul(bank(i, "value")[:, :], sa.tnT[:, :], wv[:, i * 512:(i + 1) * 512],
                                         start=True, stop=True).then_inc(v_done[i], 1)

                    def ca_query(i):
                        need(ca.tnT_ready, ca_now)
                        need(w_cq, ca_now)
                        project_T(cq, ca.tnT[:, :], i, "ca_query", cq_done[i])

                    def sa_scores(g):
                        need(q_ready[g // 2], sa_now)
                        need(k_ready[g // 2][0], sa_now)
                        need(k_ready[g // 2][1], sa_now)
                        need(masked_done[(g - 1) % NG], sa_now if g else sa_now - 1)
                        for j in range(2):
                            p = 2 * g + j
                            last = nc.tensor.matmul(sc_b[:, j * 2 * S:(j + 1) * 2 * S], qT[:, p, :], kT[:, p, :, :],
                                                    start=True, stop=True)
                        last.then_inc(sc_done[g], 1)

                    def ca_scores(g):
                        need(cq_ready[g // 2], ca_now)
                        need(keys_set, ca_now)
                        need(cmasked_done[(g - 1) % NG], ca_now if g else ca_now - 1)
                        for j in range(2):
                            p = 2 * g + j
                            parts = ((cqT_high, keys_high), (cqT_high, keys_low), (cqT_low, keys_high))
                            for i, (q, k) in enumerate(parts):
                                last = nc.tensor.matmul(csc_b[:, j * 2 * SC:(j + 1) * 2 * SC], q[:, p, :], k[:, :, :],
                                                        start=(i == 0), stop=(i == 2))
                        last.then_inc(csc_done[g], 1)

                    def sa_values(g):
                        need(probs_ready[g], sa_now)
                        need(pT_ready[(g - 1) % NG], sa_now if g else sa_now - 1)
                        if g == NG - 1 and run_qkv:
                            need(sa.tnT_ready, qkv_now)
                        for j in range(GH):
                            last = nc.tensor.transpose(pt_b[:, j * S:(j + 1) * S], probs[g % 2][:, j, :], ident[:, :])
                        last.then_inc(pt_done[g], 1)

                    def sa_outputs(g):
                        need(pT_ready[g], sa_now)
                        need(v_ready[g // 2], sa_now)
                        need(oT_ready[(g - 1) % NG], sa_now if g else sa_now - 1)
                        for j in range(GH):
                            h, half = g * GH + j, j % 2
                            last = nc.tensor.matmul(pv_b[half * D:(half + 1) * D, (j // 2) * S:(j // 2 + 1) * S],
                                                    v[:, h * D:(h + 1) * D], pT[g % 2][:, j, :], start=True, stop=True)
                        last.then_inc(pv_done[g], 1)

                    def ca_values(g):
                        need(cprobs_ready[g], ca_now)
                        need(cpT_ready[(g - 1) % NG], ca_now if g else ca_now - 1)
                        if g == 0:
                            need(ca.tnT_ready, ca_now)
                        for j in range(GH):
                            last = nc.tensor.transpose(cpt_b[0:SC, j * S:(j + 1) * S], c_probs[g % 2][:, j, :], ident[:, :])
                        last.then_inc(cpt_done[g], 1)

                    def ca_outputs(g):
                        need(cpT_ready[g], ca_now)
                        need(vals_set, ca_now)
                        if g == 0 and run_ff:
                            need(ff.tnT_ready, ff_now)
                        need(coT_ready[(g - 1) % NG], ca_now if g else ca_now - 1)
                        pairs = c_pT[g % 2][:, :, :].rearrange("k (j e) q -> k j e q", e=2)
                        for half in range(2):
                            last = nc.tensor.matmul(cpv_b[half * D:(half + 1) * D, 0:2 * S], ctx_vals[:, :],
                                                    pairs[:, :, half, :], start=True, stop=True)
                        last.then_inc(cpv_done[g], 1)

                    def out_projection(oT, oT_ready, wo, loaded, now, i, name, done):
                        for ready in oT_ready:
                            need(ready, now)
                        need(loaded, now)
                        out = bank(i, name)
                        for p in range(NP):
                            last = nc.tensor.matmul(out[:, 0:E], oT[:, p, :], wo[:, p, :], start=(p == 0), stop=(p == NP - 1))
                        last.then_inc(done, 1)

                    def sa_project():
                        out_projection(oT, oT_ready, sa_wo, w_so, sa_now, 0, "sa_project", o_done)

                    def ca_project():
                        out_projection(c_oT, coT_ready, co, w_co, ff_now, 1, "ca_project", co_done)

                    def feed_up():
                        need(ff.tnT_ready, ff_now)
                        need(w_ff, ff_now)
                        out = bank(0, "up")
                        for c in range(NF):
                            last = nc.tensor.matmul(out[:, c * S:(c + 1) * S], w1[:, c * 128:(c + 1) * 128], ff.tnT[:, :],
                                                    start=True, stop=True)
                        last.then_inc(up_done, 1)

                    def feed_down():
                        need(hid_ready, ff_now)
                        out = bank(1, "down")
                        for c in range(NF):
                            last = nc.tensor.matmul(out[:, 0:E], hid[:, c, :], w2[:, c, :], start=(c == 0), stop=(c == NF - 1))
                        last.then_inc(down_done, 1)

                    if run_sa:
                        sa_scores(0)
                    if run_ca:
                        turn(ca, ca_now, cpt_b, cpT_ready[NG - 1])
                    if run_ff:
                        ca_project()
                    if run_sa:
                        sa_scores(1)
                    if run_ca:
                        ca_query(0)
                        ca_query(1)
                    if run_sa:
                        sa_scores(2)
                    if run_ff:
                        turn(ff, ff_now, cpv_b, coT_ready[NG - 1])
                    if run_sa:
                        sa_values(0)
                    if run_ca:
                        ca_scores(0)
                    if run_ff:
                        feed_up()
                    if run_sa:
                        sa_scores(3)
                        sa_outputs(0)
                        sa_values(1)
                    if run_ca:
                        ca_scores(1)
                    if run_ff:
                        feed_down()
                    if run_sa:
                        sa_values(2)
                        sa_outputs(1)
                    if run_ca:
                        ca_scores(2)
                    if run_qkv:
                        turn(sa, qkv_now, pt_b, pT_ready[NG - 2])
                    if run_ca:
                        ca_values(0)
                    if run_sa:
                        sa_outputs(2)
                    if run_qkv:
                        query(1)
                    if run_sa:
                        sa_values(3)
                    if run_qkv:
                        key(0)
                    if run_ca:
                        ca_scores(3)
                    if run_sa:
                        sa_outputs(3)
                    if run_ca:
                        ca_outputs(0)
                        ca_values(1)
                    if run_sa:
                        sa_project()
                    if run_ca:
                        ca_outputs(1)
                        ca_values(2)
                    if run_qkv:
                        key(1)
                        query(0)
                    if run_ca:
                        ca_outputs(2)
                        ca_values(3)
                    if run_qkv:
                        value(1)
                        value(0)
                    if run_ca:
                        ca_outputs(3)

                run(pe, body)

            def copies_out(need, copy):
                qkv_now, ca_now = 2, 0

                def take_pT(g, now, turned, bank, rows, pT, users, ready):
                    need(turned[g], now)
                    need(users[(g - 2) % NG], now if g >= 2 else now - 1)
                    copy(pT[g % 2][:, :, :], bank[0:rows, :].rearrange("p (j q) -> p j q", j=GH)).then_inc(ready[g], 1)

                def take_oT(g, now, done, bank, oT, projected, ready):
                    need(done[g], now)
                    need(projected, now - 1)
                    copy(oT[:, 2 * g:2 * g + 2, :], bank[:, 0:2 * S].rearrange("p (j q) -> p j q", j=2)).then_inc(ready[g], 1)

                def take_ca_query(i):
                    need(cq_done[i], ca_now)
                    need(csc_done[2 * i + 1], ca_now - 1)
                    copy(cqT_high[:, 4 * i:4 * i + 4, :], pj[i][:, :].rearrange("p (c q) -> p c q", c=4)).then_inc(cq_high_ready[i], 1)

                def take_query(i):
                    need(q_done[i], qkv_now)
                    need(sc_done[2 * i + 1], qkv_now - 1)
                    copy(qT[:, 4 * i:4 * i + 4, :], pj[i][:, :].rearrange("p (c q) -> p c q", c=4), -(D ** -0.5)).then_inc(q_ready[i], 1)

                def take_key(i, half):
                    need(k_done[i], qkv_now)
                    need(sc_done[2 * i + 1], qkv_now - 1)
                    rows = slice(half * D, (half + 1) * D)
                    copy(kT[rows, 4 * i:4 * i + 4, half, :], pj[i][rows, :].rearrange("p (c k) -> p c k", c=4)).then_inc(k_ready[i][half], 1)

                def take_value(i):
                    need(v_done[i], qkv_now)
                    need(pv_done[2 * i + 1], qkv_now - 1)
                    copy(v[:, i * 512:(i + 1) * 512], pj[i][:, :]).then_inc(v_ready[i], 1)

                return take_pT, take_oT, take_ca_query, take_query, take_key, take_value

            @block.scalar
            def _(act):
                act.wait_ge(const_done, 1)

                def body(n, at):
                    need, held = counted(act, at)
                    run_qkv, run_sa, run_ca, run_ff = stages(n)
                    qkv_now, sa_now, ca_now, ff_now = 2, 1, 0, -1
                    take_pT, take_oT, take_ca_query, take_query, take_key, take_value = copies_out(
                        need, lambda out, in_, scale=1.0: nc.scalar.activation(out, in_, ACT.Copy, scale=scale))

                    def affine(st, now, bank, gain, offset, user):
                        need(st.turned, now)
                        if st is ff:
                            need(w_ff, now)
                        need(user, now - 1)
                        nc.scalar.activation(st.tnT[:, :], bank[:, 0:S], ACT.Identity, bias=offset[:, 0:1],
                                             scale=gain[:, 0:1]).then_inc(st.tnT_ready, 1)

                    def exps(g, now, masked_done, masked, least, probs, total, turned, done):
                        need(masked_done[g], now)
                        need(turned[(g - 2) % NG], now if g >= 2 else now - 1)
                        for j in range(GH):
                            h = g * GH + j
                            last = nc.scalar.activation(probs[g % 2][:, j, :], masked[g % 2][:, j, :], ACT.Exp,
                                                        bias=least[:, h:h + 1], scale=-1.0, accum_out=total[:, h:h + 1])
                        last.then_inc(done[g], 1)

                    def sa_exps(g):
                        exps(g, sa_now, masked_done, masked, least, probs, total, pt_done, exp_done)

                    def ca_exps(g):
                        exps(g, ca_now, cmasked_done, c_masked, c_least, c_probs, c_total, cpt_done, cexp_done)

                    if run_ca:
                        affine(ca, ca_now, cpt_b, norm_g, norm_b, cq_done[1])
                    if run_sa:
                        sa_exps(0)
                    if run_ca:
                        take_ca_query(0)
                    if run_sa:
                        sa_exps(1)
                    if run_ff:
                        affine(ff, ff_now, cpv_b, pre_g, pre_b, up_done)
                    if run_sa:
                        take_pT(0, sa_now, pt_done, pt_b, S, pT, pv_done, pT_ready)
                        sa_exps(2)
                    if run_ca:
                        ca_exps(0)
                    if run_sa:
                        take_pT(1, sa_now, pt_done, pt_b, S, pT, pv_done, pT_ready)
                        take_oT(0, sa_now, pv_done, pv_b, oT, o_done, oT_ready)
                        sa_exps(3)
                        take_oT(1, sa_now, pv_done, pv_b, oT, o_done, oT_ready)
                    if run_qkv:
                        affine(sa, qkv_now, pt_b, norm_g, norm_b, v_done[0])
                    if run_ca:
                        ca_exps(1)
                    if run_qkv:
                        take_query(1)
                    if run_sa:
                        take_pT(3, sa_now, pt_done, pt_b, S, pT, pv_done, pT_ready)
                    if run_ca:
                        ca_exps(2)
                    if run_sa:
                        take_oT(3, sa_now, pv_done, pv_b, oT, o_done, oT_ready)
                    if run_ca:
                        take_oT(0, ca_now, cpv_done, cpv_b, c_oT, co_done, coT_ready)
                        take_pT(1, ca_now, cpt_done, cpt_b, SC, c_pT, cpv_done, cpT_ready)
                        ca_exps(3)
                        take_oT(1, ca_now, cpv_done, cpv_b, c_oT, co_done, coT_ready)
                    if run_qkv:
                        take_query(0)
                    if run_ca:
                        take_oT(2, ca_now, cpv_done, cpv_b, c_oT, co_done, coT_ready)
                        take_pT(3, ca_now, cpt_done, cpt_b, SC, c_pT, cpv_done, cpT_ready)
                    if run_qkv:
                        take_value(0)
                    if run_ca:
                        take_oT(3, ca_now, cpv_done, cpv_b, c_oT, co_done, coT_ready)

                run(act, body)

            @block.gpsimd
            def _(pool):
                nc.gpsimd.memset(mhalf[:, :], -0.5).then_inc(zeros_done, 1)
                nc.gpsimd.memset(kT[:, :, :, :], 0.0).then_inc(zeros_done, 1)
                pool.wait_ge(zeros_done, 2)
                pool.sem_inc(const_done, 1)

                def body(n, at):
                    need, held = counted(pool, at)
                    run_qkv, run_sa, run_ca, run_ff = stages(n)
                    qkv_now, sa_now, ca_now, ff_now = 2, 1, 0, -1

                    def rows_of(batch, what=t_all):
                        return what[:, bass.ds(batch, 1), :].rearrange("p o e -> p (o e)")

                    def rstd(st, now):
                        held(st.mv_done, now)
                        nc.gpsimd.tensor_scalar(st.ve[:, :], st.mv[:, 1:2], LN_EPS, None, ALU.add).then_inc(st.ve_done, 1)
                        held(st.ve_done, now)
                        nc.gpsimd.tensor_tensor(st.rstd[:, :], st.ve[:, :], mhalf[:, :], ALU.pow).then_inc(st.rstd_done, 1)

                    def plus_bias(st, now, batch, bias, loaded, used):
                        held(loaded, now)
                        held(used, now - 1)
                        nc.gpsimd.tensor_tensor(st.tb[:, :], rows_of(batch), bias[:, :], ALU.add).then_inc(st.tb_ready, 1)

                    def normalise(g, now, parts, probs, part, ready, w):
                        held(parts[g], now)
                        nc.gpsimd.tensor_tensor(probs[g % 2][:, :, :], probs[g % 2][:, :, :],
                                                bcast(part[:, g * GH:(g + 1) * GH], [S, GH, w]), ALU.mult).then_inc(ready[g], 1)

                    def sa_norm(g):
                        normalise(g, sa_now, part_done, probs, part, probs_ready, S)

                    def ca_norm(g):
                        normalise(g, ca_now, cpart_done, c_probs, c_part, cprobs_ready, SC)

                    def set_keys():
                        held(csc_done[NG - 1], ca_now - 1)
                        for keys, part in ((keys_high, ctxT), (keys_low, ctxT_low)):
                            last = nc.gpsimd.tensor_tensor(keys[:, :, :], part[:, bass.ds((n - 1) % B, 1), :].to_broadcast([128, 2, SC]),
                                                           bcast(own_half[:, :], [128, 2, SC]), ALU.mult)
                        last.then_inc(keys_set, 1)

                    def set_ca_mask():
                        held(cmasked_done[NG - 1], ca_now - 1)
                        nc.gpsimd.tensor_copy(ca_mask_now[:, :], rows_of((n - 1) % B, ca_mask)).then_inc(ca_mask_set, 1)

                    def set_vals():
                        held(cpv_done[NG - 1], ca_now - 1)
                        nc.gpsimd.tensor_copy(ctx_vals[:, :], rows_of((n - 1) % B, ctx_all)).then_inc(vals_set, 1)

                    def set_sa_mask():
                        held(masked_done[NG - 1], qkv_now - 1)
                        nc.gpsimd.tensor_copy(sa_mask_now[:, :], rows_of((n + 1) % B, sa_mask)).then_inc(sa_mask_set, 1)

                    if run_qkv:
                        rstd(sa, qkv_now)
                    if run_ca:
                        set_vals()
                    if run_sa:
                        plus_bias(sa, sa_now, n % B, sa_ob, w_so, sa_out)
                    if run_ca:
                        set_keys()
                    if run_ff:
                        rstd(ff, ff_now)
                    if run_sa:
                        sa_norm(0)
                    if run_ff:
                        plus_bias(ff, ff_now, (n - 2) % B, b2, w_ff, ff_out)
                    if run_ca:
                        set_ca_mask()
                        plus_bias(ca, ca_now, (n - 1) % B, ca_ob, w_co, ca_out)
                    if run_sa:
                        sa_norm(1)
                        sa_norm(2)
                    if run_ca:
                        ca_norm(0)
                    if run_sa:
                        sa_norm(3)
                    if run_qkv:
                        set_sa_mask()
                    if run_ca:
                        ca_norm(1)
                        ca_norm(2)
                        ca_norm(3)
                    if run_sa:
                        rstd(ca, sa_now)

                pool.wait_ge(halves_ready, 3)
                run(pool, body)

            @block.vector
            def _(dve):
                nc.vector.memset(own_half[:, :], 0.0).then_inc(halves_ready, 1)
                dve.wait_ge(halves_ready, 1)
                for half in range(2):
                    nc.vector.memset(own_half[half * D:(half + 1) * D, half:half + 1], 1.0).then_inc(halves_ready, 1)
                dve.wait_ge(const_done, 1)

                def body(n, at):
                    need, held = counted(dve, at)
                    run_qkv, run_sa, run_ca, run_ff = stages(n)
                    qkv_now, sa_now, ca_now, ff_now = 2, 1, 0, -1

                    def copy(out, in_, scale=1.0):
                        if scale == 1.0:
                            return nc.vector.tensor_copy(out, in_)
                        return nc.vector.tensor_scalar(out, in_, scale, None, ALU.mult)

                    take_pT, take_oT, take_ca_query, take_query, take_key, take_value = copies_out(need, copy)

                    def rows_of(batch):
                        return t_all[:, bass.ds(batch, 1), :].rearrange("p o e -> p (o e)")

                    def stats(st, now, batch, written):
                        if written is not None:
                            held(written, now)
                        nc.vector.bn_stats(st.stats[:, :], rows_of(batch)).then_inc(st.stats_done, 1)
                        held(st.stats_done, now)
                        held(st.ve_done, now - 1)
                        nc.vector.bn_aggr(st.mv[:, :], st.stats[:, :]).then_inc(st.mv_done, 1)

                    def centre(st, now, batch):
                        held(st.rstd_done, now)
                        held(st.turned, now - 1)
                        nc.vector.tensor_scalar(st.z[:, :], rows_of(batch), st.mv[:, 0:1], st.rstd[:, 0:1],
                                                ALU.subtract, ALU.mult).then_inc(st.z_done, 1)

                    def mask(g, now, done, bank, mask, mask_set, masked, least, exps, ready, w):
                        held(done[g], now)
                        held(mask_set, now)
                        held(exps[(g - 2) % NG], now if g >= 2 else now - 1)
                        for j in range(GH):
                            h = g * GH + j
                            last = nc.vector.tensor_tensor_reduce(out=masked[g % 2][:, j, :], in0=bank[:, j * w:(j + 1) * w], in1=mask[:, :],
                                                                  scale=1.0, scalar=3e38, op0=ALU.add, op1=ALU.min,
                                                                  accum_out=least[:, h:h + 1])
                        last.then_inc(ready[g], 1)

                    def sa_mask_(g):
                        mask(g, sa_now, sc_done, sc_b, sa_mask_now, sa_mask_set, masked, least, exp_done, masked_done, S)

                    def ca_mask_(g):
                        mask(g, ca_now, csc_done, csc_b, ca_mask_now, ca_mask_set, c_masked, c_least, cexp_done, cmasked_done, SC)

                    def ca_query_low(i):
                        need(cq_high_ready[i], ca_now)
                        nc.vector.tensor_tensor(cqT_low[:, 4 * i:4 * i + 4, :], pj[i][:, :].rearrange("p (c q) -> p c q", c=4),
                                                cqT_high[:, 4 * i:4 * i + 4, :].bitcast(F32), ALU.subtract).then_inc(cq_ready[i], 1)

                    def over(g, now, exps, total, part, done):
                        need(exps[g], now)
                        nc.vector.reciprocal(part[:, g * GH:(g + 1) * GH], total[:, g * GH:(g + 1) * GH]).then_inc(done[g], 1)

                    def sa_over(g):
                        over(g, sa_now, exp_done, total, part, part_done)

                    def ca_over(g):
                        over(g, ca_now, cexp_done, c_total, c_part, cpart_done)

                    def relu_up():
                        need(up_done, ff_now)
                        need(down_done, ff_now - 1)
                        for c in range(NF):
                            last = nc.vector.tensor_scalar(hid[:, c, :], pj[0][:, c * S:(c + 1) * S], b1[:, c:c + 1], 0.0,
                                                           ALU.add, ALU.max)
                        last.then_inc(hid_ready, 1)

                    def add_out(st, now, batch, done, bank, out):
                        held(st.tb_ready, now)
                        held(done, now)
                        nc.vector.tensor_tensor(rows_of(batch), bank[:, 0:E], st.tb[:, :], ALU.add).then_inc(out, 1)

                    if run_qkv:
                        stats(sa, qkv_now, (n + 1) % B, None)
                    if run_sa:
                        sa_mask_(0)
                    if run_qkv:
                        centre(sa, qkv_now, (n + 1) % B)
                    if run_ff:
                        add_out(ca, ff_now, (n - 2) % B, co_done, pj[1], ca_out)
                        stats(ff, ff_now, (n - 2) % B, ca_out)
                    if run_sa:
                        sa_over(0)
                        sa_mask_(1)
                    if run_ff:
                        centre(ff, ff_now, (n - 2) % B)
                    if run_ca:
                        ca_query_low(0)
                    if run_sa:
                        sa_mask_(2)
                        sa_over(1)
                    if run_ca:
                        take_ca_query(1)
                        ca_mask_(0)
                    if run_ff:
                        relu_up()
                    if run_sa:
                        sa_over(2)
                    if run_ca:
                        ca_query_low(1)
                    if run_sa:
                        sa_mask_(3)
                    if run_ca:
                        ca_over(0)
                        ca_mask_(1)
                    if run_ff:
                        add_out(ff, ff_now, (n - 2) % B, down_done, pj[1], ff_out)
                    if run_sa:
                        take_pT(2, sa_now, pt_done, pt_b, S, pT, pv_done, pT_ready)
                        sa_over(3)
                    if run_ca:
                        ca_mask_(2)
                        take_pT(0, ca_now, cpt_done, cpt_b, SC, c_pT, cpv_done, cpT_ready)
                    if run_sa:
                        take_oT(2, sa_now, pv_done, pv_b, oT, o_done, oT_ready)
                    if run_ca:
                        ca_over(1)
                    if run_qkv:
                        take_key(0, 0)
                        take_key(0, 1)
                    if run_ca:
                        ca_over(2)
                        ca_mask_(3)
                    if run_sa:
                        add_out(sa, sa_now, n % B, o_done, pj[0], sa_out)
                    if run_ca:
                        ca_over(3)
                        take_pT(2, ca_now, cpt_done, cpt_b, SC, c_pT, cpv_done, cpT_ready)
                    if run_qkv:
                        take_key(1, 1)
                        take_key(1, 0)
                    if run_sa:
                        stats(ca, sa_now, n % B, sa_out)
                        centre(ca, sa_now, n % B)
                    if run_qkv:
                        take_value(1)

                run(dve, body)


_AS_THEY_ARE = [f"{m}_xattn_{k}" for m in ("L0", "L3") for k in ("Wq", "bq", "Wk", "bk", "Wv", "bv", "Wo", "bo")] + \
    [f"L1_xattn_{k}" for k in ("Wq", "bq", "Wk", "bk", "Wv", "bv", "gamma", "beta")] + \
    [f"L2_xattn_{k}" for k in ("norm_g", "norm_b", "sa_q", "sa_ow", "sa_ob", "ca_ow", "ca_ob", "ff_w1",
                               "ff_w2", "ff_b2", "pre_g", "pre_b")] + \
    ["x", "ctx_512", "mask_BxSxS_ik0", "mask_Bx1xS2_if1"]


def kernel(**inputs):
    import numpy as np
    import concourse.bacc as bacc
    from concourse.bass_utils import run_bass_kernel_spmd

    laid = {k: inputs[k] for k in _AS_THEY_ARE}
    kv, ckv = np.asarray(inputs["L2_xattn_sa_kv"]), np.asarray(inputs["L2_xattn_ca_kv"])
    laid["sa_k"], laid["sa_v"] = kv[:, :, :HD], kv[:, :, HD:]
    laid["cakT"], laid["cavT"] = ckv[:, :, :HD].transpose(0, 2, 1), ckv[:, :, HD:].transpose(0, 2, 1)
    laid["caqT"] = np.asarray(inputs["L2_xattn_ca_q"]).transpose(0, 2, 1)
    laid["ffb1T"] = np.asarray(inputs["L2_xattn_ff_b1"]).reshape(L, NF, 128).transpose(0, 2, 1)
    laid["ctxT"] = np.asarray(inputs["ctx_512"]).transpose(2, 0, 1)

    nc = bacc.Bacc("TRN2", target_bir_lowering=False, num_devices=1)
    arrays, args = {}, {}
    for name, value in laid.items():
        value = np.ascontiguousarray(value)
        arrays[f"in_{name}"] = value
        args[name] = nc.dram_tensor(f"in_{name}", value.shape, mybir.dt.from_np(value.dtype), kind="ExternalInput").ap()
    args["out"] = nc.dram_tensor("out_t", (B, S, E), F32, kind="ExternalOutput").ap()
    build(nc, args)
    r = run_bass_kernel_spmd(nc, [arrays], core_ids=[0])
    return r.results[0]["out_t"]
```
